# Optimizing a Trainium2 kernel written in Bass

```python
import numpy as np
import jax
import jax.numpy as jnp

def _softmax(x, axis=-1):
    return jax.nn.softmax(x, axis=axis)

def _gelu(x):
    return jax.nn.gelu(x, approximate=True)

def _silu(x):
    return jax.nn.silu(x)

def _sigmoid(x):
    return jax.nn.sigmoid(x)

def _layernorm(x, axis=-1, eps=1e-05):
    m = jnp.mean(x, axis=axis, keepdims=True)
    v = jnp.var(x, axis=axis, keepdims=True)
    return (x - m) / jnp.sqrt(v + eps)

def _scatter_add(tgt, idx, src, axis=0):
    return tgt.at[idx].add(src)

def _segment_sum(src, seg, n):
    return jax.ops.segment_sum(src, seg, n)
kernel_name = 'mk_gnn_preln_d4_gnn_r32_34ef06'

def setup_inputs(seed: int=0):
    np.random.seed(seed)
    _w = jnp.asarray

    def _rec_inputs():
        import jax
        import jax.numpy as jnp
        _gk = jax.random.key(seed)
        x = -0.0003713 + 1 * jax.random.normal(jax.random.fold_in(_gk, 1), (3125, 256), jnp.float32)
        _s = jax.random.randint(jax.random.fold_in(_gk, 2), (25000,), 0, 3125, jnp.int32)
        _d = jax.random.randint(jax.random.fold_in(_gk, 3), (25000,), 0, 3125, jnp.int32)
        _loop = jnp.arange(3125, dtype=jnp.int32)
        src = jnp.concatenate([_s, _d, _loop])
        dst = jnp.concatenate([_d, _s, _loop])
        _o = jnp.argsort(dst, stable=True)
        src = src[_o]
        dst = dst[_o]
        edge_attr_4 = jax.random.uniform(jax.random.fold_in(_gk, 11), (53125, 4), jnp.float32, 0.0, 0.999999)
        edge_attr_64 = 0.000279952 + 1.00013 * jax.random.normal(jax.random.fold_in(_gk, 12), (53125, 64), jnp.float32)
        return (x, src, dst, edge_attr_4, edge_attr_64)
    x, src, dst, edge_attr_4, edge_attr_64 = _rec_inputs()

    def _L0_gnn_setup():
        import jax, jax.numpy as jnp
        import numpy as np
        N = 50000
        E = 15625
        CH = 256
        H1, C1 = (4, 64)
        H2, C2 = (8, 32)
        CONCAT = H1 * C1 + H2 * C2

        def _layer_norm(x, gamma, beta, eps=1e-05):
            mu = jnp.mean(x, axis=-1, keepdims=True)
            var = jnp.var(x, axis=-1, keepdims=True)
            return (x - mu) * jax.lax.rsqrt(var + eps) * gamma + beta

        def _gat_conv(x, src, dst, W, a_src, a_dst, bias, heads, out_ch, n_nodes):
            h = (x @ W).reshape(n_nodes, heads, out_ch)
            alpha_s = jnp.einsum('nhc,hc->nh', h, a_src)
            alpha_d = jnp.einsum('nhc,hc->nh', h, a_dst)
            e = jax.nn.leaky_relu(alpha_s[src] + alpha_d[dst], negative_slope=0.2)
            m = jax.ops.segment_max(e, dst, num_segments=n_nodes)
            ex = jnp.exp(e - m[dst])
            denom = jax.ops.segment_sum(ex, dst, num_segments=n_nodes)
            a = ex / (denom[dst] + 1e-16)
            msg = h[src] * a[:, :, None]
            out = jax.ops.segment_sum(msg, dst, num_segments=n_nodes)
            return out.reshape(n_nodes, heads * out_ch) + bias
        key = jax.random.key(seed)
        ks = jax.random.split(key, 16)
        s = 0.05
        x = jax.random.normal(ks[0], (N, CH), dtype=jnp.float32)
        edge_index = jax.random.randint(ks[1], (2, E), 0, N, dtype=jnp.int64)
        return {'x': x, 'edge_index': edge_index, 'gamma': jnp.ones((CH,), jnp.float32), 'beta': jnp.zeros((CH,), jnp.float32), 'W1': jax.random.normal(ks[2], (CH, H1 * C1), jnp.float32) * s, 'a_src1': jax.random.normal(ks[3], (H1, C1), jnp.float32) * s, 'a_dst1': jax.random.normal(ks[4], (H1, C1), jnp.float32) * s, 'b1': jnp.zeros((H1 * C1,), jnp.float32), 'W2': jax.random.normal(ks[5], (CH, H2 * C2), jnp.float32) * s, 'a_src2': jax.random.normal(ks[6], (H2, C2), jnp.float32) * s, 'a_dst2': jax.random.normal(ks[7], (H2, C2), jnp.float32) * s, 'b2': jnp.zeros((H2 * C2,), jnp.float32), 'Wu': jax.random.normal(ks[8], (CONCAT, CH), jnp.float32) * s, 'bu': jnp.zeros((CH,), jnp.float32)}
    _L0_gnn_all = _L0_gnn_setup()
    _L0_gnn_in = {k: v for k, v in _L0_gnn_all.items() if k in ('gamma', 'beta', 'W1', 'a_src1', 'a_dst1', 'b1', 'W2', 'a_src2', 'a_dst2', 'b2', 'Wu', 'bu')}
    del _L0_gnn_all

    def _L1_gnn_setup():
        import jax, jax.numpy as jnp
        import numpy as np
        N_NODES = 50000
        N_EDGES = 10000
        HIDDEN = 256
        N_LAYERS = 5
        BN_EPS = 1e-05

        def _mpnn(x, edge_index, edge_attr, mlp_w, mlp_b, ew1, ew2, bn_g, bn_b):
            n = x.shape[0]
            row, col = (edge_index[0], edge_index[1])
            deg = jax.ops.segment_sum(jnp.ones((edge_index.shape[1],), x.dtype), col, num_segments=n)
            dinv = jnp.where(deg > 0, deg ** (-0.5), 0.0)
            norm = dinv[row] * dinv[col]
            h = x
            for l in range(N_LAYERS):
                edge_fea = jnp.concatenate([edge_attr[:, 3:] @ ew1[l], edge_attr[:, 0:3] @ ew2[l]], axis=-1)
                msg = norm[:, None] * (h[row] + edge_fea)
                agg = jax.ops.segment_sum(msg, col, num_segments=n)
                h = jax.nn.relu(jnp.concatenate([h, agg], axis=1) @ mlp_w[l] + mlp_b[l])
                mu = h.mean(axis=0)
                var = h.var(axis=0)
                h = (h - mu) * jax.lax.rsqrt(var + BN_EPS) * bn_g[l] + bn_b[l]
                if l != N_LAYERS - 1:
                    h = jax.nn.relu(h)
            return h
        key = jax.random.key(seed)
        ks = jax.random.split(key, 8)
        x = jax.random.normal(ks[0], (N_NODES, HIDDEN), dtype=jnp.float32)
        edge_index = jax.random.randint(ks[1], (2, N_EDGES), 0, N_NODES, dtype=jnp.int64)
        edge_attr = jax.random.uniform(ks[2], (N_EDGES, 4), dtype=jnp.float32)
        mlp_w = jax.random.normal(ks[3], (N_LAYERS, 2 * HIDDEN, HIDDEN), dtype=jnp.float32) * (1.0 / np.sqrt(2 * HIDDEN))
        mlp_b = jnp.zeros((N_LAYERS, HIDDEN), dtype=jnp.float32)
        ew1 = jax.random.normal(ks[4], (N_LAYERS, 1, HIDDEN // 2), dtype=jnp.float32)
        ew2 = jax.random.normal(ks[5], (N_LAYERS, 3, HIDDEN // 2), dtype=jnp.float32) * (1.0 / np.sqrt(3.0))
        bn_g = jnp.ones((N_LAYERS, HIDDEN), dtype=jnp.float32)
        bn_b = jnp.zeros((N_LAYERS, HIDDEN), dtype=jnp.float32)
        return {'x': x, 'edge_index': edge_index, 'edge_attr': edge_attr, 'mlp_w': mlp_w, 'mlp_b': mlp_b, 'ew1': ew1, 'ew2': ew2, 'bn_g': bn_g, 'bn_b': bn_b}
    _L1_gnn_all = _L1_gnn_setup()
    _L1_gnn_in = {k: v for k, v in _L1_gnn_all.items() if k in ('mlp_w', 'mlp_b', 'ew1', 'ew2', 'bn_g', 'bn_b')}
    del _L1_gnn_all

    def _L2_gnn_setup():
        import jax, jax.numpy as jnp
        import numpy as np
        N_NODES = 3125
        IN_FEATS = 256
        OUT_FEATS = 256
        N_EDGES = 100000
        key = jax.random.key(seed)
        k1, k2, k3, k4 = jax.random.split(key, 4)
        x = jax.random.normal(k1, (N_NODES, IN_FEATS), dtype=jnp.float32)
        edge_index = jax.random.randint(k2, (2, N_EDGES), 0, N_NODES, dtype=jnp.int64)
        scale = 1.0 / np.sqrt(IN_FEATS)
        W = jax.random.uniform(k3, (IN_FEATS, OUT_FEATS), dtype=jnp.float32, minval=-scale, maxval=scale)
        b = jax.random.uniform(k4, (OUT_FEATS,), dtype=jnp.float32, minval=-scale, maxval=scale)
        return {'x': x, 'edge_index': edge_index, 'W': W, 'b': b}
    _L2_gnn_all = _L2_gnn_setup()
    _L2_gnn_in = {k: v for k, v in _L2_gnn_all.items() if k in ('W', 'b')}
    del _L2_gnn_all

    def _L3_gnn_setup():
        import jax, jax.numpy as jnp
        import numpy as np
        N, E, H, ED = (625, 10000, 256, 64)
        key = jax.random.key(seed)
        ks = jax.random.split(key, 12)

        def init_w(k, shape, fan_in):
            return (jax.random.normal(k, shape, jnp.float32) / np.sqrt(fan_in)).astype(jnp.float32)
        h = jax.random.normal(ks[0], (N, H), jnp.float32)
        edge_indices = jax.random.randint(ks[1], (2, E), 0, N, jnp.int32)
        edge_attr = jax.random.normal(ks[2], (E, ED), jnp.float32)
        din = 2 * H + ED
        W1 = init_w(ks[3], (H, din), din)
        b1 = jnp.zeros((H,), jnp.float32)
        W2 = init_w(ks[4], (H, H), H)
        b2 = jnp.zeros((H,), jnp.float32)
        W_ih = init_w(ks[5], (3 * H, H), H)
        b_ih = jnp.zeros((3 * H,), jnp.float32)
        W_hh = init_w(ks[6], (3 * H, H), H)
        b_hh = jnp.zeros((3 * H,), jnp.float32)
        return {'h': h, 'edge_indices': edge_indices, 'edge_attr': edge_attr, 'W1': W1, 'b1': b1, 'W2': W2, 'b2': b2, 'W_ih': W_ih, 'b_ih': b_ih, 'W_hh': W_hh, 'b_hh': b_hh}
    _L3_gnn_all = _L3_gnn_setup()
    _L3_gnn_in = {k: v for k, v in _L3_gnn_all.items() if k in ('W1', 'b1', 'W2', 'b2', 'W_ih', 'b_ih', 'W_hh', 'b_hh')}
    del _L3_gnn_all
    return {'x': x, 'src': src, 'dst': dst, 'edge_attr_4': edge_attr_4, 'edge_attr_64': edge_attr_64, 'L0_gnn_gamma': _L0_gnn_in['gamma'], 'L0_gnn_beta': _L0_gnn_in['beta'], 'L0_gnn_W1': _L0_gnn_in['W1'], 'L0_gnn_a_src1': _L0_gnn_in['a_src1'], 'L0_gnn_a_dst1': _L0_gnn_in['a_dst1'], 'L0_gnn_b1': _L0_gnn_in['b1'], 'L0_gnn_W2': _L0_gnn_in['W2'], 'L0_gnn_a_src2': _L0_gnn_in['a_src2'], 'L0_gnn_a_dst2': _L0_gnn_in['a_dst2'], 'L0_gnn_b2': _L0_gnn_in['b2'], 'L0_gnn_Wu': _L0_gnn_in['Wu'], 'L0_gnn_bu': _L0_gnn_in['bu'], 'L1_gnn_mlp_w': _L1_gnn_in['mlp_w'], 'L1_gnn_mlp_b': _L1_gnn_in['mlp_b'], 'L1_gnn_ew1': _L1_gnn_in['ew1'], 'L1_gnn_ew2': _L1_gnn_in['ew2'], 'L1_gnn_bn_g': _L1_gnn_in['bn_g'], 'L1_gnn_bn_b': _L1_gnn_in['bn_b'], 'L2_gnn_W': _L2_gnn_in['W'], 'L2_gnn_b': _L2_gnn_in['b'], 'L3_gnn_W1': _L3_gnn_in['W1'], 'L3_gnn_b1': _L3_gnn_in['b1'], 'L3_gnn_W2': _L3_gnn_in['W2'], 'L3_gnn_b2': _L3_gnn_in['b2'], 'L3_gnn_W_ih': _L3_gnn_in['W_ih'], 'L3_gnn_b_ih': _L3_gnn_in['b_ih'], 'L3_gnn_W_hh': _L3_gnn_in['W_hh'], 'L3_gnn_b_hh': _L3_gnn_in['b_hh']}

def reference(x, src, dst, edge_attr_4, edge_attr_64, L0_gnn_gamma, L0_gnn_beta, L0_gnn_W1, L0_gnn_a_src1, L0_gnn_a_dst1, L0_gnn_b1, L0_gnn_W2, L0_gnn_a_src2, L0_gnn_a_dst2, L0_gnn_b2, L0_gnn_Wu, L0_gnn_bu, L1_gnn_mlp_w, L1_gnn_mlp_b, L1_gnn_ew1, L1_gnn_ew2, L1_gnn_bn_g, L1_gnn_bn_b, L2_gnn_W, L2_gnn_b, L3_gnn_W1, L3_gnn_b1, L3_gnn_W2, L3_gnn_b2, L3_gnn_W_ih, L3_gnn_b_ih, L3_gnn_W_hh, L3_gnn_b_hh):
    import jax
    import jax.numpy as jnp

    def _L0_gnn_ref(x, edge_index, gamma, beta, W1, a_src1, a_dst1, b1, W2, a_src2, a_dst2, b2, Wu, bu):
        import jax, jax.numpy as jnp
        import numpy as np
        N = 50000
        E = 15625
        CH = 256
        H1, C1 = (4, 64)
        H2, C2 = (8, 32)
        CONCAT = H1 * C1 + H2 * C2

        def _layer_norm(x, gamma, beta, eps=1e-05):
            mu = jnp.mean(x, axis=-1, keepdims=True)
            var = jnp.var(x, axis=-1, keepdims=True)
            return (x - mu) * jax.lax.rsqrt(var + eps) * gamma + beta

        def _gat_conv(x, src, dst, W, a_src, a_dst, bias, heads, out_ch, n_nodes):
            h = (x @ W).reshape(n_nodes, heads, out_ch)
            alpha_s = jnp.einsum('nhc,hc->nh', h, a_src)
            alpha_d = jnp.einsum('nhc,hc->nh', h, a_dst)
            e = jax.nn.leaky_relu(alpha_s[src] + alpha_d[dst], negative_slope=0.2)
            m = jax.ops.segment_max(e, dst, num_segments=n_nodes)
            ex = jnp.exp(e - m[dst])
            denom = jax.ops.segment_sum(ex, dst, num_segments=n_nodes)
            a = ex / (denom[dst] + 1e-16)
            msg = h[src] * a[:, :, None]
            out = jax.ops.segment_sum(msg, dst, num_segments=n_nodes)
            return out.reshape(n_nodes, heads * out_ch) + bias
        n = x.shape[0]
        loop = jnp.arange(n, dtype=edge_index.dtype)
        src = jnp.concatenate([edge_index[0], loop])
        dst = jnp.concatenate([edge_index[1], loop])
        residual = x
        x_norm = _layer_norm(x, gamma, beta)
        out1 = _gat_conv(x_norm, src, dst, W1, a_src1, a_dst1, b1, H1, C1, n)
        out2 = _gat_conv(x_norm, src, dst, W2, a_src2, a_dst2, b2, H2, C2, n)
        x_cat = jax.nn.elu(jnp.concatenate([out1, out2], axis=-1))
        unified = x_cat @ Wu + bu
        return residual + unified

    def _L1_gnn_ref(x, edge_index, edge_attr, mlp_w, mlp_b, ew1, ew2, bn_g, bn_b):
        import jax, jax.numpy as jnp
        import numpy as np
        N_NODES = 50000
        N_EDGES = 10000
        HIDDEN = 256
        N_LAYERS = 5
        BN_EPS = 1e-05

        def _mpnn(x, edge_index, edge_attr, mlp_w, mlp_b, ew1, ew2, bn_g, bn_b):
            n = x.shape[0]
            row, col = (edge_index[0], edge_index[1])
            deg = jax.ops.segment_sum(jnp.ones((edge_index.shape[1],), x.dtype), col, num_segments=n)
            dinv = jnp.where(deg > 0, deg ** (-0.5), 0.0)
            norm = dinv[row] * dinv[col]
            h = x
            for l in range(N_LAYERS):
                edge_fea = jnp.concatenate([edge_attr[:, 3:] @ ew1[l], edge_attr[:, 0:3] @ ew2[l]], axis=-1)
                msg = norm[:, None] * (h[row] + edge_fea)
                agg = jax.ops.segment_sum(msg, col, num_segments=n)
                h = jax.nn.relu(jnp.concatenate([h, agg], axis=1) @ mlp_w[l] + mlp_b[l])
                mu = h.mean(axis=0)
                var = h.var(axis=0)
                h = (h - mu) * jax.lax.rsqrt(var + BN_EPS) * bn_g[l] + bn_b[l]
                if l != N_LAYERS - 1:
                    h = jax.nn.relu(h)
            return h
        return _mpnn(x, edge_index, edge_attr, mlp_w, mlp_b, ew1, ew2, bn_g, bn_b)

    def _L2_gnn_ref(x, edge_index, W, b):
        import jax, jax.numpy as jnp
        import numpy as np
        N_NODES = 3125
        IN_FEATS = 256
        OUT_FEATS = 256
        N_EDGES = 100000
        n = x.shape[0]
        row = edge_index[0]
        col = edge_index[1]
        h = x @ W + b
        agg = jax.ops.segment_sum(h[col], row, num_segments=n)
        deg = jax.ops.segment_sum(jnp.ones((edge_index.shape[1],), dtype=h.dtype), row, num_segments=n)
        inv_deg = jnp.where(deg > 0, 1.0 / jnp.where(deg > 0, deg, 1.0), 0.0)
        return agg * inv_deg[:, None]

    def _L3_gnn_ref(h, edge_indices, edge_attr, W1, b1, W2, b2, W_ih, b_ih, W_hh, b_hh):
        import jax, jax.numpy as jnp
        import numpy as np
        N, E, H, ED = (625, 10000, 256, 64)
        row, col = (edge_indices[0], edge_indices[1])
        edge_in = jnp.concatenate([h[row], h[col], edge_attr], axis=-1)
        msg = jax.nn.relu(edge_in @ W1.T + b1) @ W2.T + b2
        agg = jax.ops.segment_sum(msg, row, num_segments=h.shape[0])
        gx = agg @ W_ih.T + b_ih
        gh = h @ W_hh.T + b_hh
        xr, xz, xn = jnp.split(gx, 3, axis=-1)
        hr, hz, hn = jnp.split(gh, 3, axis=-1)
        r = jax.nn.sigmoid(xr + hr)
        z = jax.nn.sigmoid(xz + hz)
        n = jnp.tanh(xn + r * hn)
        h_new = (1.0 - z) * n + z * h
        return h_new
    edge_index = jnp.stack([src, dst])
    h = jnp.maximum(_layernorm(x, axis=-1), 0.0)
    x = x + _L0_gnn_ref(h, edge_index, L0_gnn_gamma, L0_gnn_beta, L0_gnn_W1, L0_gnn_a_src1, L0_gnn_a_dst1, L0_gnn_b1, L0_gnn_W2, L0_gnn_a_src2, L0_gnn_a_dst2, L0_gnn_b2, L0_gnn_Wu, L0_gnn_bu)
    h = jnp.maximum(_layernorm(x, axis=-1), 0.0)
    x = x + _L1_gnn_ref(h, edge_index, edge_attr_4, L1_gnn_mlp_w, L1_gnn_mlp_b, L1_gnn_ew1, L1_gnn_ew2, L1_gnn_bn_g, L1_gnn_bn_b)
    h = jnp.maximum(_layernorm(x, axis=-1), 0.0)
    x = x + _L2_gnn_ref(h, edge_index, L2_gnn_W, L2_gnn_b)
    h = jnp.maximum(_layernorm(x, axis=-1), 0.0)
    x = x + _L3_gnn_ref(h, edge_index, edge_attr_64, L3_gnn_W1, L3_gnn_b1, L3_gnn_W2, L3_gnn_b2, L3_gnn_W_ih, L3_gnn_b_ih, L3_gnn_W_hh, L3_gnn_b_hh)
    return x

_drawn_inputs = setup_inputs


def setup_inputs(seed=0):
    import zlib

    import numpy as np

    out = dict(_drawn_inputs(seed))
    spreads = {'L0_gnn_gamma': (1.0, 0.2),
     'L0_gnn_beta': (0.0, 0.1),
     'L0_gnn_b1': (0.0, 0.1),
     'L0_gnn_b2': (0.0, 0.1),
     'L0_gnn_bu': (0.0, 0.1),
     'L1_gnn_mlp_b': (0.0, 0.1),
     'L1_gnn_bn_g': (1.0, 0.2),
     'L1_gnn_bn_b': (0.0, 0.1),
     'L3_gnn_b1': (0.0, 0.1),
     'L3_gnn_b2': (0.0, 0.1),
     'L3_gnn_b_ih': (0.0, 0.8),
     'L3_gnn_b_hh': (0.0, 0.8)}
    factors = {'L0_gnn_a_dst1': 2.995, 'L0_gnn_a_dst2': 3.281, 'L2_gnn_b': 3.075}
    for name, (base, spread) in spreads.items():
        noise = np.random.default_rng([zlib.crc32(name.encode()), seed]).standard_normal(out[name].shape)
        drawn = base * np.exp(spread * noise) if base else spread * noise
        out[name] = jnp.asarray(drawn.astype(out[name].dtype))
    for name, factor in factors.items():
        out[name] = (out[name] * factor).astype(out[name].dtype)
    return out
```

```python
from contextlib import ExitStack

import numpy as np
import concourse.bass as bass
from concourse import mybir

F32 = mybir.dt.float32
F16 = mybir.dt.float16
BF16 = mybir.dt.bfloat16
I32 = mybir.dt.int32
U32 = mybir.dt.uint32
ALU = mybir.AluOpType
ACT = mybir.ActivationFunctionType
AX = mybir.AxisListType
ET = mybir.EngineType

P = 128
N = 3125
NT = -(-N // P)
NP = NT * P
D = 256
E = 53125
CH = -(-E // P)
EP = CH * P
GR = 110
NB = 4
S = GR * NB
assert S >= CH + NT - 1
HJ = 425
HP = E // HJ
HB = 17
HW = 16
HD = 512
ROW = HD + HW
SROW = 20
KD = NP * NP
ZF = 8000
PLAN_CHUNKS = 15
RS = 4
ED = 64
PADDST = 4095
BIG = 1.0e30
EPS = 1e-5
LAYERS = 5
W = 400
NC = NP // W
assert NC * W == NP and NC % 2 == 0
LO = 2048.0
assert HP * HJ == E and HJ % HB == 0


class Order:

    def __init__(self, engine, semaphore):
        self.engine, self.semaphore, self.base, self.n = engine, semaphore, 0, 0

    def did(self, instruction):
        instruction.then_inc(self.semaphore, 1)
        self.n += 1
        return self.n

    def need(self, n):
        self.engine.wait_ge(self.semaphore, self.base + n)

    def link(self, instruction):
        self.need(self.did(instruction))

    def enter(self, i, per):
        self.start, self.per = self.base + self.n, per
        self.base, self.n = self.start + i * per, 0

    def leave(self, rounds):
        assert self.n == self.per, (self.n, self.per)
        self.base, self.n = self.start + rounds * self.per, 0


def column(ap, k):
    return ap[:, bass.ds(k, 1)]


def read_registers(nc, table, at, count, engine, top):
    _, values = nc.values_load_multi_w_load_instructions(
        table[0:1, bass.ds(at, count)], engines=[engine], min_val=0, max_val=top,
        skip_runtime_bounds_check_because="the table is clamped to this range when it is made")
    return values


def program(nc, a, out):
    top = ExitStack()
    with top:
        def sb(name, shape, dt, ctx=top):
            return ctx.enter_context(nc.sbuf_tensor(name, shape, dt))

        def ps(name, shape, dt, ctx):
            return ctx.enter_context(nc.psum_tensor(name, shape, dt))

        def sem(name, over_stages=False):
            handle = nc.alloc_semaphore(name=name)
            (lasting if over_stages else of_stage).append(handle)
            return handle

        def end_stage():
            nc.clear_and_free_semaphores(of_stage)
            of_stage.clear()
            nc.all_engine_barrier()


        def dram(name, shape, dt):
            return nc.dram_tensor(name, shape, dt, kind="Internal").ap()

        lasting, of_stage = [], []
        top.enter_context(nc.allow_non_contiguous_dma(reason="small tables and columns, once"))
        x_sb = sb("x_sb", [P, NT, D], F32)
        iota_row = sb("iota_row", [P, P], F32)
        pidx = sb("pidx", [P, 1], F32)
        ident = sb("ident", [P, P], F32)
        ident16 = sb("ident16", [P, P], F16)
        lower = sb("lower", [P, P], F32)
        ones = sb("ones", [P, P], F32)
        deg = sb("deg", [P, NT], F32)
        dinv = sb("dinv", [P, NT], F32)
        step_table = sb("step_table", [1, 2 * S], I32)
        src_step = sb("src_step", [P, S], I32)
        dl_step = sb("dl_step", [P, S], F32)
        F_sb = sb("F_sb", [P, NT, 4], F32)
        degsrc = sb("degsrc", [P, NT], F32)
        rstd = sb("rstd", [P, NT], F32)
        shift = sb("shift", [P, NT], F32)
        stats = sb("stats", [P, NT, 6], F32)
        norm_small = sb("norm_small", [P, 5, NT], F32)
        tab = sb("tab", [P, NT, 2 * HW], F32)
        early = top.enter_context(ExitStack())
        zeros = sb("zeros", [P, ZF], F32, early)
        waits_passed = sem("waits_passed", True)
        key_step = sb("key_step", [P, S], F32, early)
        last_step = sb("last_step", [P, S], F32, early)
        attr4_step = sb("attr4_step", [P, S, 4], F32, early)
        self_s = sb("self_s", [P, NT, HW], F32, early)

        step_dram = dram("step_dram", [2 * S], I32)
        pen_dram = dram("pen_dram", [S * P], F32)
        key_dram = dram("key_dram", [S * P], F32)
        pair_dram = dram("pair_dram", [S, 2, P], F32)
        sums_dram = [dram(f"sums_dram{n}", [NP + P, D], F32) for n in range(RS)]
        seg_dram = dram("seg_dram", [S * P + 2], F32)
        att_dram = dram("att_dram", [NP, ROW], F32)
        score_dram = dram("score_dram", [NP, SROW], F32)
        count_dram = dram("count_dram", [KD + P, 1], F32)

        with ExitStack() as ctx:
            iota_i = sb("iota_i", [P, P], I32, ctx)
            pidx_i = sb("pidx_i", [P, 1], I32, ctx)
            dst_i = sb("dst_i", [HP, HJ], I32, ctx)
            lo_i = sb("lo_i", [HP, HJ], I32, ctx)
            hi_i = sb("hi_i", [HP, HJ], I32, ctx)
            lo_f = sb("lo_f", [HP, HJ], F32, ctx)
            hi_f = sb("hi_f", [HP, HJ], F32, ctx)
            lo_hot = sb("lo_hot", [HP, 2, HB, P], BF16, ctx)
            hi_hot = sb("hi_hot", [HP, 2, HB, NT], BF16, ctx)
            hist = ps("hist", [P, NT], F32, ctx)
            dst_in, x_in, iota_made = sem("dst_in"), sem("x_in"), sem("iota_made")
            count_order, hots_ready, hots_used = sem("count_order"), sem("hots_ready"), sem("hots_used")
            sums_zeroed = sem("sums_zeroed", True)
            zeros_ready, zeros_out, hist_zero = sem("zeros_ready"), sem("zeros_out", True), sem("hist_zero")
            NZ = KD // (P * ZF)
            with nc.Block() as block:
                @block.sync
                def _(sp):
                    sp.dma_start(dst_i[:], a["dst"][0:E].rearrange("(p j) -> p j", p=HP)).then_inc(dst_in, 16)
                    sp.dma_start(x_sb[:], a["x"].rearrange("(t p) d -> p t d", p=P)).then_inc(x_in, 16)
                    sp.wait_ge(zeros_ready, 1)
                    whole = count_dram[0:KD, :].rearrange("(z p f) o -> z p (f o)", z=NZ, p=P)
                    with sp.Fori(0, NZ) as z:
                        sp.dma_start(whole[bass.ds(z, 1)].rearrange("z p f -> (z p) f"), zeros[:]).then_inc(zeros_out, 16)
                    sp.dma_start(count_dram[KD:KD + P, :], zeros[:, 0:1]).then_inc(zeros_out, 16)
                    width = (NP + P) * D // P
                    for n in range(RS):
                        sp.dma_start(sums_dram[n].rearrange("(p r) d -> p (r d)", p=P), zeros[:, 0:width]).then_inc(sums_zeroed, 16)
                    sp.wait_ge(x_in, 16)

                @block.gpsimd
                def _(pool):
                    nc.gpsimd.memset(zeros[:], 0.0).then_inc(zeros_ready, 1)
                    nc.gpsimd.iota(iota_i[:], pattern=[[1, P]], base=0, channel_multiplier=0).then_inc(iota_made, 1)
                    nc.gpsimd.iota(pidx_i[:], pattern=[[0, 1]], base=0, channel_multiplier=1).then_inc(iota_made, 1)

                @block.vector
                def _(dve):
                    o = Order(dve, count_order)
                    nc.vector.memset(hist[:], 0.0).then_inc(hist_zero, 1)
                    dve.wait_ge(iota_made, 2)
                    o.did(nc.vector.tensor_copy(iota_row[:], iota_i[:]))
                    o.did(nc.vector.memset(ones[:], 1.0))
                    o.link(nc.vector.tensor_copy(pidx[:], pidx_i[:]))
                    o.did(nc.vector.tensor_scalar(ident[:], iota_row[:], pidx[:, 0:1], None, ALU.is_equal))
                    o.did(nc.vector.tensor_scalar(ident16[:], iota_row[:], pidx[:, 0:1], None, ALU.is_equal))
                    o.did(nc.vector.tensor_scalar(lower[:], iota_row[:], pidx[:, 0:1], None, ALU.is_lt))
                    dve.wait_ge(dst_in, 16)
                    o.did(nc.vector.tensor_scalar(lo_i[:], dst_i[:], P - 1, None, ALU.bitwise_and))
                    o.link(nc.vector.tensor_scalar(hi_i[:], dst_i[:], 7, None, ALU.logical_shift_right))
                    o.did(nc.vector.tensor_copy(lo_f[:], lo_i[:]))
                    o.link(nc.vector.tensor_copy(hi_f[:], hi_i[:]))
                    with dve.Fori(0, HJ // HB) as b:
                        with_slot = bass.ds(b % 2, 1)
                        dve.wait_ge(hots_used, b)
                        nc.vector.tensor_tensor(
                            lo_hot[:, with_slot].rearrange("p o j n -> p (o j) n"),
                            iota_row[0:HP].unsqueeze(1).broadcast_to([HP, HB, P]),
                            lo_f[:, bass.ds(b * HB, HB)].unsqueeze(2).broadcast_to([HP, HB, P]), ALU.is_equal)
                        nc.vector.tensor_tensor(
                            hi_hot[:, with_slot].rearrange("p o j n -> p (o j) n"),
                            iota_row[0:HP, 0:NT].unsqueeze(1).broadcast_to([HP, HB, NT]),
                            hi_f[:, bass.ds(b * HB, HB)].unsqueeze(2).broadcast_to([HP, HB, NT]),
                            ALU.is_equal).then_inc(hots_ready, 1)
                    dve.wait_ge(hots_used, HJ // HB + 1)
                    nc.vector.tensor_copy(deg[:], hist[:])

                @block.tensor
                def _(pe):
                    pe.wait_ge(hist_zero, 1)
                    pe.nop().then_inc(hots_used, 1)
                    with pe.Fori(0, HJ // HB) as b:
                        pe.wait_ge(hots_ready, b + 1)
                        for j in range(HB):
                            last = nc.tensor.matmul(
                                hist[:], lo_hot[:, bass.ds(b % 2, 1), j, :].rearrange("p o n -> p (o n)"),
                                hi_hot[:, bass.ds(b % 2, 1), j, :].rearrange("p o n -> p (o n)"),
                                start=False, stop=True, skip_group_check=True)
                        last.then_inc(hots_used, 1)

        with ExitStack() as ctx:
            col = sb("col", [NT, 8], F32, ctx)
            col_i = sb("col_i", [NT, 4], I32, ctx)
            chunks_bc = sb("chunks_bc", [NT, P], F32, ctx)
            first_bc = sb("first_bc", [NT, P], F32, ctx)
            tri_ex = sb("tri_ex", [NT, NT], F32, ctx)
            tri_in = sb("tri_in", [NT, NT], F32, ctx)
            base_row = sb("base_row", [GR, NT], F32, ctx)
            incl_row = sb("incl_row", [GR, NT], F32, ctx)
            step_i = sb("step_i", [GR, NB], I32, ctx)
            step_f = sb("step_f", [GR, NB], F32, ctx)
            sel = sb("sel", [GR, NB, NT], F32, ctx)
            tile_f = sb("tile_f", [GR, NB], F32, ctx)
            tile_c = sb("tile_c", [GR, NB], F32, ctx)
            chunk_f = sb("chunk_f", [GR, NB], F32, ctx)
            chunk_i = sb("chunk_i", [GR, NB], I32, ctx)
            table_i = sb("table_i", [GR, 2, NB], I32, ctx)
            srcrow = sb("srcrow", [GR, NB, P], I32, ctx)
            dstrow = sb("dstrow", [GR, NB, P], I32, ctx)
            attrrow = sb("attrrow", [GR, NB, P, 4], F32, ctx)
            src_f = sb("src_f", [GR, NB, P], F32, ctx)
            dl_row = sb("dl_row", [GR, NB, P], F32, ctx)
            seg_row = sb("seg_row", [GR, NB, P], F32, ctx)
            key_row = sb("key_row", [GR, NB, P], F32, ctx)
            v1 = sb("v1", [GR, NB, P], F32, ctx)
            v2 = sb("v2", [GR, NB, P], F32, ctx)
            before = sb("before", [GR, NB, P], F32, ctx)
            after = sb("after", [GR, NB, P], F32, ctx)
            last_row = sb("last_row", [GR, NB, P], F32, ctx)
            msg_row = sb("msg_row", [GR, NB, P], F32, ctx)
            ends = sb("ends", [1, 2], F32, ctx)
            tile_off = sb("tile_off", [GR, NB], F32, ctx)
            few = ps("few", [P, 512], F32, ctx)
            turned = [ps(f"turned{i}", [P, 512], F32, ctx) for i in range(4)]
            plan = sem("plan")
            pe_few, rows_in, table_out, table_in = sem("pe_few"), sem("rows_in"), sem("table_out"), sem("table_in")
            seg_out, seg_in, pen_out, turned_ready, turned_used = (
                sem("seg_out"), sem("seg_in"), sem("pen_out"), sem("turned_ready"), sem("turned_used"))
            steps_made = sem("steps_made")
            row_ready = sem("row_ready")
            COUNT, START, END, CHUNKS, FIRST, SOME = range(6)
            with nc.Block() as block:
                @block.gpsimd
                def _(pool):
                    nc.gpsimd.iota(step_i[:], pattern=[[GR, NB]], base=0, channel_multiplier=1).then_inc(steps_made, 1)
                    pool.wait_ge(row_ready, 1)
                    for b in range(NB):
                        for rows, name in ((srcrow[:, b, :], "src"), (dstrow[:, b, :], "dst"),
                                           (attrrow[:, b].rearrange("p e c -> p (e c)"), "attr4")):
                            table = a[name].rearrange("(c e) -> c e", c=CH) if name != "attr4" else \
                                a[name].rearrange("(c e) f -> c (e f)", c=CH)
                            nc.gpsimd.indirect_dma_start(
                                rows, None, table, bass.IndirectOffsetOnAxis(ap=chunk_i[:, b:b + 1].bitcast(U32), axis=0)
                            ).then_inc(rows_in, 16)

                @block.tensor
                def _(pe):
                    nc.tensor.matmul(few[0:NT, 0:1], deg[:], ones[:, 0:1], start=True, stop=True).then_inc(pe_few, 1)
                    pe.wait_ge(plan, 3)
                    nc.tensor.matmul(few[0:NT, 1:2], tri_ex[:], col[:, COUNT:COUNT + 1], start=True, stop=True).then_inc(pe_few, 1)
                    pe.wait_ge(plan, PLAN_CHUNKS)
                    nc.tensor.matmul(few[0:GR, 32:32 + NT], chunks_bc[:, 0:GR], tri_in[:], start=True, stop=True)
                    nc.tensor.matmul(few[0:GR, 64:64 + NT], chunks_bc[:, 0:GR], tri_ex[:], start=True, stop=True)
                    nc.tensor.matmul(few[0:GR, 96:96 + NT], first_bc[:, 0:GR], ident[0:NT, 0:NT], start=True, stop=True).then_inc(pe_few, 1)
                    n = 0
                    for what, rows in (("src", src_f), ("dl", dl_row), ("key", key_row), ("last", last_row)):
                        pe.wait_ge(row_ready, 2 + n)
                        for b in range(NB):
                            t = nc.tensor.transpose(turned[n % 4][:, b * GR:(b + 1) * GR], rows[:, b, :], ident[0:GR, 0:GR])
                        t.then_inc(turned_ready, 1)
                        n += 1
                    for c in range(4):
                        pe.wait_ge(turned_used, n - 3)
                        for b in range(NB):
                            t = nc.tensor.transpose(turned[n % 4][:, b * GR:(b + 1) * GR], attrrow[:, b, :, c], ident[0:GR, 0:GR])
                        t.then_inc(turned_ready, 1)
                        n += 1

                @block.sync
                def _(sp):
                    sp.wait_ge(row_ready, 1)
                    for r in range(2):
                        sp.dma_start(step_dram[r * S:(r + 1) * S].rearrange("(b p) -> p b", b=NB), table_i[:, r, :]).then_inc(table_out, 16)
                    sp.wait_ge(table_out, 32)
                    sp.dma_start(step_table[:], step_dram.rearrange("(o s) -> o s", o=1)).then_inc(table_in, 16)
                    sp.wait_ge(row_ready, 4)
                    sp.dma_start(seg_dram[1:S * P + 1].rearrange("(b p e) -> p b e", b=NB, p=GR), seg_row[:]).then_inc(seg_out, 16)
                    sp.dma_start(seg_dram[0:1].rearrange("(o s) -> o s", o=1), ends[:, 0:1]).then_inc(seg_out, 16)
                    sp.dma_start(seg_dram[S * P + 1:S * P + 2].rearrange("(o s) -> o s", o=1), ends[:, 1:2]).then_inc(seg_out, 16)
                    sp.wait_ge(seg_out, 48)
                    sp.dma_start(before[:], seg_dram[0:S * P].rearrange("(b p e) -> p b e", b=NB, p=GR)).then_inc(seg_in, 16)
                    sp.dma_start(after[:], seg_dram[2:S * P + 2].rearrange("(b p e) -> p b e", b=NB, p=GR)).then_inc(seg_in, 16)
                    sp.dma_start(key_dram.rearrange("(b p e) -> p b e", b=NB, p=GR), key_row[:]).then_inc(pen_out, 16)
                    sp.wait_ge(row_ready, 5)
                    sp.dma_start(pen_dram.rearrange("(b p e) -> p b e", b=NB, p=GR), v1[:]).then_inc(pen_out, 16)
                    for n, rows in enumerate((dl_row, msg_row)):
                        sp.dma_start(pair_dram.rearrange("(b p) n e -> n p b e", b=NB)[n], rows[:]).then_inc(pen_out, 16)
                    sp.wait_ge(pen_out, 64)
                    sp.wait_ge(table_in, 16)

                @block.vector
                def _(dve):
                    o = Order(dve, plan)
                    TT, TS = nc.vector.tensor_tensor, nc.vector.tensor_scalar
                    o.did(TS(tri_ex[:], iota_row[0:NT, 0:NT], pidx[0:NT, 0:1], None, ALU.is_gt))
                    o.did(TS(tri_in[:], iota_row[0:NT, 0:NT], pidx[0:NT, 0:1], None, ALU.is_ge))
                    dve.wait_ge(pe_few, 1)
                    o.link(nc.vector.tensor_copy(col[:, COUNT:COUNT + 1], few[0:NT, 0:1]))
                    dve.wait_ge(pe_few, 2)
                    o.did(nc.vector.tensor_copy(col_i[:, 0:1], few[0:NT, 1:2]))
                    o.link(nc.vector.tensor_copy(col[:, START:START + 1], few[0:NT, 1:2]))
                    o.did(TS(col[:, SOME:SOME + 1], col[:, COUNT:COUNT + 1], 0.5, None, ALU.is_ge))
                    o.link(TT(col[:, END:END + 1], col[:, START:START + 1], col[:, COUNT:COUNT + 1], ALU.add))
                    o.link(TS(col[:, END:END + 1], col[:, END:END + 1], -1.0, 0.0, ALU.add, ALU.max))
                    o.link(nc.vector.tensor_copy(col_i[:, 1:2], col[:, END:END + 1]))
                    o.link(TS(col_i[:, 2:4], col_i[:, 0:2], 7, None, ALU.logical_shift_right))
                    o.link(nc.vector.tensor_copy(col[:, 6:8], col_i[:, 2:4]))
                    o.did(TS(first_bc[:], ones[0:NT, :], col[:, 6:7], None, ALU.mult))
                    o.link(TT(col[:, CHUNKS:CHUNKS + 1], col[:, 7:8], col[:, 6:7], ALU.subtract))
                    o.link(TS(col[:, CHUNKS:CHUNKS + 1], col[:, CHUNKS:CHUNKS + 1], 1.0, col[:, SOME:SOME + 1], ALU.add, ALU.mult))
                    o.link(TS(chunks_bc[:], ones[0:NT, :], col[:, CHUNKS:CHUNKS + 1], None, ALU.mult))
                    assert o.n == PLAN_CHUNKS
                    dve.wait_ge(steps_made, 1)
                    o.did(nc.vector.tensor_copy(step_f[:], step_i[:]))
                    dve.wait_ge(pe_few, 3)
                    o.did(nc.vector.tensor_copy(incl_row[:], few[0:GR, 32:32 + NT]))
                    o.link(nc.vector.tensor_copy(base_row[:], few[0:GR, 96:96 + NT]))
                    o.link(TT(base_row[:], base_row[:], few[0:GR, 64:64 + NT], ALU.subtract))
                    spread = [GR, NB, NT]
                    o.link(TT(sel[:], step_f[:].unsqueeze(2).broadcast_to(spread), incl_row[:].unsqueeze(1).broadcast_to(spread), ALU.is_ge))
                    o.link(nc.vector.tensor_reduce(tile_f[:], sel[:], AX.X, ALU.add))
                    o.link(TT(sel[:], iota_row[0:GR, 0:NT].unsqueeze(1).broadcast_to(spread), tile_f[:].unsqueeze(2).broadcast_to(spread), ALU.is_equal))
                    o.link(TT(sel[:], sel[:], base_row[:].unsqueeze(1).broadcast_to(spread), ALU.mult))
                    o.link(nc.vector.tensor_reduce(chunk_f[:], sel[:], AX.X, ALU.add))
                    o.link(TT(chunk_f[:], chunk_f[:], step_f[:], ALU.add))
                    o.link(TS(chunk_f[:], chunk_f[:], float(CH - 1), None, ALU.min))
                    o.did(TS(tile_c[:], tile_f[:], float(NT - 1), None, ALU.min))
                    o.did(TS(tile_off[:], tile_f[:], float(P), None, ALU.mult))
                    o.link(nc.vector.tensor_copy(chunk_i[:], chunk_f[:]))
                    o.did(nc.vector.tensor_copy(table_i[:, 0, :], tile_c[:]))
                    o.link(TS(table_i[:, 1, :], chunk_f[:], float(P), None, ALU.mult))
                    dve.nop().then_inc(row_ready, 1)
                    dve.wait_ge(rows_in, 16 * 3 * NB)
                    flat = [GR, NB, P]
                    o.did(nc.vector.tensor_copy(src_f[:], srcrow[:]))
                    o.link(nc.vector.tensor_copy(seg_row[:], dstrow[:]))
                    o.link(TT(dl_row[:], seg_row[:], tile_off[:].unsqueeze(2).broadcast_to(flat), ALU.subtract))
                    dve.nop().then_inc(row_ready, 1)
                    dve.nop().then_inc(row_ready, 1)
                    o.did(TS(tile_off[:], tile_f[:], 4096.0, None, ALU.mult))
                    o.did(TS(v1[:], dl_row[:], 0.0, None, ALU.is_ge))
                    o.link(TS(v2[:], dl_row[:], float(P), None, ALU.is_lt))
                    o.did(TT(v1[:], v1[:], v2[:], ALU.mult))
                    o.did(nc.vector.memset(ends[:], -1.0))
                    o.link(nc.vector.scalar_tensor_tensor(key_row[:], src_f[:], float(NP), seg_row[:], ALU.mult, ALU.add))
                    own = iota_row[0:GR].unsqueeze(1).broadcast_to(flat)
                    o.link(TT(seg_row[:], seg_row[:], tile_off[:].unsqueeze(2).broadcast_to(flat), ALU.add))
                    o.link(TT(key_row[:], key_row[:], own, ALU.subtract))
                    o.link(nc.vector.scalar_tensor_tensor(key_row[:], key_row[:], -float(KD), v1[:], ALU.add, ALU.mult))
                    o.link(TT(key_row[:], key_row[:], own, ALU.add))
                    o.did(TS(key_row[:], key_row[:], float(KD), None, ALU.add))
                    o.link(TT(msg_row[:], src_f[:], own, ALU.subtract))
                    o.link(nc.vector.scalar_tensor_tensor(msg_row[:], msg_row[:], -float(NP), v1[:], ALU.add, ALU.mult))
                    o.link(nc.vector.scalar_tensor_tensor(msg_row[:], msg_row[:], float(NP), own, ALU.add, ALU.add))
                    dve.nop().then_inc(row_ready, 1)
                    dve.wait_ge(seg_in, 32)
                    o.did(TT(last_row[:], seg_row[:], after[:], ALU.not_equal))
                    o.link(TT(v1[:], seg_row[:], before[:], ALU.not_equal))
                    o.link(TS(v1[:], v1[:], -BIG, None, ALU.mult))
                    dve.nop().then_inc(row_ready, 1)
                    targets = (src_step[:], dl_step[:], key_step[:], last_step[:]) + tuple(attr4_step[:, :, c] for c in range(4))
                    for n, target in enumerate(targets):
                        dve.wait_ge(turned_ready, n + 1)
                        nc.vector.tensor_copy(target, turned[n % 4][:, 0:S]).then_inc(turned_used, 1)

        def norm_scales(name, source, t0=None):
            order, var_ready, root_ready = sem(name + "_order"), sem(name + "_var_ready"), sem(name + "_root_ready")
            mean, diff, var, root, half = (norm_small[:, i, :] for i in range(5))
            with nc.Block() as block:
                @block.vector
                def _(dve):
                    o = Order(dve, order)
                    with dve.Fori(0, NT) as t:
                        o.enter(t, 1)
                        o.did(nc.vector.bn_stats(stats[:, bass.ds(t, 1), :].rearrange("p o s -> p (o s)"),
                                                 source[:, bass.ds(t, 1), :].rearrange("p o d -> p (o d)")))
                    o.leave(NT)
                    o.need(o.n)
                    o.did(nc.vector.tensor_tensor(mean, stats[:, :, 1], stats[:, :, 4], ALU.add))
                    o.did(nc.vector.tensor_tensor(diff, stats[:, :, 1], stats[:, :, 4], ALU.subtract))
                    o.link(nc.vector.tensor_tensor(var, stats[:, :, 2], stats[:, :, 5], ALU.add))
                    o.did(nc.vector.tensor_scalar(mean, mean, 0.5, None, ALU.mult))
                    o.did(nc.vector.tensor_scalar(var, var, 1.0 / D, EPS, ALU.mult, ALU.add))
                    o.link(nc.vector.tensor_tensor(half, diff, diff, ALU.mult))
                    o.link(nc.vector.scalar_tensor_tensor(var, half, 0.25, var, ALU.mult, ALU.add))
                    dve.nop().then_inc(var_ready, 1)
                    dve.wait_ge(root_ready, 1)
                    o.link(nc.vector.reciprocal(rstd[:], root))
                    o.link(nc.vector.scalar_tensor_tensor(shift[:], mean, -1.0, rstd[:], ALU.mult, ALU.mult))

                @block.scalar
                def _(act):
                    act.wait_ge(var_ready, 1)
                    nc.scalar.activation(root, var, ACT.Sqrt).then_inc(root_ready, 1)

        def norm_apply(name, source, target, func):
            with nc.Block() as block:
                @block.scalar
                def _(act):
                    with act.Fori(0, NT) as t:
                        nc.scalar.activation(target[:, bass.ds(t, 1), :].rearrange("p o d -> p (o d)"),
                                             source[:, bass.ds(t, 1), :].rearrange("p o d -> p (o d)"), func,
                                             bias=column(shift, t), scale=column(rstd, t))

        norm_scales("n0", x_sb)
        with ExitStack() as ctx:
            h0 = sb("h0", [P, NT, D], F32, ctx)
            wall = sb("wall", [P, 2, HD + 2 * HW], F32, ctx)
            arep = sb("arep", [P, 2, HD], F32, ctx)
            aprod = sb("aprod", [P, HD], F32, ctx)
            score_w = sb("score_w", [P, 2, 2, 12], F32, ctx)
            gb = sb("gb", [P, 2, 2], F32, ctx)
            bw = sb("bw", [1, HD + 2 * HW], F32, ctx)
            zs = sb("zs", [P, 5, D], F32, ctx)
            zT = sb("zT", [P, 5, 2, P], F32, ctx)
            orow = sb("orow", [P, 5, ROW], F32, ctx)
            srow = sb("srow", [P, 5, SROW], F32, ctx)
            dsmall = sb("dsmall", [P, 2, NT], F32, ctx)
            p_zT = [ps(f"p_zT{i}", [P, 2, P], F32, ctx) for i in range(2)]
            p_h = [ps(f"p_h{i}", [P, HD], F32, ctx) for i in range(2)]
            p_s = [ps(f"p_s{i}", [P, 2 * HW], F32, ctx) for i in range(2)]
            p_b = ps("p_b", [1, 1024], F32, ctx)
            norm_apply("n0", x_sb, h0, ACT.Relu)
            norm_scales("n1", h0)
            w_in, w_order, w_ready, bias_mm, bias_sb = sem("w_in"), sem("w_order"), sem("w_ready"), sem("bias_mm"), sem("bias_sb")
            dvar, droot = sem("dvar"), sem("droot")
            with nc.Block() as block:
                @block.sync
                def _(sp):
                    for k in range(2):
                        sp.dma_start(wall[:, k, 0:256], a["W1"][k * P:(k + 1) * P, :]).then_inc(w_in, 16)
                        sp.dma_start(wall[:, k, 256:512], a["W2"][k * P:(k + 1) * P, :]).then_inc(w_in, 16)
                    for n, (one, two) in enumerate((("a_src1", "a_src2"), ("a_dst1", "a_dst2"))):
                        for c, name in enumerate((one, two)):
                            row = a[name].rearrange("h c -> (h c)")
                            sp.dma_start(arep[:, n, c * 256:(c + 1) * 256], row.partition_broadcast(P)).then_inc(w_in, 16)
                    sp.dma_start(gb[:, :, 0], a["gamma"].rearrange("(k p) -> p k", k=2)).then_inc(w_in, 16)
                    sp.dma_start(gb[:, :, 1], a["beta"].rearrange("(k p) -> p k", k=2)).then_inc(w_in, 16)

                @block.vector
                def _(dve):
                    o = Order(dve, w_order)
                    dve.wait_ge(w_in, 160)
                    for k in range(2):
                        for n in range(2):
                            o.link(nc.vector.tensor_tensor(aprod[:], wall[:, k, 0:HD], arep[:, n, :], ALU.mult))
                            o.did(nc.vector.tensor_reduce(score_w[:, k, n, 0:4], aprod[:, 0:256].rearrange("p (h c) -> p h c", h=4), AX.X, ALU.add))
                            o.link(nc.vector.tensor_reduce(score_w[:, k, n, 4:12], aprod[:, 256:512].rearrange("p (h c) -> p h c", h=8), AX.X, ALU.add))
                            at = HD + n * HW
                            o.did(nc.vector.tensor_copy(wall[:, k, at:at + 8].rearrange("p (h o) -> p h o", o=2),
                                                        score_w[:, k, n, 0:4].unsqueeze(2).broadcast_to([P, 4, 2])))
                            o.link(nc.vector.tensor_copy(wall[:, k, at + 8:at + 16], score_w[:, k, n, 4:12]))
                    dve.nop().then_inc(w_ready, 1)
                    dve.wait_ge(bias_mm, 1)
                    nc.vector.tensor_copy(bw[:, 0:HD], p_b[:, 0:HD]).then_inc(bias_sb, 1)
                    nc.vector.tensor_copy(bw[:, HD:], p_b[:, 512:512 + 2 * HW]).then_inc(bias_sb, 1)
                    for k in range(2):
                        o.did(nc.vector.tensor_scalar(wall[:, k, :], wall[:, k, :], gb[:, k, 0:1], None, ALU.mult))
                    o.did(nc.vector.tensor_scalar(dsmall[:, 0, :], deg[:], 0.5, None, ALU.is_ge))
                    o.link(nc.vector.tensor_scalar(dsmall[:, 1, :], deg[:], 1.0, None, ALU.max))
                    dve.nop().then_inc(dvar, 1)
                    dve.wait_ge(droot, 1)
                    o.link(nc.vector.reciprocal(dinv[:], dinv[:]))
                    o.link(nc.vector.tensor_tensor(dinv[:], dinv[:], dsmall[:, 0, :], ALU.mult))

                @block.scalar
                def _(act):
                    act.wait_ge(dvar, 1)
                    nc.scalar.activation(dinv[:], dsmall[:, 1, :], ACT.Sqrt).then_inc(droot, 1)

                @block.tensor
                def _(pe):
                    pe.wait_ge(w_ready, 1)
                    for k in range(2):
                        nc.tensor.matmul(p_b[:, 0:HD], gb[:, k, 1:2], wall[:, k, 0:HD], start=(k == 0), stop=(k == 1))
                    for k in range(2):
                        m = nc.tensor.matmul(p_b[:, 512:512 + 2 * HW], gb[:, k, 1:2], wall[:, k, HD:], start=(k == 0), stop=(k == 1))
                    m.then_inc(bias_mm, 1)

            z_ready, zT_ps, zT_sb, tabs_ps, feat_out, score_out = (
                sem("z_ready"), sem("zT_ps"), sem("zT_sb"), sem("tabs_ps"), sem("feat_out"), sem("score_out"))
            row_out = [sem(f"row_out{u}") for u in range(5)]
            x_sum = sem("x_sum")
            R = NT // 5
            with nc.Block() as block:
                @block.scalar
                def _(act):
                    with act.Fori(0, R) as i:
                        for u in range(5):
                            t = i * 5 + u
                            act.wait_ge(zT_ps, i * 5 + u + 1)
                            nc.scalar.activation(zs[:, u, :], h0[:, bass.ds(t, 1), :].rearrange("p o d -> p (o d)"), ACT.Identity,
                                                 bias=column(shift, t), scale=column(rstd, t)).then_inc(z_ready, 1)
                        for u in range(5):
                            act.wait_ge(tabs_ps, i * 5 + u + 1)
                            act.wait_ge(row_out[u], i * 32)
                            nc.scalar.copy(orow[:, u, 0:HD], p_h[u % 2][:]).then_inc(feat_out, 1)

                @block.tensor
                def _(pe):
                    pe.nop().then_inc(zT_ps, 5)
                    with pe.Fori(0, R) as i:
                        for u in range(5):
                            pe.wait_ge(z_ready, i * 5 + u + 1)
                            pe.wait_ge(zT_sb, i * 5 + u)
                            for k in range(2):
                                m = nc.tensor.transpose(p_zT[0][:, k, :], zs[:, u, k * P:(k + 1) * P], ident[:])
                            m.then_inc(zT_ps, 1)
                            pe.wait_ge(zT_sb, i * 5 + u + 1)
                            if u >= 2:
                                pe.wait_ge(feat_out, i * 5 + u - 1)
                                pe.wait_ge(score_out, i * 5 + u - 1)
                            else:
                                pe.wait_ge(feat_out, i * 5)
                                pe.wait_ge(score_out, i * 5)
                            for w, target in ((slice(0, HD), p_h[u % 2]), (slice(HD, HD + 2 * HW), p_s[u % 2])):
                                for k in range(2):
                                    nc.tensor.matmul(target[:], zT[:, u, k, :], wall[:, k, w], start=(k == 0), stop=False)
                                m = nc.tensor.matmul(target[:], ones[0:1, :], bw[:, w], start=False, stop=True)
                            m.then_inc(tabs_ps, 1)

                @block.vector
                def _(dve):
                    with dve.Fori(0, R) as i:
                        for u in range(5):
                            t = i * 5 + u
                            dve.wait_ge(zT_ps, 5 + i * 5 + u + 1)
                            nc.vector.tensor_copy(zT[:, u], p_zT[0][:]).then_inc(zT_sb, 1)
                            dve.wait_ge(tabs_ps, i * 5 + u + 1)
                            dve.wait_ge(row_out[u], i * 32)
                            nc.vector.tensor_copy(orow[:, u, HD:], p_s[u % 2][:, 0:HW])
                            nc.vector.tensor_copy(srow[:, u, 0:HW], p_s[u % 2][:, 0:HW])
                            nc.vector.tensor_copy(srow[:, u, HW:SROW], column(dinv, t).broadcast_to([P, SROW - HW]))
                            nc.vector.tensor_copy(tab[:, bass.ds(t, 1), 0:HW].rearrange("p o h -> p (o h)"),
                                                  p_s[u % 2][:, HW:]).then_inc(score_out, 1)
                    nc.vector.tensor_tensor(x_sb[:], x_sb[:], h0[:], ALU.add).then_inc(x_sum, 1)

                @block.sync
                def _(sp):
                    with sp.Fori(0, R) as i:
                        for u in range(5):
                            t = i * 5 + u
                            sp.wait_ge(feat_out, i * 5 + u + 1)
                            sp.wait_ge(score_out, i * 5 + u + 1)
                            sp.dma_start(att_dram[bass.ds(t * P, P), :], orow[:, u, :]).then_inc(row_out[u], 16)
                            sp.dma_start(score_dram[bass.ds(t * P, P), :], srow[:, u, :]).then_inc(row_out[u], 16)
                    for u in range(5):
                        sp.wait_ge(row_out[u], 32 * R)
        end_stage()

        G4 = S // 4
        with ExitStack() as ctx:
            top_acc = sb("top_acc", [P, NT, SROW], F32, ctx)
            idx = [sb(f"idx{q}", [P, 4], I32, ctx) for q in range(2)]
            score_g = [sb(f"score_g{q}", [P, 4, SROW], F32, ctx) for q in range(2)]
            pen = [sb(f"pen{q}", [HW, 4 * P], F32, ctx) for q in range(2)]
            run = [sb(f"run{q}", [HW, 4 * P], F32, ctx) for q in range(2)]
            hot = [sb(f"hot{q}", [P, 4, P], F32, ctx) for q in range(2)]
            rhs = [sb(f"rhs{q}", [P, 4, SROW], F32, ctx) for q in range(2)]
            key_rep = [sb(f"key_rep{q}", [P, 4, P], F32, ctx) for q in range(2)]
            same = sb("same", [P, 4, P], F32, ctx)
            earlier = sb("earlier", [P, 4, P], F32, ctx)
            number = [sb(f"number{q}", [P, 4], F32, ctx) for q in range(2)]
            prior = sb("prior", [P, 4], F32, ctx)
            place_f = sb("place_f", [P, 4], F32, ctx)
            no_edge = sb("no_edge", [P, NT], F32, ctx)
            place = [sb(f"place{q}", [P, 4], I32, ctx) for q in range(2)]
            own_place = sb("own_place", [P, 1], F32, ctx)
            p_in = [ps(f"p_in{q}", [HW, 4 * P], F32, ctx) for q in range(2)]
            p_run = [ps(f"p_run{q}", [P, 4, HW], F32, ctx) for q in range(2)]
            p_top = [ps(f"p_top{q}", [P, 4, SROW], F32, ctx) for q in range(2)]
            idx_ready, scores_in = sem("a_idx_ready"), [sem(f"a_scores_in{q}") for q in range(2)]
            rep_in = [sem(f"a_rep_in{q}") for q in range(2)]
            turned_in, run_ready, run_turned, rhs_ready, tops, added = (
                sem("a_turned_in"), sem("a_run_ready"), sem("a_run_turned"), sem("a_rhs_ready"), sem("a_tops"), sem("a_added"))
            place_ready, placed, a_order = sem("a_place_ready"), sem("a_placed"), sem("a_order")
            keys_used, self_in, loops = sem("a_keys_used"), sem("a_self_in"), sem("a_loops")
            scores_used, places_free = sem("a_scores_used"), sem("a_places_free")
            with nc.Block() as block:
                @block.sync
                def _(sp):
                    sp.dma_start(self_s[:], score_dram.rearrange("(t p) s -> p t s", p=P)[:, :, 0:HW]).then_inc(self_in, 16)
                    with sp.Fori(0, G4 // 2) as i:
                        for q in range(2):
                            g = i * 2 + q
                            sp.wait_ge(keys_used, g)
                            sp.dma_start(pen[q][:], pen_dram[bass.ds(g * 4 * P, 4 * P)].partition_broadcast(HW)).then_inc(rep_in[q], 16)
                            sp.dma_start(key_rep[q][:].rearrange("p u e -> p (u e)"),
                                         key_dram[bass.ds(g * 4 * P, 4 * P)].partition_broadcast(P)).then_inc(rep_in[q], 16)

                @block.scalar
                def _(act):
                    with act.Fori(0, G4 // 2) as i:
                        for q in range(2):
                            g = i * 2 + q
                            act.wait_ge(scores_in[q], i * 64)
                            nc.scalar.copy(idx[q][:], src_step[:, bass.ds(g * 4, 4)]).then_inc(idx_ready, 1)
                    act.wait_ge(loops, 1)
                    nc.scalar.activation(self_s[:], self_s[:], ACT.Exp)

                @block.gpsimd
                def _(pool):
                    def gather(q, u):
                        nc.gpsimd.indirect_dma_start(
                            score_g[q][:, u, :], None, score_dram,
                            bass.IndirectOffsetOnAxis(ap=idx[q][:, u:u + 1].bitcast(U32), axis=0)).then_inc(scores_in[q], 16)

                    def scatter(g, q, u):
                        pool.wait_ge(placed, (g * 4 + u) * 16)
                        pool.nop().then_inc(places_free if u == 0 else waits_passed, 1)
                        nc.gpsimd.indirect_dma_start(
                            count_dram, bass.IndirectOffsetOnAxis(ap=place[q][:, u:u + 1].bitcast(U32), axis=0),
                            number[q][:, u:u + 1], None, compute_op=ALU.add).then_inc(placed, 16)

                    def scatter_and_gather_ahead(g, q, ahead):
                        pool.wait_ge(place_ready, g + 1)
                        if ahead:
                            pool.wait_ge(idx_ready, g + 2)
                            pool.wait_ge(scores_used, g + 1)
                            pool.nop().then_inc(waits_passed, 1)
                        for u in range(4):
                            if ahead:
                                gather(1 - q, u)
                            scatter(g, q, u)

                    pool.wait_ge(idx_ready, 1)
                    for u in range(4):
                        gather(0, u)
                    pool.wait_ge(zeros_out, 16 * (NZ + 1))
                    with pool.Fori(0, G4 // 2 - 1) as i:
                        for q in range(2):
                            scatter_and_gather_ahead(i * 2 + q, q, True)
                    scatter_and_gather_ahead(G4 - 2, 0, True)
                    scatter_and_gather_ahead(G4 - 1, 1, False)
                    pool.wait_ge(placed, G4 * 64)

                @block.tensor
                def _(pe):
                    with pe.Fori(0, G4 // 2) as i:
                        for q in range(2):
                            g = i * 2 + q
                            pe.wait_ge(scores_in[q], i * 64 + 64)
                            for u in range(4):
                                m = nc.tensor.transpose(p_in[q][:, u * P:(u + 1) * P], score_g[q][:, u, 0:HW], ident[:])
                            m.then_inc(turned_in, 1)
                            pe.wait_ge(run_ready, g + 1)
                            for u in range(4):
                                m = nc.tensor.matmul(p_run[q][:, u, :], run[q][:, u * P:(u + 1) * P], ident[0:HW, 0:HW], start=True, stop=True)
                            m.then_inc(run_turned, 1)
                            pe.wait_ge(rhs_ready, g + 1)
                            for u in range(4):
                                m = nc.tensor.matmul(p_top[q][:, u, :], hot[q][:, u, :], rhs[q][:, u, :], start=True, stop=True)
                            m.then_inc(tops, 1)

                @block.vector
                def _(dve):
                    o = Order(dve, a_order)
                    TT, TS = nc.vector.tensor_tensor, nc.vector.tensor_scalar
                    dve.nop().then_inc(keys_used, 1)
                    dve.nop().then_inc(scores_used, 1)
                    o.did(nc.vector.memset(top_acc[:], 0.0))
                    o.did(nc.vector.memset(run[1][:], 0.0))
                    o.link(TS(own_place[:], pidx[:], float(KD), None, ALU.add))
                    with dve.Fori(0, G4 // 2) as i:
                        o.enter(i, 2 * 7)
                        tiles = read_registers(nc, step_table, i * 8, 8, ET.DVE, NT - 1)
                        for q in range(2):
                            g = i * 2 + q
                            grp = bass.ds(g * 4, 4)
                            spread = [P, 4, P]
                            TT(hot[q][:], iota_row[:].unsqueeze(1).broadcast_to(spread),
                               dl_step[:, grp].unsqueeze(2).broadcast_to(spread), ALU.is_equal)
                            dve.wait_ge(rep_in[q], i * 32 + 32)
                            dve.wait_ge(turned_in, g + 1)
                            nc.vector.tensor_tensor_scan(run[q][:], pen[q][:], p_in[q][:], run[1 - q][:, 4 * P - 1:4 * P],
                                                         ALU.add, ALU.max).then_inc(run_ready, 1)
                            here = key_step[:, grp]
                            o.link(TT(same[:], key_rep[q][:], here.unsqueeze(2).broadcast_to(spread), ALU.is_equal))
                            o.did(TT(earlier[:], same[:], lower[:].unsqueeze(1).broadcast_to(spread), ALU.mult))
                            dve.wait_ge(places_free, g)
                            nc.vector.tensor_reduce(number[q][:], same[:], AX.X, ALU.add)
                            o.need(o.n)
                            o.link(nc.vector.tensor_reduce(prior[:], earlier[:], AX.X, ALU.add))
                            o.link(TS(prior[:], prior[:], 0.5, None, ALU.is_lt))
                            o.link(TT(place_f[:], here, own_place[:].broadcast_to([P, 4]), ALU.subtract))
                            o.link(TT(place_f[:], place_f[:], prior[:], ALU.mult))
                            o.link(TT(place[q][:], place_f[:], own_place[:].broadcast_to([P, 4]), ALU.add))
                            dve.nop().then_inc(place_ready, 1)
                            dve.wait_ge(run_ready, g + 1)
                            dve.nop().then_inc(keys_used, 1)
                            TT(rhs[q][:, :, HW:SROW], attr4_step[:, grp, :], score_g[q][:, :, HW:HW + 1].broadcast_to([P, 4, 4]), ALU.mult)
                            dve.wait_ge(run_turned, g + 1)
                            TT(rhs[q][:, :, 0:HW], p_run[q][:], last_step[:, grp].unsqueeze(2).broadcast_to([P, 4, HW]),
                               ALU.mult).then_inc(rhs_ready, 1)
                            dve.wait_ge(rhs_ready, g + 1)
                            dve.nop().then_inc(scores_used, 1)
                            dve.wait_ge(tops, g + 1)
                            for u in range(4):
                                acc = top_acc[:, bass.ds(tiles[q * 4 + u], 1), :].rearrange("p o s -> p (o s)")
                                TT(acc, acc, p_top[q][:, u, :], ALU.add).then_inc(added, 1)
                                dve.wait_ge(added, g * 4 + u + 1)
                        o.leave(G4 // 2)
                    lo, hi = tab[:, :, 0:HW], tab[:, :, HW:]
                    every = [P, NT, HW]
                    dve.wait_ge(self_in, 16)
                    o.link(TS(no_edge[:], deg[:], 0.5, -BIG, ALU.is_lt, ALU.mult))
                    o.link(TT(hi, top_acc[:, :, 0:HW], no_edge[:].unsqueeze(2).broadcast_to(every), ALU.add))
                    o.link(TT(hi, hi, self_s[:], ALU.max))
                    o.did(TT(hi, hi, lo, ALU.add))
                    o.link(TT(self_s[:], self_s[:], lo, ALU.add))
                    o.did(nc.vector.scalar_tensor_tensor(self_s[:], self_s[:], 0.2, self_s[:], ALU.mult, ALU.max))
                    o.link(nc.vector.scalar_tensor_tensor(hi, hi, 0.2, hi, ALU.mult, ALU.max))
                    TT(self_s[:], self_s[:], hi, ALU.subtract).then_inc(loops, 1)
                    o.link(nc.vector.tensor_copy(F_sb[:], top_acc[:, :, HW:]))
        end_stage()

        with ExitStack() as ctx:
            acc = sb("acc", [P, NT, ROW], F32, ctx)
            with ExitStack() as inner:
                idx = [sb(f"b_idx{q}", [P, 4], I32, inner) for q in range(2)]
                row_g = [sb(f"row_g{q}", [P, 4, ROW], F32, inner) for q in range(2)]
                hot = [sb(f"b_hot{q}", [P, 4, P], F32, inner) for q in range(2)]
                hotT = [sb(f"b_hotT{q}", [P, 4, P], F32, inner) for q in range(2)]
                zz = sb("zz", [P, 4, HW], F32, inner)
                weight = [sb(f"weight{q}", [P, 4, HW], F32, inner) for q in range(2)]
                msg = [sb(f"msg{q}", [P, 4, HD], F32, inner) for q in range(2)]
                p_turn = ps("b_p_turn", [P, 4, P], F32, inner)
                p_tab = ps("b_p_tab", [P, 4, 2 * HW], F32, inner)
                p_out = [ps(f"b_p_out{v}", [P, HD], F32, inner) for v in range(2)]
                p_den = [ps(f"b_p_den{v}", [P, HW], F32, inner) for v in range(2)]
                idx_ready, rows_in_q = sem("b_idx_ready"), [sem(f"b_rows_in{q}") for q in range(2)]
                hot_ready, hot_turned, hotT_ready, tab_ready, arg_ready, weight_ready, msg_ready, sums_ready, added = (
                    sem("b_hot_ready"), sem("b_hot_turned"), sem("b_hotT_ready"), sem("b_tab_ready"), sem("b_arg_ready"),
                    sem("b_weight_ready"), sem("b_msg_ready"), sem("b_sums_ready"), sem("b_added"))
                rows_used, b_order, own_in = sem("b_rows_used"), sem("b_order"), sem("b_own_in")
                with nc.Block() as block:
                    @block.sync
                    def _(sp):
                        sp.dma_start(acc[:], att_dram.rearrange("(t p) s -> p t s", p=P)).then_inc(own_in, 16)

                    @block.scalar
                    def _(act):
                        def indices(g, q, i):
                            act.wait_ge(rows_in_q[q], i * 64)
                            nc.scalar.copy(idx[q][:], src_step[:, bass.ds(g * 4, 4)]).then_inc(idx_ready, 1)

                        indices(0, 0, 0)
                        with act.Fori(0, G4 // 2) as i:
                            for q in range(2):
                                g = i * 2 + q
                                if q == 0:
                                    indices(g + 1, 1, i)
                                else:
                                    act.wait_ge(rows_in_q[0], i * 64 + 64)
                                    nc.scalar.copy(idx[0][:], src_step[:, bass.ds((g + 1) * 4 % S, 4)]).then_inc(idx_ready, 1)
                                act.wait_ge(hot_turned, g + 1)
                                nc.scalar.copy(hotT[q][:], p_turn[:]).then_inc(hotT_ready, 1)
                                act.wait_ge(arg_ready, g + 1)
                                nc.scalar.activation(weight[q][:], zz[:], ACT.Exp).then_inc(weight_ready, 1)

                    @block.gpsimd
                    def _(pool):
                        with pool.Fori(0, G4 // 2) as i:
                            for q in range(2):
                                g = i * 2 + q
                                pool.wait_ge(idx_ready, g + 1)
                                pool.wait_ge(rows_used, g)
                                pool.nop().then_inc(waits_passed, 1)
                                for u in range(4):
                                    nc.gpsimd.indirect_dma_start(
                                        row_g[q][:, u, :], None, att_dram,
                                        bass.IndirectOffsetOnAxis(ap=idx[q][:, u:u + 1].bitcast(U32), axis=0)).then_inc(rows_in_q[q], 16)

                    @block.tensor
                    def _(pe):
                        with pe.Fori(0, G4 // 2) as i:
                            tiles = read_registers(nc, step_table, i * 8, 8, ET.PE, NT - 1)
                            for q in range(2):
                                g = i * 2 + q
                                pe.wait_ge(hot_ready, g + 1)
                                for u in range(4):
                                    m = nc.tensor.transpose(p_turn[:, u, :], hot[q][:, u, :], ident[:])
                                m.then_inc(hot_turned, 1)
                                pe.wait_ge(hotT_ready, g + 1)
                                for u in range(4):
                                    m = nc.tensor.matmul(p_tab[:, u, :], hotT[q][:, u, :],
                                                         tab[:, bass.ds(tiles[q * 4 + u], 1), :].rearrange("p o h -> p (o h)"),
                                                         start=True, stop=True)
                                m.then_inc(tab_ready, 1)
                                for u in range(4):
                                    pe.wait_ge(msg_ready, g * 4 + u + 1)
                                    pe.wait_ge(added, g * 4 + u)
                                    nc.tensor.matmul(p_out[u % 2][:], hot[q][:, u, :], msg[q][:, u, :], start=True, stop=True)
                                    nc.tensor.matmul(p_den[u % 2][:], hot[q][:, u, :], weight[q][:, u, :],
                                                     start=True, stop=True).then_inc(sums_ready, 1)

                    @block.vector
                    def _(dve):
                        o = Order(dve, b_order)
                        TT = nc.vector.tensor_tensor
                        dve.nop().then_inc(rows_used, 1)
                        dve.wait_ge(own_in, 16)
                        for t in range(NT):
                            TT(acc[:, t, 0:HD].rearrange("p (h c) -> p h c", h=HW), acc[:, t, 0:HD].rearrange("p (h c) -> p h c", h=HW),
                               self_s[:, t, :].unsqueeze(2).broadcast_to([P, HW, HD // HW]), ALU.mult)
                        nc.vector.tensor_copy(acc[:, :, HD:], self_s[:]).then_inc(added, 1)
                        spread = [P, 4, P]

                        def make_hot(g, q):
                            TT(hot[q][:], iota_row[:].unsqueeze(1).broadcast_to(spread),
                               dl_step[:, bass.ds(g * 4, 4)].unsqueeze(2).broadcast_to(spread), ALU.is_equal).then_inc(hot_ready, 1)

                        make_hot(0, 0)
                        with dve.Fori(0, G4 // 2) as i:
                            o.enter(i, 2 * 3)
                            tiles = read_registers(nc, step_table, i * 8, 8, ET.DVE, NT - 1)
                            for q in range(2):
                                g = i * 2 + q
                                dve.wait_ge(rows_in_q[q], i * 64 + 64)
                                dve.wait_ge(tab_ready, g + 1)
                                o.link(TT(zz[:], p_tab[:, :, 0:HW], row_g[q][:, :, HD:], ALU.add))
                                o.link(nc.vector.scalar_tensor_tensor(zz[:], zz[:], 0.2, zz[:], ALU.mult, ALU.max))
                                o.link(TT(zz[:], zz[:], p_tab[:, :, HW:], ALU.subtract))
                                dve.wait_ge(weight_ready, g)
                                nc.vector.tensor_scalar(zz[:], zz[:], 0.0, None, ALU.min).then_inc(arg_ready, 1)
                                make_hot((g + 1) % G4, 1 - q)
                                dve.wait_ge(weight_ready, g + 1)
                                for u in range(4):
                                    TT(msg[q][:, u, :].rearrange("p (h c) -> p h c", h=HW), row_g[q][:, u, 0:HD].rearrange("p (h c) -> p h c", h=HW),
                                       weight[q][:, u, :].unsqueeze(2).broadcast_to([P, HW, HD // HW]), ALU.mult).then_inc(msg_ready, 1)
                                for u in range(4):
                                    if u == 0:
                                        dve.wait_ge(msg_ready, g * 4 + 4)
                                        dve.nop().then_inc(rows_used, 1)
                                    dve.wait_ge(sums_ready, g * 4 + u + 1)
                                    dve.wait_ge(added, g * 4 + u + 1)
                                    own = acc[:, bass.ds(tiles[q * 4 + u], 1), :].rearrange("p o s -> p (o s)")
                                    TT(own[:, 0:HD], own[:, 0:HD], p_out[u % 2][:], ALU.add)
                                    TT(own[:, HD:], own[:, HD:], p_den[u % 2][:], ALU.add).then_inc(added, 1)
                            o.leave(G4 // 2)
            with ExitStack() as inner:
                wu = sb("wu", [P, 4, D], F32, inner)
                brow = sb("brow", [P, HD + D], F32, inner)
                den = sb("den", [P, NT, HW], F32, inner)
                val = sb("val", [P, 5, HD], F32, inner)
                neg = sb("neg", [P, 5, HD], F32, inner)
                valT = sb("valT", [P, 5, 4, P], F32, inner)
                p_val = [ps(f"p_val{v}", [P, 4, P], F32, inner) for v in range(2)]
                p_uni = [ps(f"p_uni{v}", [P, D], F32, inner) for v in range(2)]
                c_in, c_order, neg_ready, exp_ready, elu_ready, val_turned, valT_ready, uni_ready, x_added = (
                    sem("c_in"), sem("c_order"), sem("neg_ready"), sem("exp_ready"), sem("elu_ready"), sem("val_turned"),
                    sem("valT_ready"), sem("uni_ready"), sem("x_added"))
                with nc.Block() as block:
                    @block.sync
                    def _(sp):
                        sp.dma_start(wu[:], a["Wu"].rearrange("(k p) d -> p k d", k=4)).then_inc(c_in, 16)
                        for name, w in (("b1", slice(0, 256)), ("b2", slice(256, HD)), ("bu", slice(HD, HD + D))):
                            sp.dma_start(brow[:, w], a[name].partition_broadcast(P)).then_inc(c_in, 16)

                    @block.vector
                    def _(dve):
                        o = Order(dve, c_order)
                        TT = nc.vector.tensor_tensor
                        o.link(nc.vector.tensor_scalar(den[:], acc[:, :, HD:], 1e-16, None, ALU.add))
                        o.link(nc.vector.reciprocal(den[:], den[:]))
                        dve.wait_ge(c_in, 64)
                        with dve.Fori(0, R) as i:
                            o.enter(i, 5 * 3)
                            for u in range(5):
                                t = i * 5 + u
                                dve.wait_ge(val_turned, i * 5 + u + 1)
                                o.link(TT(val[:, u, :].rearrange("p (h c) -> p h c", h=HW),
                                          acc[:, bass.ds(t, 1), 0:HD].rearrange("p o (h c) -> p (o h) c", h=HW),
                                          den[:, bass.ds(t, 1), :].rearrange("p o h -> p (o h)").unsqueeze(2).broadcast_to([P, HW, HD // HW]), ALU.mult))
                                o.link(TT(val[:, u, :], val[:, u, :], brow[:, 0:HD], ALU.add))
                                nc.vector.tensor_scalar(neg[:, u, :], val[:, u, :], 0.0, None, ALU.min).then_inc(neg_ready, 1)
                                o.link(nc.vector.tensor_scalar(val[:, u, :], val[:, u, :], 0.0, -1.0, ALU.max, ALU.add))
                                dve.wait_ge(exp_ready, t + 1)
                                TT(val[:, u, :], val[:, u, :], neg[:, u, :], ALU.add).then_inc(elu_ready, 1)
                            for u in range(5):
                                t = i * 5 + u
                                dve.wait_ge(uni_ready, t + 1)
                                own = x_sb[:, bass.ds(t, 1), :].rearrange("p o d -> p (o d)")
                                TT(own, own, p_uni[u % 2][:], ALU.add).then_inc(x_added, 1)
                        o.leave(R)
                        dve.wait_ge(x_added, NT)
                        o.link(TT(x_sb[:], x_sb[:], brow[:, HD:].unsqueeze(1).broadcast_to([P, NT, D]), ALU.add))

                    @block.scalar
                    def _(act):
                        with act.Fori(0, R) as i:
                            for u in range(5):
                                act.wait_ge(neg_ready, i * 5 + u + 1)
                                nc.scalar.activation(neg[:, u, :], neg[:, u, :], ACT.Exp).then_inc(exp_ready, 1)
                            for u in range(5):
                                act.wait_ge(val_turned, 5 + i * 5 + u + 1)
                                nc.scalar.copy(valT[:, u], p_val[u % 2][:]).then_inc(valT_ready, 1)

                    @block.tensor
                    def _(pe):
                        pe.nop().then_inc(val_turned, 5)
                        with pe.Fori(0, R) as i:
                            for u in range(5):
                                t = i * 5 + u
                                pe.wait_ge(elu_ready, t + 1)
                                pe.wait_ge(valT_ready, t if u < 2 else t - 1)
                                for k in range(4):
                                    m = nc.tensor.transpose(p_val[u % 2][:, k, :], val[:, u, k * P:(k + 1) * P], ident[:])
                                m.then_inc(val_turned, 1)
                                pe.wait_ge(valT_ready, t + 1)
                                pe.wait_ge(x_added, t if u < 2 else t - 1)
                                for k in range(4):
                                    m = nc.tensor.matmul(p_uni[u % 2][:], valT[:, u, k, :], wu[:, k, :], start=(k == 0), stop=(k == 3))
                                m.then_inc(uni_ready, 1)
        early.close()

        by_src = dram("by_src", [NP, NP], F16)
        by_dst = dram("by_dst", [NP, NP], F16)
        with ExitStack() as ctx:
            cnt = [sb(f"cnt{q}", [P, NP], F32, ctx) for q in range(2)]
            half = [sb(f"half{q}", [P, NP], F16, ctx) for q in range(2)]
            halfT = [sb(f"halfT{q}", [P, NT, P], F16, ctx) for q in range(2)]
            p_t = [ps(f"cv_p{v}", [P, 5, P], F16, ctx) for v in range(2)]
            cnt_in = [sem(f"cnt_in{q}") for q in range(2)]
            halves, blocks, blocks_out, blocks_free = sem("halves"), sem("blocks"), sem("blocks_out"), sem("blocks_free")
            stored = [sem(f"stored{q}") for q in range(2)]
            with nc.Block() as block:
                def tile_of(i, q):
                    return i * 2 + q

                @block.sync
                def _(sp):
                    def load(t, q):
                        sp.wait_ge(halves, t + 1)
                        sp.nop().then_inc(waits_passed, 1)
                        sp.dma_start(cnt[q][:], count_dram[bass.ds(t * (P * NP), P * NP), :].rearrange("(p f) o -> p (f o)", p=P)).then_inc(cnt_in[q], 16)

                    def store(t, q):
                        sp.wait_ge(halves, t + 3)
                        sp.nop().then_inc(waits_passed, 1)
                        sp.dma_start(by_src[bass.ds(t * P, P), :], half[q][:]).then_inc(stored[q], 16)
                        sp.wait_ge(blocks_out, t * 5 + 5)
                        sp.nop().then_inc(waits_passed, 1)
                        sp.dma_start(by_dst.rearrange("(k p) s -> p k s", p=P)[:, :, bass.ds(t * P, P)], halfT[q][:]).then_inc(stored[q], 16)

                    load(0, 0)
                    with sp.Fori(0, NT // 2) as i:
                        for q in range(2):
                            load(i * 2 + q + 1, 1 - q)
                            store(i * 2 + q, q)
                    store(NT - 1, 0)
                    sp.wait_ge(stored[0], 32 * (NT // 2 + 1))
                    sp.wait_ge(stored[1], 32 * (NT // 2))

                @block.scalar
                def _(act):
                    act.nop().then_inc(halves, 2)

                    def convert(t, q, i):
                        act.wait_ge(cnt_in[q], i * 16 + 16)
                        act.wait_ge(stored[q], i * 32)
                        nc.scalar.activation(half[q][:], cnt[q][:], ACT.Copy, accum_out=column(degsrc, t)).then_inc(halves, 1)

                    with act.Fori(0, NT // 2) as i:
                        for q in range(2):
                            convert(i * 2 + q, q, i)
                    convert(NT - 1, 0, NT // 2)

                @block.tensor
                def _(pe):
                    def turn(t, q):
                        pe.wait_ge(halves, t + 3)
                        for b in range(5):
                            pe.wait_ge(blocks_free, t * 5 + b)
                            for k in range(5):
                                m = nc.tensor.transpose(p_t[(b + q) % 2][:, k, :], half[q][:, (b * 5 + k) * P:(b * 5 + k + 1) * P], ident16[:])
                            m.then_inc(blocks, 1)

                    with pe.Fori(0, NT // 2) as i:
                        for q in range(2):
                            turn(i * 2 + q, q)
                    turn(NT - 1, 0)

                @block.vector
                def _(dve):
                    dve.nop().then_inc(blocks_free, 1)

                    def take(t, q, i):
                        for b in range(5):
                            if b == 0:
                                dve.wait_ge(stored[q], i * 32)
                            dve.wait_ge(blocks, t * 5 + b + 1)
                            nc.vector.tensor_copy(halfT[q][:, b * 5:b * 5 + 5, :], p_t[(b + q) % 2][:]).then_inc(blocks_out, 1)
                            dve.wait_ge(blocks_out, t * 5 + b + 1)
                            dve.nop().then_inc(blocks_free, 1)

                    with dve.Fori(0, NT // 2) as i:
                        for q in range(2):
                            take(i * 2 + q, q, i)
                    take(NT - 1, 0, NT // 2)
        end_stage()

        with ExitStack() as ctx:
            hT = sb("hT", [P, 2, NP], F32, ctx)
            aggT = sb("aggT", [P, 2, NP], F32, ctx)
            parts = sb("parts", [P, NT, 2, 2, P], F16, ctx)
            cbuf = [sb(f"cbuf{q}", [P, NT, W], F16, ctx) for q in range(2)]
            wslot = sb("wslot", [P, 4, D], F32, ctx)
            ewslot = sb("ewslot", [4, D], F32, ctx)
            FT = sb("FT", [4, NP], F32, ctx)
            dinv_rep = sb("dinv_rep", [P, NP], F32, ctx)
            low_sb = [sb(f"low_sb{m}", [P, W], F32, ctx) for m in range(2)]
            rest = [sb(f"rest{v}", [P, 2, P], F32, ctx) for v in range(2)]
            bn_tab = sb("bn_tab", [P, LAYERS, 3, 2], F32, ctx)
            floor = sb("floor", [P, LAYERS], F32, ctx)
            bn_raw = sb("bn_raw", [P, 2, NC, 6], F32, ctx)
            bn_mv = sb("bn_mv", [P, 2, 2], F32, ctx)
            bn_rs = sb("bn_rs", [P, 4, 2], F32, ctx)
            dinv_dram = dram("dinv_dram", [NP], F32)
            p_hi = [ps(f"p_hi{m}", [P, W], F32, ctx) for m in range(2)]
            p_lo = [ps(f"p_lo{m}", [P, W], F32, ctx) for m in range(2)]
            p_new = [ps(f"p_new{m}", [P, W], F32, ctx) for m in range(2)]
            p_turn = [ps(f"l_p_turn{v}", [P, 2, P], F32, ctx) for v in range(2)]

            h1 = aggT[:].rearrange("p m n -> p (m n)").rearrange("p (t d) -> p t d", d=D)
            norm_scales("n2", x_sb)
            norm_apply("n2", x_sb, h1, ACT.Relu)
            s_turned, s_taken, s_in, s_dv = sem("s_turned"), sem("s_taken"), sem("s_in"), sem("s_dv")
            with nc.Block() as block:
                @block.sync
                def _(sp):
                    sp.dma_start(dinv_dram.rearrange("(t p) -> p t", p=P), dinv[:]).then_inc(s_in, 16)
                    sp.wait_ge(s_in, 16)
                    sp.dma_start(dinv_rep[:], dinv_dram.partition_broadcast(P)).then_inc(s_in, 16)
                    for n, name in enumerate(("mlp_b", "bn_g", "bn_b")):
                        for m in range(2):
                            sp.dma_start(bn_tab[:, :, n, m], a[name].rearrange("l (m p) -> m p l", m=2)[m]).then_inc(s_in, 16)
                    sp.wait_ge(s_in, 16 * 8)

                @block.tensor
                def _(pe):
                    for t in range(NT):
                        if t >= 2:
                            pe.wait_ge(s_taken, t - 1)
                        for m in range(2):
                            k = nc.tensor.transpose(p_turn[t % 2][:, m, :], h1[:, t, m * P:(m + 1) * P], ident[:])
                        k.then_inc(s_turned, 1)
                    for t in range(NT):
                        pe.wait_ge(s_taken, NT + t - 1 if t else NT)
                        nc.tensor.transpose(p_turn[t % 2][0:4, 0, :], F_sb[:, t, :], ident[:]).then_inc(s_turned, 1)

                @block.vector
                def _(dve):
                    nc.vector.memset(floor[:], 0.0).then_inc(s_dv, 1)
                    dve.wait_ge(s_dv, 1)
                    nc.vector.memset(floor[:, LAYERS - 1:], -3.0e38)
                    nc.vector.memset(ewslot[:], 0.0)
                    for t in range(NT):
                        dve.wait_ge(s_turned, t + 1)
                        nc.vector.tensor_copy(hT[:, :, t * P:(t + 1) * P], p_turn[t % 2][:]).then_inc(s_taken, 1)
                    for t in range(NT):
                        dve.wait_ge(s_turned, NT + t + 1)
                        nc.vector.tensor_copy(FT[:, t * P:(t + 1) * P], p_turn[t % 2][0:4, 0, :]).then_inc(s_taken, 1)

            (turned, rest_ready, high_ready, low_ready, sums, low_out, agg_ready, news, new_ready, chunk_used, layer_done,
             var_ready, root_ready, bn_order, scaled, w_loaded, w_used) = (sem("l_" + x) for x in (
                 "turned", "rest_ready", "high_ready", "low_ready", "sums", "low_out", "agg_ready", "news", "new_ready", "chunk_used",
                 "layer_done", "var_ready", "root_ready", "bn_order", "scaled", "w_loaded", "w_used"))
            halfway, halfway2 = sem("l_halfway"), sem("l_halfway2")
            chunk_in = [sem(f"l_chunk_in{q}") for q in range(2)]

            def load_chunk(sp, matrix, l, i, q):
                sp.wait_ge(chunk_used, l * NC + i * 2 + q)
                sp.nop().then_inc(waits_passed, 1)
                sp.dma_start(cbuf[q][:], matrix.rearrange("(k p) n -> p k n", p=P)[:, :, bass.ds((i * 2 + q) * W, W)]).then_inc(chunk_in[q], 16)

            def aggregate(pe, l, c, q, edge_term):
                pe.wait_ge(chunk_in[q], l * (16 * NC // 2) + (c - q) * 8 + 16)
                for m in range(2):
                    pe.wait_ge(agg_ready, l * (2 * NC) + c * 2 + m + 1)
                    for k in range(NT):
                        nc.tensor.matmul(p_lo[m][:], parts[:, k, m, 1, :], cbuf[q][:, k, :], start=(k == 0), stop=(k == NT - 1))
                        last = nc.tensor.matmul(p_hi[m][:], parts[:, k, m, 0, :], cbuf[q][:, k, :], start=(k == 0),
                                                stop=(k == NT - 1 and not edge_term))
                    if edge_term:
                        last = nc.tensor.matmul(p_hi[m][:], ewslot[:, m * P:(m + 1) * P], FT[:, bass.ds(c * W, W)], start=False, stop=True)
                    last.then_inc(sums, 1)
                pe.wait_ge(sums, l * (2 * NC) + c * 2 + 2)
                pe.nop().then_inc(chunk_used, 1)

            def take_low(act, l, c):
                for m in range(2):
                    act.wait_ge(sums, l * (2 * NC) + c * 2 + m + 1)
                    act.wait_ge(agg_ready, l * (2 * NC) + c * 2 + m + 1)
                    nc.scalar.mul(low_sb[m][:], p_lo[m][:], 1.0 / LO).then_inc(low_out, 1)

            def sum_up(dve, l, c, by_degree):
                for m in range(2):
                    dve.wait_ge(low_out, l * (2 * NC) + c * 2 + m + 1)
                    part = aggT[:, m, bass.ds(c * W, W)]
                    whole = nc.vector.tensor_tensor(part, p_hi[m][:], low_sb[m][:], ALU.add)
                    if by_degree:
                        whole.then_inc(halfway, 1)
                        dve.wait_ge(halfway, l * (2 * NC) + c * 2 + m + 1)
                        whole = nc.vector.tensor_tensor(part, part, dinv_rep[:, bass.ds(c * W, W)], ALU.mult)
                    whole.then_inc(agg_ready, 1)

            with nc.Block() as block:
                @block.sync
                def _(sp):
                    with sp.Fori(0, LAYERS) as l:
                        sp.wait_ge(w_used, l)
                        sp.nop().then_inc(waits_passed, 1)
                        sp.dma_start(wslot[:], a["mlp_w"][bass.ds(l, 1)].rearrange("l (k p) d -> p (l k) d", p=P)).then_inc(w_loaded, 16)
                        sp.dma_start(ewslot[0:3, P:D], a["ew2"][bass.ds(l, 1)].rearrange("l c d -> (l c) d")).then_inc(w_loaded, 16)
                        sp.dma_start(ewslot[3:4, 0:P], a["ew1"][bass.ds(l, 1)].rearrange("l c d -> (l c) d")).then_inc(w_loaded, 16)
                        with sp.Fori(0, NC // 2) as i:
                            for q in range(2):
                                load_chunk(sp, by_src, l, i, q)

                @block.tensor
                def _(pe):
                    pe.nop().then_inc(chunk_used, 1)

                    def layer_product(l, c):
                        pe.wait_ge(agg_ready, l * (2 * NC) + c * 2 + 4)
                        for m in range(2):
                            pe.wait_ge(new_ready, l * (2 * NC) + c * 2 + m + 1)
                            for k in range(4):
                                state = (hT if k < 2 else aggT)[:, k % 2, bass.ds(c * W, W)]
                                r = nc.tensor.matmul(p_new[m][:], wslot[:, k, m * P:(m + 1) * P], state, start=(k == 0), stop=(k == 3))
                            r.then_inc(news, 1)

                    with pe.Fori(0, LAYERS) as l:
                        pe.wait_ge(layer_done, l)
                        for t in range(NT):
                            pe.wait_ge(rest_ready, l * NT + t + 1)
                            for m in range(2):
                                r = nc.tensor.transpose(p_turn[t % 2][:, m, :], hT[:, m, t * P:(t + 1) * P], ident[:])
                            r.then_inc(turned, 1)
                        pe.wait_ge(w_loaded, l * 48 + 48)
                        pe.wait_ge(low_ready, (l + 1) * NT)
                        aggregate(pe, l, 0, 0, True)
                        with pe.Fori(0, NC // 2 - 1) as i:
                            for q in (1, 0):
                                c = i * 2 + (1 if q else 2)
                                aggregate(pe, l, c, q, True)
                                layer_product(l, c - 1)
                        aggregate(pe, l, NC - 1, 1, True)
                        layer_product(l, NC - 2)
                        layer_product(l, NC - 1)

                @block.scalar
                def _(act):
                    act.nop().then_inc(new_ready, 2)

                    def take_new(l, c):
                        act.wait_ge(news, l * (2 * NC) + c * 2 + 2)
                        act.nop().then_inc(waits_passed, 1)
                        for m in range(2):
                            nc.scalar.activation(hT[:, m, bass.ds(c * W, W)], p_new[m][:], ACT.Relu,
                                                 bias=bn_tab[:, bass.ds(l, 1), 0, m]).then_inc(new_ready, 1)

                    with act.Fori(0, LAYERS) as l:
                        for t in range(NT + 1):
                            if t < NT:
                                act.wait_ge(turned, l * NT + t + 1)
                                nc.scalar.activation(parts[:, t, :, 0, :], p_turn[t % 2][:], ACT.Copy, scale=dinv[:, t:t + 1]).then_inc(high_ready, 1)
                            if t > 0:
                                act.wait_ge(rest_ready, l * NT + t + 2)
                                nc.scalar.mul(parts[:, t - 1, :, 1, :], rest[(t - 1) % 2][:], LO).then_inc(low_ready, 1)
                        take_low(act, l, 0)
                        with act.Fori(0, NC // 2 - 1) as i:
                            for q in (1, 0):
                                c = i * 2 + (1 if q else 2)
                                take_low(act, l, c)
                                take_new(l, c - 1)
                        take_low(act, l, NC - 1)
                        take_new(l, NC - 2)
                        take_new(l, NC - 1)
                        act.wait_ge(var_ready, l + 1)
                        nc.scalar.activation(bn_rs[:, 0, :], bn_rs[:, 3, :], ACT.Sqrt).then_inc(root_ready, 1)
                        act.wait_ge(bn_order, l * 6 + 5)
                        for m in range(2):
                            nc.scalar.activation(hT[:, m, :], hT[:, m, :], ACT.Identity, bias=bn_rs[:, 2, m:m + 1],
                                                 scale=bn_rs[:, 1, m:m + 1]).then_inc(scaled, 1)

                @block.vector
                def _(dve):
                    TT, TS, STT = nc.vector.tensor_tensor, nc.vector.tensor_scalar, nc.vector.scalar_tensor_tensor
                    dve.nop().then_inc(rest_ready, 2)
                    dve.nop().then_inc(agg_ready, 2)
                    o = Order(dve, bn_order)

                    with dve.Fori(0, LAYERS) as l:
                        for t in range(NT):
                            dve.wait_ge(high_ready, l * NT + t + 1)
                            dve.wait_ge(low_ready, l * NT + (t - 1 if t > 1 else 0))
                            STT(rest[t % 2][:], p_turn[t % 2][:], dinv[:, t:t + 1], parts[:, t, :, 0, :], ALU.mult, ALU.subtract).then_inc(rest_ready, 1)
                        with dve.Fori(0, NC) as c:
                            sum_up(dve, l, c, True)
                        o.enter(l, 6)
                        for c in range(NC):
                            for m in range(2):
                                if c % 2 == 0:
                                    dve.wait_ge(new_ready, l * (2 * NC) + c * 2 + 2 + 4) if m == 0 else None
                                n = min(W, N - c * W)
                                k = nc.vector.bn_stats(bn_raw[:, m, c, :], hT[:, m, c * W:c * W + n])
                        o.link(k)
                        dve.nop().then_inc(waits_passed, 1)
                        for m in range(2):
                            k = nc.vector.bn_aggr(bn_mv[:, m, :], bn_raw[:, m].rearrange("p c s -> p (c s)"))
                        o.link(k)
                        o.link(TS(bn_rs[:, 3, :], bn_mv[:, :, 1], EPS, None, ALU.add))
                        dve.nop().then_inc(var_ready, 1)
                        dve.wait_ge(root_ready, l + 1)
                        gain, offset = (bn_tab[:, bass.ds(l, 1), n, :].rearrange("p o m -> p (o m)") for n in (1, 2))
                        nc.vector.reciprocal(bn_rs[:, 1, :], bn_rs[:, 0, :]).then_inc(halfway2, 1)
                        dve.wait_ge(halfway2, l * 3 + 1)
                        TT(bn_rs[:, 1, :], bn_rs[:, 1, :], gain, ALU.mult).then_inc(halfway2, 1)
                        dve.wait_ge(halfway2, l * 3 + 2)
                        TT(bn_rs[:, 2, :], bn_mv[:, :, 0], bn_rs[:, 1, :], ALU.mult).then_inc(halfway2, 1)
                        dve.wait_ge(halfway2, l * 3 + 3)
                        o.link(TT(bn_rs[:, 2, :], offset, bn_rs[:, 2, :], ALU.subtract))
                        dve.nop().then_inc(w_used, 1)
                        dve.nop().then_inc(bn_order, 1)
                        for m in range(2):
                            dve.wait_ge(scaled, l * 2 + m + 1)
                            k = TS(hT[:, m, :], hT[:, m, :], column(floor, l), None, ALU.max)
                        k.then_inc(bn_order, 1)
                        dve.wait_ge(bn_order, l * 6 + 6)
                        dve.nop().then_inc(layer_done, 1)

            with nc.Block() as block:
                @block.tensor
                def _(pe):
                    for t in range(NT):
                        if t >= 2:
                            pe.wait_ge(s_taken, 2 * NT + t - 1)
                        for m in range(2):
                            k = nc.tensor.transpose(p_turn[t % 2][:, m, :], hT[:, m, t * P:(t + 1) * P], ident[:])
                        k.then_inc(s_turned, 1)

                @block.vector
                def _(dve):
                    for t in range(NT):
                        dve.wait_ge(s_turned, 2 * NT + t + 1)
                        nc.vector.tensor_tensor(x_sb[:, t, :].rearrange("p (m d) -> p m d", m=2), x_sb[:, t, :].rearrange("p (m d) -> p m d", m=2),
                                                p_turn[t % 2][:], ALU.add).then_inc(s_taken, 1)
            norm_scales("n3", x_sb)
            norm_apply("n3", x_sb, h1, ACT.Relu)
            split, g_in, g_order = sem("g_split"), sem("g_in"), sem("g_order")
            with ExitStack() as inner:
                gw = sb("gw", [P, 2, D], F32, inner)
                g_brow = sb("g_brow", [P, D], F32, inner)
                inv_deg = sb("inv_deg", [P, NT], F32, inner)
                has_deg = sb("has_deg", [P, NT], F32, inner)
                with nc.Block() as block:
                    @block.sync
                    def _(sp):
                        sp.dma_start(gw[:], a["L2_W"].rearrange("(k p) d -> p k d", k=2)).then_inc(g_in, 16)
                        sp.dma_start(g_brow[:], a["L2_b"].partition_broadcast(P)).then_inc(g_in, 16)
                        sp.wait_ge(g_in, 32)

                    @block.scalar
                    def _(act):
                        h_parts = h1.rearrange("p t (m d) -> p t m d", m=2)
                        nc.scalar.copy(parts[:, :, :, 0, :], h_parts).then_inc(split, 1)
                        act.wait_ge(split, 2)
                        nc.scalar.mul(parts[:, :, :, 1, :], h_parts, LO)

                    @block.vector
                    def _(dve):
                        o = Order(dve, g_order)
                        h_parts = h1.rearrange("p t (m d) -> p t m d", m=2)
                        o.did(nc.vector.tensor_scalar(has_deg[:], degsrc[:], 0.5, None, ALU.is_ge))
                        o.link(nc.vector.tensor_scalar(inv_deg[:], degsrc[:], 1.0, None, ALU.max))
                        o.link(nc.vector.reciprocal(inv_deg[:], inv_deg[:]))
                        o.link(nc.vector.tensor_tensor(inv_deg[:], inv_deg[:], has_deg[:], ALU.mult))
                        dve.wait_ge(split, 1)
                        nc.vector.tensor_tensor(h_parts, h_parts, parts[:, :, :, 0, :], ALU.subtract).then_inc(split, 1)

                with nc.Block() as block:
                    @block.sync
                    def _(sp):
                        with sp.Fori(0, NC // 2) as i:
                            for q in range(2):
                                load_chunk(sp, by_dst, LAYERS, i, q)

                    @block.tensor
                    def _(pe):
                        with pe.Fori(0, NC // 2) as i:
                            for q in range(2):
                                aggregate(pe, LAYERS, i * 2 + q, q, False)

                    @block.scalar
                    def _(act):
                        with act.Fori(0, NC) as c:
                            take_low(act, LAYERS, c)

                    @block.vector
                    def _(dve):
                        with dve.Fori(0, NC) as c:
                            sum_up(dve, LAYERS, c, False)

                p_conv, conv_ready, conv_taken = p_turn, sem("conv_ready"), sem("conv_taken")
                with nc.Block() as block:
                    @block.tensor
                    def _(pe):
                        for t in range(NT):
                            if t >= 2:
                                pe.wait_ge(conv_taken, t - 1)
                            for k in range(2):
                                r = nc.tensor.matmul(p_conv[t % 2][:].rearrange("p m d -> p (m d)"), aggT[:, k, t * P:(t + 1) * P], gw[:, k, :],
                                                     start=(k == 0), stop=(k == 1))
                            r.then_inc(conv_ready, 1)

                    @block.vector
                    def _(dve):
                        STT = nc.vector.scalar_tensor_tensor
                        for t in range(NT):
                            STT(x_sb[:, t, :], g_brow[:], has_deg[:, t:t + 1], x_sb[:, t, :], ALU.mult, ALU.add).then_inc(g_order, 1)
                        for t in range(NT):
                            dve.wait_ge(conv_ready, t + 1)
                            dve.wait_ge(g_order, 4 + t + 1)
                            STT(x_sb[:, t, :], p_conv[t % 2][:].rearrange("p m d -> p (m d)"), inv_deg[:, t:t + 1], x_sb[:, t, :],
                                ALU.mult, ALU.add).then_inc(conv_taken, 1)
        end_stage()

        with ExitStack() as ctx:
            h3 = sb("h3", [P, NT, D], F32, ctx)
            h3T = sb("h3T", [P, 2, NP], F32, ctx)
            m_in = sem("m_in")
            norm_scales("n4", x_sb)
            norm_apply("n4", x_sb, h3, ACT.Relu)

            src_dram = dram("src_dram", [NP, D], F32)
            with ExitStack() as inner:
                dst_part = sb("dst_part", [P, NT, D], F32, inner)
                attr_w = sb("attr_w", [ED, D], F32, inner)
                with ExitStack() as inmost:
                    node_w = sb("node_w", [P, 4, D], F32, inmost)
                    m_brow = sb("m_brow", [P, D], F32, inmost)
                    src_part = sb("src_part", [P, NT, D], F32, inmost)
                    p_turn = [ps(f"m_p_turn{v}", [P, 2, P], F32, inmost) for v in range(2)]
                    p_parts = [[ps(f"m_p_parts{v}{n}", [P, D], F32, inmost) for n in range(2)] for v in range(2)]
                    turned, taken, products, src_ready, dst_ready, src_out = (
                        sem("m_" + x) for x in ("turned", "taken", "products", "src_ready", "dst_ready", "src_out"))
                    with nc.Block() as block:
                        @block.sync
                        def _(sp):
                            sp.dma_start(node_w[:], a["m_W1T"][0:2 * D].rearrange("(k p) d -> p k d", p=P)).then_inc(m_in, 16)
                            sp.dma_start(attr_w[:], a["m_W1T"][2 * D:]).then_inc(m_in, 16)
                            sp.dma_start(m_brow[:], a["m_b1"].partition_broadcast(P)).then_inc(m_in, 16)
                            for part in range(5):
                                sp.wait_ge(src_ready, (part + 1) * 5)
                                sp.dma_start(src_dram.rearrange("(t p) d -> p t d", p=P)[:, part * 5:part * 5 + 5, :],
                                             src_part[:, part * 5:part * 5 + 5, :]).then_inc(src_out, 16)
                            sp.wait_ge(src_out, 80)

                        @block.tensor
                        def _(pe):
                            def turn(t):
                                if t >= 2:
                                    pe.wait_ge(taken, t - 1)
                                for m in range(2):
                                    k = nc.tensor.transpose(p_turn[t % 2][:, m, :], h3[:, t, m * P:(m + 1) * P], ident[:])
                                k.then_inc(turned, 1)

                            turn(0)
                            pe.wait_ge(m_in, 48)
                            for t in range(NT):
                                if t + 1 < NT:
                                    turn(t + 1)
                                pe.wait_ge(taken, t + 1)
                                if t >= 2:
                                    pe.wait_ge(src_ready, t - 1)
                                    pe.wait_ge(dst_ready, t - 1)
                                for n in range(2):
                                    for k in range(2):
                                        r = nc.tensor.matmul(p_parts[t % 2][n][:], h3T[:, k, t * P:(t + 1) * P], node_w[:, 2 * n + k, :],
                                                             start=(k == 0), stop=(k == 1))
                                r.then_inc(products, 1)

                        @block.scalar
                        def _(act):
                            for t in range(NT):
                                act.wait_ge(products, t + 1)
                                nc.scalar.copy(dst_part[:, t, :], p_parts[t % 2][1][:]).then_inc(dst_ready, 1)

                        @block.vector
                        def _(dve):
                            def take(t):
                                dve.wait_ge(turned, t + 1)
                                nc.vector.tensor_copy(h3T[:, :, t * P:(t + 1) * P], p_turn[t % 2][:]).then_inc(taken, 1)

                            take(0)
                            dve.wait_ge(m_in, 48)
                            for t in range(NT):
                                if t + 1 < NT:
                                    take(t + 1)
                                dve.wait_ge(products, t + 1)
                                nc.vector.tensor_tensor(src_part[:, t, :], p_parts[t % 2][0][:], m_brow[:], ALU.add).then_inc(src_ready, 1)

                msg_step = sb("msg_step", [P, S], F32, inner)
                own_row = sb("own_row", [P, 1], F32, inner)
                idx = [sb(f"m_idx{q}", [P, 4], I32, inner) for q in range(2)]
                msg = [sb(f"m_msg{q}", [P, 4, D], F32, inner) for q in range(2)]
                attrT = [sb(f"attrT{q}", [ED, 4, P], F32, inner) for q in range(2)]
                pair = [sb(f"pair{q}", [P, 4, 2, P], F32, inner) for q in range(2)]
                hotT = [sb(f"m_hotT{q}", [P, 4, P], F32, inner) for q in range(2)]
                same = [sb(f"m_same{q}", [P, 4, P], F32, inner) for q in range(2)]
                earlier = sb("m_earlier", [P, 4, P], F32, inner)
                prior = sb("m_prior", [P, 4], F32, inner)
                place_f = sb("m_place_f", [P, 4], F32, inner)
                place = [sb(f"m_place{q}", [P, 4], I32, inner) for q in range(2)]
                merged = [sb(f"merged{q}", [P, 4, D], F32, inner) for q in range(2)]
                valid = sb("m_valid", [P, S], F32, inner)
                p_pre = [ps(f"p_pre{q}", [P, 4, D], F32, inner) for q in range(2)]
                p_merged = [ps(f"p_merged{q}", [P, 4, D], F32, inner) for q in range(2)]
                (m_order, loop_order, idx_ready, hot_ready, place_ready, pair_used, pre_done, pre_added, msg_ready, merge_done, out_ready,
                 places_free) = (sem("e_" + x) for x in (
                     "order", "loop_order", "idx_ready", "hot_ready", "place_ready", "pair_used", "pre_done", "pre_added", "msg_ready", "merge_done",
                     "out_ready", "places_free"))
                rows_in = [sem(f"e_rows_in{q}") for q in range(2)]
                edges_in = [sem(f"e_edges_in{q}") for q in range(2)]
                landed = [sem(f"e_landed{n}") for n in range(RS)]
                with nc.Block() as block:
                    @block.vector
                    def _(dve):
                        o = Order(dve, m_order)
                        TS, STT = nc.vector.tensor_scalar, nc.vector.scalar_tensor_tensor
                        o.did(TS(own_row[:], pidx[:], float(NP), None, ALU.add))
                        o.did(TS(valid[:], dl_step[:], 0.0, None, ALU.is_ge))
                        o.link(nc.vector.tensor_copy(msg_step[:], src_step[:]))
                        o.link(STT(valid[:], dl_step[:], float(P), valid[:], ALU.is_lt, ALU.mult))
                        o.link(TS(msg_step[:], msg_step[:], own_row[:, 0:1], None, ALU.subtract))
                        o.link(nc.vector.tensor_tensor(msg_step[:], msg_step[:], valid[:], ALU.mult))
                        TS(msg_step[:], msg_step[:], own_row[:, 0:1], None, ALU.add)

                with nc.Block() as block:
                    @block.sync
                    def _(sp):
                        def load(g, q, first):
                            sp.wait_ge(pre_done, g)
                            sp.wait_ge(pair_used, g)
                            sp.nop().then_inc(waits_passed, 1)
                            sp.dma_start(pair[q][:].rearrange("p u n e -> p (u n e)"),
                                         pair_dram[bass.ds(g * 4, 4)].rearrange("s n e -> (s n e)").partition_broadcast(P)).then_inc(edges_in[q], 16)
                            for u in range(4):
                                sp.dma_start(attrT[q][:, u, :], a["attr64T"][:, bass.ds(first[u], P)]).then_inc(edges_in[q], 16)

                        with sp.Fori(0, G4 // 2) as i:
                            first = read_registers(nc, step_table, i * 8 + S, 8, ET.SP, (CH - 1) * P)
                            for q in range(2):
                                load(i * 2 + q, q, first[q * 4:q * 4 + 4])

                    @block.gpsimd
                    def _(pool):
                        def gather(g, q, before=0):
                            for n in range(RS):
                                pool.wait_ge(landed[n], before * 16)
                            pool.nop().then_inc(places_free, 1)
                            pool.wait_ge(idx_ready, g + 1)
                            pool.wait_ge(merge_done, g)
                            pool.nop().then_inc(waits_passed, 1)
                            for u in range(4):
                                nc.gpsimd.indirect_dma_start(
                                    msg[q][:, u, :], None, src_dram,
                                    bass.IndirectOffsetOnAxis(ap=idx[q][:, u:u + 1].bitcast(U32), axis=0)).then_inc(rows_in[q], 16)

                        def scatter(g, q):
                            pool.wait_ge(place_ready, g + 1)
                            pool.wait_ge(out_ready, g + 2)
                            for u in range(4):
                                pool.wait_ge(landed[u], g * 16)
                                pool.nop().then_inc(waits_passed, 1)
                                nc.gpsimd.indirect_dma_start(
                                    sums_dram[u], bass.IndirectOffsetOnAxis(ap=place[q][:, u:u + 1].bitcast(U32), axis=0),
                                    merged[q][:, u, :], None, compute_op=ALU.add).then_inc(landed[u], 16)

                        gather(0, 0)
                        pool.wait_ge(sums_zeroed, 16 * RS)
                        with pool.Fori(0, G4 // 2 - 1) as i:
                            for q in range(2):
                                gather(i * 2 + q + 1, 1 - q, i * 2 + q)
                                scatter(i * 2 + q, q)
                        gather(G4 - 1, 1, G4 - 2)
                        scatter(G4 - 2, 0)
                        scatter(G4 - 1, 1)
                        for n in range(RS):
                            pool.wait_ge(landed[n], G4 * 16)

                    @block.scalar
                    def _(act):
                        act.nop().then_inc(out_ready, 1)

                        def indices(g, q, i):
                            act.wait_ge(rows_in[q], i * 64)
                            nc.scalar.copy(idx[q][:], src_step[:, bass.ds(g * 4, 4)]).then_inc(idx_ready, 1)

                        def finish(g, q):
                            act.wait_ge(pre_added, g + 2)
                            nc.scalar.activation(msg[q][:], msg[q][:], ACT.Relu).then_inc(msg_ready, 1)
                            act.wait_ge(merge_done, g + 2)
                            act.wait_ge(places_free, g + 1)
                            nc.scalar.copy(merged[q][:], p_merged[q][:]).then_inc(out_ready, 1)

                        indices(0, 0, 0)
                        with act.Fori(0, G4 // 2 - 1) as i:
                            indices(i * 2 + 1, 1, i)
                            finish(i * 2, 0)
                            indices(i * 2 + 2, 0, i + 1)
                            finish(i * 2 + 1, 1)
                        indices(G4 - 1, 1, G4 // 2 - 1)
                        finish(G4 - 2, 0)
                        finish(G4 - 1, 1)

                    @block.tensor
                    def _(pe):
                        pe.nop().then_inc(pre_done, 1)
                        pe.nop().then_inc(merge_done, 1)

                        def products(g, q, i, tiles):
                            pe.wait_ge(edges_in[q], i * 80 + 80)
                            pe.wait_ge(hot_ready, g + 1)
                            pe.wait_ge(pre_added, g)
                            for u in range(4):
                                nc.tensor.matmul(p_pre[q][:, u, :], hotT[q][:, u, :],
                                                 dst_part[:, bass.ds(tiles[u], 1), :].rearrange("p o d -> p (o d)"), start=True, stop=False)
                                r = nc.tensor.matmul(p_pre[q][:, u, :], attrT[q][:, u, :], attr_w[:], start=False, stop=True)
                            r.then_inc(pre_done, 1)

                        def merge(g, q):
                            pe.wait_ge(msg_ready, g + 1)
                            pe.wait_ge(place_ready, g + 1)
                            pe.wait_ge(out_ready, g)
                            for u in range(4):
                                r = nc.tensor.matmul(p_merged[q][:, u, :], same[q][:, u, :], msg[q][:, u, :], start=True, stop=True)
                            r.then_inc(merge_done, 1)

                        products(0, 0, 0, read_registers(nc, step_table, 0, 4, ET.PE, NT - 1))
                        with pe.Fori(0, G4 // 2 - 1) as i:
                            tiles = read_registers(nc, step_table, i * 8 + 4, 8, ET.PE, NT - 1)
                            products(i * 2 + 1, 1, i, tiles[0:4])
                            merge(i * 2, 0)
                            products(i * 2 + 2, 0, i + 1, tiles[4:8])
                            merge(i * 2 + 1, 1)
                        products(G4 - 1, 1, G4 // 2 - 1, read_registers(nc, step_table, S - 4, 4, ET.PE, NT - 1))
                        merge(G4 - 2, 0)
                        merge(G4 - 1, 1)

                    @block.vector
                    def _(dve):
                        TT, TS = nc.vector.tensor_tensor, nc.vector.tensor_scalar
                        o = Order(dve, loop_order)
                        dve.nop().then_inc(pair_used, 1)
                        dve.nop().then_inc(pre_added, 1)
                        spread = [P, 4, P]

                        def choose(g, q, i):
                            dve.wait_ge(edges_in[q], i * 80 + 80)
                            dve.wait_ge(pre_done, g)
                            TS(hotT[q][:], pair[q][:, :, 0, :], pidx[:, 0:1], None, ALU.is_equal).then_inc(hot_ready, 1)
                            here = msg_step[:, bass.ds(g * 4, 4)]
                            dve.wait_ge(merge_done, g)
                            o.link(TT(same[q][:], pair[q][:, :, 1, :], here.unsqueeze(2).broadcast_to(spread), ALU.is_equal))
                            dve.nop().then_inc(pair_used, 1)
                            o.link(TT(earlier[:], same[q][:], lower[:].unsqueeze(1).broadcast_to(spread), ALU.mult))
                            o.link(nc.vector.tensor_reduce(prior[:], earlier[:], AX.X, ALU.add))
                            o.link(TS(prior[:], prior[:], 0.5, None, ALU.is_lt))
                            o.link(TT(place_f[:], here, own_row[:].broadcast_to([P, 4]), ALU.subtract))
                            o.link(TT(place_f[:], place_f[:], prior[:], ALU.mult))
                            dve.wait_ge(places_free, g + 1)
                            TT(place[q][:], place_f[:], own_row[:].broadcast_to([P, 4]), ALU.add).then_inc(place_ready, 1)

                        def sum_parts(g, q, i):
                            dve.wait_ge(rows_in[q], i * 64 + 64)
                            dve.wait_ge(pre_done, g + 2)
                            for v in range(2):
                                k = TT(msg[q][:, 2 * v:2 * v + 2, :], msg[q][:, 2 * v:2 * v + 2, :], p_pre[q][:, 2 * v:2 * v + 2, :], ALU.add)
                            k.then_inc(pre_added, 1)

                        choose(0, 0, 0)
                        with dve.Fori(0, G4 // 2 - 1) as i:
                            o.enter(i, 12)
                            choose(i * 2 + 1, 1, i)
                            sum_parts(i * 2, 0, i)
                            choose(i * 2 + 2, 0, i + 1)
                            sum_parts(i * 2 + 1, 1, i)
                        o.leave(G4 // 2 - 1)
                        choose(G4 - 1, 1, G4 // 2 - 1)
                        sum_parts(G4 - 2, 0, G4 // 2 - 1)
                        sum_parts(G4 - 1, 1, G4 // 2 - 1)
            w2 = sb("m_w2", [P, 2, D], F32, ctx)
            wi = sb("m_wi", [P, 2, 3 * D], F32, ctx)
            wh = sb("m_wh", [P, 2, 3 * D], F32, ctx)
            b2 = sb("m_b2row", [P, D], F32, ctx)
            bi = sb("m_bi", [P, 3 * D], F32, ctx)
            bh = sb("m_bh", [P, 3 * D], F32, ctx)
            parts_in = [sb(f"parts_in{q}", [P, RS, D], F32, ctx) for q in range(2)]
            agg = [sb(f"u_agg{q}", [P, D], F32, ctx) for q in range(2)]
            aggT = [sb(f"u_aggT{q}", [P, 2, P], F32, ctx) for q in range(2)]
            agg2 = [sb(f"u_agg2{q}", [P, D], F32, ctx) for q in range(2)]
            agg2T = [sb(f"u_agg2T{q}", [P, 2, P], F32, ctx) for q in range(2)]
            hslot = [sb(f"u_hslot{q}", [P, 2, P], F32, ctx) for q in range(2)]
            gates = [sb(f"gates{q}", [P, 2 * D], F32, ctx) for q in range(2)]
            cand = [sb(f"cand{q}", [P, 2 * D], F32, ctx) for q in range(2)]
            p_t = [ps(f"u_p_t{q}", [P, 2, P], F32, ctx) for q in range(2)]
            p_2 = [ps(f"u_p_2{q}", [P, D], F32, ctx) for q in range(2)]
            p_rz = [ps(f"u_p_rz{q}", [P, 2 * D], F32, ctx) for q in range(2)]
            p_n = [ps(f"u_p_n{q}", [P, 2 * D], F32, ctx) for q in range(2)]
            (u_in, u_order, bias_ready, agg_ready, turns, copies, second, agg2_ready, slot_ready, gates_ps, rz_ready, rz_done, tanh_in,
             tanh_done, rows_ready, parts_free) = (sem("u_" + x) for x in (
                 "in", "order", "bias_ready", "agg_ready", "turns", "copies", "second", "agg2_ready", "slot_ready", "gates_ps", "rz_ready",
                 "rz_done", "tanh_in", "tanh_done", "rows_ready", "parts_free"))
            u_parts = [sem(f"u_parts{q}") for q in range(2)]
            stored = sem("stored")

            def each_tile(engine, work):
                with engine.Fori(0, NT // 2) as i:
                    for q in range(2):
                        work(i * 2 + q, q, i)
                work(NT - 1, 0, NT // 2)

            with nc.Block() as block:
                @block.sync
                def _(sp):
                    sp.dma_start(w2[:], a["m_W2T"].rearrange("(k p) d -> p k d", k=2)).then_inc(u_in, 16)
                    sp.dma_start(wi[:], a["m_W_ihT"].rearrange("(k p) d -> p k d", k=2)).then_inc(u_in, 16)
                    sp.dma_start(wh[:], a["m_W_hhT"].rearrange("(k p) d -> p k d", k=2)).then_inc(u_in, 16)
                    for name, row in (("m_b2", b2), ("m_b_ih", bi), ("m_b_hh", bh)):
                        sp.dma_start(row[:], a[name].partition_broadcast(P)).then_inc(u_in, 16)

                    def load(t, q, i):
                        sp.wait_ge(parts_free, t)
                        sp.nop().then_inc(waits_passed, 1)
                        for n in range(RS):
                            sp.dma_start(parts_in[q][:, n, :], sums_dram[n][bass.ds(t * P, P), :]).then_inc(u_parts[q], 16)

                    each_tile(sp, load)

                @block.gpsimd
                def _(pool):
                    def store(t, q, i):
                        pool.wait_ge(rows_ready, t + 1)
                        pool.nop().then_inc(waits_passed, 1)
                        pool.dma_start(out[bass.ds(t * P, P), :], x_sb[:, bass.ds(t, 1), :].rearrange("p o d -> p (o d)")).then_inc(stored, 16)

                    with pool.Fori(0, NT - 1) as t:
                        store(t, 0, 0)
                    pool.wait_ge(rows_ready, NT)
                    pool.dma_start(out[(NT - 1) * P:N, :], x_sb[0:N - (NT - 1) * P, NT - 1, :]).then_inc(stored, 16)
                    pool.wait_ge(stored, 16 * NT)

                @block.tensor
                def _(pe):
                    pe.wait_ge(u_in, 96)

                    def work(t, q, i):
                        pe.wait_ge(agg_ready, t + 1)
                        pe.wait_ge(copies, t * 2)
                        for m in range(2):
                            r = nc.tensor.transpose(p_t[0][:, m, :], agg[q][:, m * P:(m + 1) * P], ident[:])
                        r.then_inc(turns, 1)
                        pe.wait_ge(slot_ready, t + 1)
                        pe.wait_ge(rz_ready, t)
                        pe.wait_ge(tanh_in, t)
                        for k in range(2):
                            nc.tensor.matmul(p_rz[q][:], hslot[q][:, k, :], wh[:, k, 0:2 * D], start=(k == 0), stop=False)
                        for k in range(2):
                            nc.tensor.matmul(p_n[q][:, D:], hslot[q][:, k, :], wh[:, k, 2 * D:], start=(k == 0), stop=(k == 1))
                        pe.wait_ge(copies, t * 2 + 1)
                        pe.wait_ge(agg2_ready, t)
                        for k in range(2):
                            r = nc.tensor.matmul(p_2[q][:], aggT[q][:, k, :], w2[:, k, :], start=(k == 0), stop=(k == 1))
                        r.then_inc(second, 1)
                        pe.wait_ge(agg2_ready, t + 2)
                        for m in range(2):
                            r = nc.tensor.transpose(p_t[1][:, m, :], agg2[q][:, m * P:(m + 1) * P], ident[:])
                        r.then_inc(turns, 1)
                        pe.wait_ge(copies, t * 2 + 2)
                        for k in range(2):
                            nc.tensor.matmul(p_rz[q][:], agg2T[q][:, k, :], wi[:, k, 0:2 * D], start=False, stop=(k == 1))
                        for k in range(2):
                            r = nc.tensor.matmul(p_n[q][:, 0:D], agg2T[q][:, k, :], wi[:, k, 2 * D:], start=(k == 0), stop=(k == 1))
                        r.then_inc(gates_ps, 1)

                    each_tile(pe, work)

                @block.scalar
                def _(act):
                    act.nop().then_inc(gates_ps, 1)

                    def work(t, q, i):
                        act.wait_ge(gates_ps, t)
                        nc.scalar.copy(hslot[q][:], h3T[:, :, bass.ds(t * P, P)]).then_inc(slot_ready, 1)
                        act.wait_ge(turns, t * 2 + 1)
                        nc.scalar.copy(aggT[q][:], p_t[0][:]).then_inc(copies, 1)
                        act.wait_ge(turns, t * 2 + 2)
                        nc.scalar.copy(agg2T[q][:], p_t[1][:]).then_inc(copies, 1)
                        act.wait_ge(rz_ready, t + 2)
                        nc.scalar.activation(gates[q][:], gates[q][:], ACT.Sigmoid).then_inc(rz_done, 1)
                        act.wait_ge(tanh_in, t + 2)
                        nc.scalar.activation(cand[q][:, 0:D], cand[q][:, 0:D], ACT.Tanh).then_inc(tanh_done, 1)

                    each_tile(act, work)

                @block.vector
                def _(dve):
                    TT, STT = nc.vector.tensor_tensor, nc.vector.scalar_tensor_tensor
                    o = Order(dve, u_order)
                    for s in (parts_free, agg2_ready, rz_ready, tanh_in):
                        dve.nop().then_inc(s, 1)
                    dve.wait_ge(u_in, 96)
                    o.link(TT(bh[:, 0:2 * D], bh[:, 0:2 * D], bi[:, 0:2 * D], ALU.add))

                    def work(t, q, i):
                        dve.wait_ge(u_parts[q], i * (16 * RS) + 16 * RS)
                        o.link(TT(parts_in[q][:, 0:2, :], parts_in[q][:, 0:2, :], parts_in[q][:, 2:4, :], ALU.add))
                        TT(agg[q][:], parts_in[q][:, 0, :], parts_in[q][:, 1, :], ALU.add).then_inc(agg_ready, 1)
                        dve.wait_ge(agg_ready, t + 1)
                        dve.nop().then_inc(parts_free, 1)
                        dve.wait_ge(second, t + 1)
                        STT(agg2[q][:], b2[:], column(degsrc, t), p_2[q][:], ALU.mult, ALU.add).then_inc(agg2_ready, 1)
                        dve.wait_ge(gates_ps, t + 2)
                        TT(gates[q][:], p_rz[q][:], bh[:, 0:2 * D], ALU.add).then_inc(rz_ready, 1)
                        TT(cand[q][:, 0:D], p_n[q][:, 0:D], bi[:, 2 * D:], ALU.add)
                        o.link(TT(cand[q][:, D:], p_n[q][:, D:], bh[:, 2 * D:], ALU.add))
                        dve.wait_ge(rz_done, t + 1)
                        o.link(TT(cand[q][:, D:], cand[q][:, D:], gates[q][:, 0:D], ALU.mult))
                        TT(cand[q][:, 0:D], cand[q][:, 0:D], cand[q][:, D:], ALU.add).then_inc(tanh_in, 1)
                        dve.wait_ge(tanh_done, t + 1)
                        own = x_sb[:, bass.ds(t, 1), :].rearrange("p o d -> p (o d)")
                        o.did(TT(own, own, cand[q][:, 0:D], ALU.add))
                        o.link(TT(cand[q][:, D:], h3[:, bass.ds(t, 1), :].rearrange("p o d -> p (o d)"), cand[q][:, 0:D], ALU.subtract))
                        o.link(TT(cand[q][:, D:], cand[q][:, D:], gates[q][:, D:], ALU.mult))
                        TT(own, own, cand[q][:, D:], ALU.add).then_inc(rows_ready, 1)

                    o.enter(0, 0)
                    base = o.base
                    def numbered(t, q, i):
                        o.base, o.n = base + t * 6, 0
                        work(t, q, i)
                        assert o.n == 6

                    each_tile(dve, numbered)


NAMES = {
    "gamma": "L0_gnn_gamma", "beta": "L0_gnn_beta", "W1": "L0_gnn_W1", "a_src1": "L0_gnn_a_src1", "a_dst1": "L0_gnn_a_dst1",
    "b1": "L0_gnn_b1", "W2": "L0_gnn_W2", "a_src2": "L0_gnn_a_src2", "a_dst2": "L0_gnn_a_dst2", "b2": "L0_gnn_b2",
    "Wu": "L0_gnn_Wu", "bu": "L0_gnn_bu",
    "mlp_w": "L1_gnn_mlp_w", "mlp_b": "L1_gnn_mlp_b", "ew1": "L1_gnn_ew1", "ew2": "L1_gnn_ew2", "bn_g": "L1_gnn_bn_g", "bn_b": "L1_gnn_bn_b",
    "L2_W": "L2_gnn_W", "L2_b": "L2_gnn_b",
    "m_b1": "L3_gnn_b1", "m_b2": "L3_gnn_b2", "m_b_ih": "L3_gnn_b_ih", "m_b_hh": "L3_gnn_b_hh",
}
TURNED = {"m_W1T": "L3_gnn_W1", "m_W2T": "L3_gnn_W2", "m_W_ihT": "L3_gnn_W_ih", "m_W_hhT": "L3_gnn_W_hh"}


def kernel(**inputs):
    import concourse.bacc as bacc
    from concourse.bass_utils import run_bass_kernel_spmd

    given = {name: np.asarray(value) for name, value in inputs.items()}

    def padded(array, rows, fill=0):
        whole = np.full((rows,) + array.shape[1:], fill, array.dtype)
        whole[:array.shape[0]] = array
        return whole

    arrays = {
        "x": padded(given["x"], NP),
        "src": padded(given["src"], EP),
        "dst": padded(given["dst"], EP, PADDST),
        "attr4": padded(given["edge_attr_4"], EP),
        "attr64T": np.ascontiguousarray(padded(given["edge_attr_64"], EP).T),
    }
    arrays.update({short: np.ascontiguousarray(given[name]) for short, name in NAMES.items()})
    arrays.update({short: np.ascontiguousarray(given[name].T) for short, name in TURNED.items()})

    nc = bacc.Bacc("TRN2", target_bir_lowering=False, num_devices=1)
    a = {name: nc.dram_tensor("in_" + name, array.shape, mybir.dt.from_np(array.dtype), kind="ExternalInput").ap()
         for name, array in arrays.items()}
    out = nc.dram_tensor("out", [N, D], F32, kind="ExternalOutput").ap()
    program(nc, a, out)
    result = run_bass_kernel_spmd(nc, [{"in_" + name: array for name, array in arrays.items()}], core_ids=[0])
    return result.results[0]["out"]
```

```python
from contextlib import ExitStack

import numpy as np
import concourse.bass as bass
from concourse import mybir

F32 = mybir.dt.float32
F16 = mybir.dt.float16
BF16 = mybir.dt.bfloat16
I32 = mybir.dt.int32
U32 = mybir.dt.uint32
ALU = mybir.AluOpType
ACT = mybir.ActivationFunctionType
AX = mybir.AxisListType
ET = mybir.EngineType

P = 128
N = 3125
NT = -(-N // P)
NP = NT * P
D = 256
E = 53125
CH = -(-E // P)
EP = CH * P
GR = 110
NB = 4
S = GR * NB
assert S >= CH + NT - 1
HJ = 425
HP = E // HJ
HB = 17
HW = 16
HD = 512
ROW = HD + HW
SROW = 20
KD = NP * NP
ZF = 8000
PLAN_CHUNKS = 15
RS = 4
ED = 64
PADDST = 4095
BIG = 1.0e30
EPS = 1e-5
LAYERS = 5
W = 400
NC = NP // W
assert NC * W == NP and NC % 2 == 0
LO = 2048.0
assert HP * HJ == E and HJ % HB == 0


class Order:

    def __init__(self, engine, semaphore):
        self.engine, self.semaphore, self.base, self.n = engine, semaphore, 0, 0

    def did(self, instruction):
        instruction.then_inc(self.semaphore, 1)
        self.n += 1
        return self.n

    def need(self, n):
        self.engine.wait_ge(self.semaphore, self.base + n)

    def link(self, instruction):
        self.need(self.did(instruction))

    def begin(self, per, first=0):
        self.start, self.per = self.base + self.n - first * per, per

    def enter(self, i):
        self.base, self.n = self.start + i * self.per, 0

    def leave(self, rounds):
        assert self.n == self.per, (self.n, self.per)
        self.base, self.n = self.start + rounds * self.per, 0


def looped(engine, rounds, work):
    work(0)
    with engine.Fori(1, rounds) as i:
        work(i)


def column(ap, k):
    return ap[:, bass.ds(k, 1)]


def read_registers(nc, table, at, count, engine, top):
    _, values = nc.values_load_multi_w_load_instructions(
        table[0:1, bass.ds(at, count)], engines=[engine], min_val=0, max_val=top,
        skip_runtime_bounds_check_because="the table is clamped to this range when it is made")
    return values


def program(nc, a, out):
    top = ExitStack()
    with top:
        def sb(name, shape, dt, ctx=top):
            return ctx.enter_context(nc.sbuf_tensor(name, shape, dt))

        def ps(name, shape, dt, ctx):
            return ctx.enter_context(nc.psum_tensor(name, shape, dt))

        def sem(name, over_stages=False):
            handle = nc.alloc_semaphore(name=name)
            (lasting if over_stages else of_stage).append(handle)
            return handle

        def end_stage():
            nc.clear_and_free_semaphores(of_stage)
            of_stage.clear()
            nc.all_engine_barrier()


        def is_first(j):
            return isinstance(j, int) and j == 0

        def dram(name, shape, dt):
            return nc.dram_tensor(name, shape, dt, kind="Internal").ap()

        lasting, of_stage = [], []
        top.enter_context(nc.allow_non_contiguous_dma(reason="small tables and columns, once"))
        x_sb = sb("x_sb", [P, NT, D], F32)
        iota_row = sb("iota_row", [P, P], F32)
        pidx = sb("pidx", [P, 1], F32)
        ident = sb("ident", [P, P], F32)
        ident16 = sb("ident16", [P, P], F16)
        lower = sb("lower", [P, P], F32)
        ones = sb("ones", [P, P], F32)
        deg = sb("deg", [P, NT], F32)
        dinv = sb("dinv", [P, NT], F32)
        step_table = sb("step_table", [1, 2 * S], I32)
        src_step = sb("src_step", [P, S], I32)
        dl_step = sb("dl_step", [P, S], F32)
        F_sb = sb("F_sb", [P, NT, 4], F32)
        degsrc = sb("degsrc", [P, NT], F32)
        rstd = sb("rstd", [P, NT], F32)
        shift = sb("shift", [P, NT], F32)
        stats = sb("stats", [P, NT, 6], F32)
        norm_small = sb("norm_small", [P, 5, NT], F32)
        tab = sb("tab", [P, NT, 2 * HW], F32)
        early = top.enter_context(ExitStack())
        zeros = sb("zeros", [P, ZF], F32, early)
        waits_passed = sem("waits_passed", True)
        key_step = sb("key_step", [P, S], F32, early)
        last_step = sb("last_step", [P, S], F32, early)
        attr4_step = sb("attr4_step", [P, S, 4], F32, early)
        self_s = sb("self_s", [P, NT, HW], F32, early)

        step_dram = dram("step_dram", [2 * S], I32)
        pen_dram = dram("pen_dram", [S * P], F32)
        key_dram = dram("key_dram", [S * P], F32)
        pair_dram = dram("pair_dram", [S, 2, P], F32)
        sums_dram = [dram(f"sums_dram{n}", [NP + P, D], F32) for n in range(RS)]
        seg_dram = dram("seg_dram", [S * P + 2], F32)
        att_dram = dram("att_dram", [NP, ROW], F32)
        score_dram = dram("score_dram", [NP, SROW], F32)
        count_dram = dram("count_dram", [KD + P, 1], F32)

        with ExitStack() as ctx:
            iota_i = sb("iota_i", [P, P], I32, ctx)
            pidx_i = sb("pidx_i", [P, 1], I32, ctx)
            dst_i = sb("dst_i", [HP, HJ], I32, ctx)
            lo_i = sb("lo_i", [HP, HJ], I32, ctx)
            hi_i = sb("hi_i", [HP, HJ], I32, ctx)
            lo_f = sb("lo_f", [HP, HJ], F32, ctx)
            hi_f = sb("hi_f", [HP, HJ], F32, ctx)
            lo_hot = sb("lo_hot", [HP, 2, HB, P], BF16, ctx)
            hi_hot = sb("hi_hot", [HP, 2, HB, NT], BF16, ctx)
            hist = ps("hist", [P, NT], F32, ctx)
            dst_in, x_in, iota_made = sem("dst_in"), sem("x_in"), sem("iota_made")
            count_order, hots_ready, hots_used = sem("count_order"), sem("hots_ready"), sem("hots_used")
            sums_zeroed = sem("sums_zeroed", True)
            zeros_ready, zeros_out, hist_zero = sem("zeros_ready"), sem("zeros_out", True), sem("hist_zero")
            NZ = KD // (P * ZF)
            with nc.Block() as block:
                @block.sync
                def _(sp):
                    sp.dma_start(dst_i[:], a["dst"][0:E].rearrange("(p j) -> p j", p=HP)).then_inc(dst_in, 16)
                    sp.dma_start(x_sb[:], a["x"].rearrange("(t p) d -> p t d", p=P)).then_inc(x_in, 16)
                    sp.wait_ge(zeros_ready, 1)
                    whole = count_dram[0:KD, :].rearrange("(z p f) o -> z p (f o)", z=NZ, p=P)
                    with sp.Fori(0, NZ) as z:
                        sp.dma_start(whole[bass.ds(z, 1)].rearrange("z p f -> (z p) f"), zeros[:]).then_inc(zeros_out, 16)
                    sp.dma_start(count_dram[KD:KD + P, :], zeros[:, 0:1]).then_inc(zeros_out, 16)
                    width = (NP + P) * D // P
                    for n in range(RS):
                        sp.dma_start(sums_dram[n].rearrange("(p r) d -> p (r d)", p=P), zeros[:, 0:width]).then_inc(sums_zeroed, 16)
                    sp.wait_ge(x_in, 16)

                @block.gpsimd
                def _(pool):
                    nc.gpsimd.memset(zeros[:], 0.0).then_inc(zeros_ready, 1)
                    nc.gpsimd.iota(iota_i[:], pattern=[[1, P]], base=0, channel_multiplier=0).then_inc(iota_made, 1)
                    nc.gpsimd.iota(pidx_i[:], pattern=[[0, 1]], base=0, channel_multiplier=1).then_inc(iota_made, 1)

                @block.vector
                def _(dve):
                    o = Order(dve, count_order)
                    nc.vector.memset(hist[:], 0.0).then_inc(hist_zero, 1)
                    dve.wait_ge(iota_made, 2)
                    o.did(nc.vector.tensor_copy(iota_row[:], iota_i[:]))
                    o.did(nc.vector.memset(ones[:], 1.0))
                    o.link(nc.vector.tensor_copy(pidx[:], pidx_i[:]))
                    o.did(nc.vector.tensor_scalar(ident[:], iota_row[:], pidx[:, 0:1], None, ALU.is_equal))
                    o.did(nc.vector.tensor_scalar(ident16[:], iota_row[:], pidx[:, 0:1], None, ALU.is_equal))
                    o.did(nc.vector.tensor_scalar(lower[:], iota_row[:], pidx[:, 0:1], None, ALU.is_lt))
                    dve.wait_ge(dst_in, 16)
                    o.did(nc.vector.tensor_scalar(lo_i[:], dst_i[:], P - 1, None, ALU.bitwise_and))
                    o.link(nc.vector.tensor_scalar(hi_i[:], dst_i[:], 7, None, ALU.logical_shift_right))
                    o.did(nc.vector.tensor_copy(lo_f[:], lo_i[:]))
                    o.link(nc.vector.tensor_copy(hi_f[:], hi_i[:]))
                    with dve.Fori(0, HJ // HB) as b:
                        with_slot = bass.ds(b % 2, 1)
                        dve.wait_ge(hots_used, b + 1)
                        nc.vector.tensor_tensor(
                            lo_hot[:, with_slot].rearrange("p o j n -> p (o j) n"),
                            iota_row[0:HP].unsqueeze(1).broadcast_to([HP, HB, P]),
                            lo_f[:, bass.ds(b * HB, HB)].unsqueeze(2).broadcast_to([HP, HB, P]), ALU.is_equal)
                        nc.vector.tensor_tensor(
                            hi_hot[:, with_slot].rearrange("p o j n -> p (o j) n"),
                            iota_row[0:HP, 0:NT].unsqueeze(1).broadcast_to([HP, HB, NT]),
                            hi_f[:, bass.ds(b * HB, HB)].unsqueeze(2).broadcast_to([HP, HB, NT]),
                            ALU.is_equal).then_inc(hots_ready, 1)
                    dve.wait_ge(hots_used, HJ // HB + 2)
                    nc.vector.tensor_copy(deg[:], hist[:])

                @block.tensor
                def _(pe):
                    pe.wait_ge(hist_zero, 1)
                    pe.nop().then_inc(hots_used, 2)
                    with pe.Fori(0, HJ // HB) as b:
                        pe.wait_ge(hots_ready, b + 1)
                        for j in range(HB):
                            last = nc.tensor.matmul(
                                hist[:], lo_hot[:, bass.ds(b % 2, 1), j, :].rearrange("p o n -> p (o n)"),
                                hi_hot[:, bass.ds(b % 2, 1), j, :].rearrange("p o n -> p (o n)"),
                                start=False, stop=True, skip_group_check=True)
                        last.then_inc(hots_used, 1)

        with ExitStack() as ctx:
            col = sb("col", [NT, 8], F32, ctx)
            col_i = sb("col_i", [NT, 4], I32, ctx)
            chunks_bc = sb("chunks_bc", [NT, P], F32, ctx)
            first_bc = sb("first_bc", [NT, P], F32, ctx)
            tri_ex = sb("tri_ex", [NT, NT], F32, ctx)
            tri_in = sb("tri_in", [NT, NT], F32, ctx)
            base_row = sb("base_row", [GR, NT], F32, ctx)
            incl_row = sb("incl_row", [GR, NT], F32, ctx)
            step_i = sb("step_i", [GR, NB], I32, ctx)
            step_f = sb("step_f", [GR, NB], F32, ctx)
            sel = sb("sel", [GR, NB, NT], F32, ctx)
            tile_f = sb("tile_f", [GR, NB], F32, ctx)
            tile_c = sb("tile_c", [GR, NB], F32, ctx)
            chunk_f = sb("chunk_f", [GR, NB], F32, ctx)
            chunk_i = sb("chunk_i", [GR, NB], I32, ctx)
            table_i = sb("table_i", [GR, 2, NB], I32, ctx)
            srcrow = sb("srcrow", [GR, NB, P], I32, ctx)
            dstrow = sb("dstrow", [GR, NB, P], I32, ctx)
            attrrow = sb("attrrow", [GR, NB, P, 4], F32, ctx)
            src_f = sb("src_f", [GR, NB, P], F32, ctx)
            dl_row = sb("dl_row", [GR, NB, P], F32, ctx)
            seg_row = sb("seg_row", [GR, NB, P], F32, ctx)
            key_row = sb("key_row", [GR, NB, P], F32, ctx)
            v1 = sb("v1", [GR, NB, P], F32, ctx)
            v2 = sb("v2", [GR, NB, P], F32, ctx)
            before = sb("before", [GR, NB, P], F32, ctx)
            after = sb("after", [GR, NB, P], F32, ctx)
            last_row = sb("last_row", [GR, NB, P], F32, ctx)
            msg_row = sb("msg_row", [GR, NB, P], F32, ctx)
            ends = sb("ends", [1, 2], F32, ctx)
            tile_off = sb("tile_off", [GR, NB], F32, ctx)
            few = ps("few", [P, 512], F32, ctx)
            turned = [ps(f"turned{i}", [P, 512], F32, ctx) for i in range(4)]
            plan = sem("plan")
            pe_few, rows_in, table_out, table_in = sem("pe_few"), sem("rows_in"), sem("table_out"), sem("table_in")
            seg_out, seg_in, pen_out, turned_ready, turned_used = (
                sem("seg_out"), sem("seg_in"), sem("pen_out"), sem("turned_ready"), sem("turned_used"))
            steps_made = sem("steps_made")
            row_ready = sem("row_ready")
            COUNT, START, END, CHUNKS, FIRST, SOME = range(6)
            with nc.Block() as block:
                @block.gpsimd
                def _(pool):
                    nc.gpsimd.iota(step_i[:], pattern=[[GR, NB]], base=0, channel_multiplier=1).then_inc(steps_made, 1)
                    pool.wait_ge(row_ready, 1)
                    for b in range(NB):
                        for rows, name in ((srcrow[:, b, :], "src"), (dstrow[:, b, :], "dst"),
                                           (attrrow[:, b].rearrange("p e c -> p (e c)"), "attr4")):
                            table = a[name].rearrange("(c e) -> c e", c=CH) if name != "attr4" else \
                                a[name].rearrange("(c e) f -> c (e f)", c=CH)
                            nc.gpsimd.indirect_dma_start(
                                rows, None, table, bass.IndirectOffsetOnAxis(ap=chunk_i[:, b:b + 1].bitcast(U32), axis=0)
                            ).then_inc(rows_in, 16)

                @block.tensor
                def _(pe):
                    nc.tensor.matmul(few[0:NT, 0:1], deg[:], ones[:, 0:1], start=True, stop=True).then_inc(pe_few, 1)
                    pe.wait_ge(plan, 3)
                    nc.tensor.matmul(few[0:NT, 1:2], tri_ex[:], col[:, COUNT:COUNT + 1], start=True, stop=True).then_inc(pe_few, 1)
                    pe.wait_ge(plan, PLAN_CHUNKS)
                    nc.tensor.matmul(few[0:GR, 32:32 + NT], chunks_bc[:, 0:GR], tri_in[:], start=True, stop=True)
                    nc.tensor.matmul(few[0:GR, 64:64 + NT], chunks_bc[:, 0:GR], tri_ex[:], start=True, stop=True)
                    nc.tensor.matmul(few[0:GR, 96:96 + NT], first_bc[:, 0:GR], ident[0:NT, 0:NT], start=True, stop=True).then_inc(pe_few, 1)
                    n = 0
                    for what, rows in (("src", src_f), ("dl", dl_row), ("key", key_row), ("last", last_row)):
                        pe.wait_ge(row_ready, 2 + n)
                        for b in range(NB):
                            t = nc.tensor.transpose(turned[n % 4][:, b * GR:(b + 1) * GR], rows[:, b, :], ident[0:GR, 0:GR])
                        t.then_inc(turned_ready, 1)
                        n += 1
                    for c in range(4):
                        pe.wait_ge(turned_used, n - 3)
                        for b in range(NB):
                            t = nc.tensor.transpose(turned[n % 4][:, b * GR:(b + 1) * GR], attrrow[:, b, :, c], ident[0:GR, 0:GR])
                        t.then_inc(turned_ready, 1)
                        n += 1

                @block.sync
                def _(sp):
                    sp.wait_ge(row_ready, 1)
                    for r in range(2):
                        sp.dma_start(step_dram[r * S:(r + 1) * S].rearrange("(b p) -> p b", b=NB), table_i[:, r, :]).then_inc(table_out, 16)
                    sp.wait_ge(table_out, 32)
                    sp.dma_start(step_table[:], step_dram.rearrange("(o s) -> o s", o=1)).then_inc(table_in, 16)
                    sp.wait_ge(row_ready, 4)
                    sp.dma_start(seg_dram[1:S * P + 1].rearrange("(b p e) -> p b e", b=NB, p=GR), seg_row[:]).then_inc(seg_out, 16)
                    sp.dma_start(seg_dram[0:1].rearrange("(o s) -> o s", o=1), ends[:, 0:1]).then_inc(seg_out, 16)
                    sp.dma_start(seg_dram[S * P + 1:S * P + 2].rearrange("(o s) -> o s", o=1), ends[:, 1:2]).then_inc(seg_out, 16)
                    sp.wait_ge(seg_out, 48)
                    sp.dma_start(before[:], seg_dram[0:S * P].rearrange("(b p e) -> p b e", b=NB, p=GR)).then_inc(seg_in, 16)
                    sp.dma_start(after[:], seg_dram[2:S * P + 2].rearrange("(b p e) -> p b e", b=NB, p=GR)).then_inc(seg_in, 16)
                    sp.dma_start(key_dram.rearrange("(b p e) -> p b e", b=NB, p=GR), key_row[:]).then_inc(pen_out, 16)
                    sp.wait_ge(row_ready, 5)
                    sp.dma_start(pen_dram.rearrange("(b p e) -> p b e", b=NB, p=GR), v1[:]).then_inc(pen_out, 16)
                    for n, rows in enumerate((dl_row, msg_row)):
                        sp.dma_start(pair_dram.rearrange("(b p) n e -> n p b e", b=NB)[n], rows[:]).then_inc(pen_out, 16)
                    sp.wait_ge(pen_out, 64)
                    sp.wait_ge(table_in, 16)

                @block.vector
                def _(dve):
                    o = Order(dve, plan)
                    TT, TS = nc.vector.tensor_tensor, nc.vector.tensor_scalar
                    o.did(TS(tri_ex[:], iota_row[0:NT, 0:NT], pidx[0:NT, 0:1], None, ALU.is_gt))
                    o.did(TS(tri_in[:], iota_row[0:NT, 0:NT], pidx[0:NT, 0:1], None, ALU.is_ge))
                    dve.wait_ge(pe_few, 1)
                    o.link(nc.vector.tensor_copy(col[:, COUNT:COUNT + 1], few[0:NT, 0:1]))
                    dve.wait_ge(pe_few, 2)
                    o.did(nc.vector.tensor_copy(col_i[:, 0:1], few[0:NT, 1:2]))
                    o.link(nc.vector.tensor_copy(col[:, START:START + 1], few[0:NT, 1:2]))
                    o.did(TS(col[:, SOME:SOME + 1], col[:, COUNT:COUNT + 1], 0.5, None, ALU.is_ge))
                    o.link(TT(col[:, END:END + 1], col[:, START:START + 1], col[:, COUNT:COUNT + 1], ALU.add))
                    o.link(TS(col[:, END:END + 1], col[:, END:END + 1], -1.0, 0.0, ALU.add, ALU.max))
                    o.link(nc.vector.tensor_copy(col_i[:, 1:2], col[:, END:END + 1]))
                    o.link(TS(col_i[:, 2:4], col_i[:, 0:2], 7, None, ALU.logical_shift_right))
                    o.link(nc.vector.tensor_copy(col[:, 6:8], col_i[:, 2:4]))
                    o.did(TS(first_bc[:], ones[0:NT, :], col[:, 6:7], None, ALU.mult))
                    o.link(TT(col[:, CHUNKS:CHUNKS + 1], col[:, 7:8], col[:, 6:7], ALU.subtract))
                    o.link(TS(col[:, CHUNKS:CHUNKS + 1], col[:, CHUNKS:CHUNKS + 1], 1.0, col[:, SOME:SOME + 1], ALU.add, ALU.mult))
                    o.link(TS(chunks_bc[:], ones[0:NT, :], col[:, CHUNKS:CHUNKS + 1], None, ALU.mult))
                    assert o.n == PLAN_CHUNKS
                    dve.wait_ge(steps_made, 1)
                    o.did(nc.vector.tensor_copy(step_f[:], step_i[:]))
                    dve.wait_ge(pe_few, 3)
                    o.did(nc.vector.tensor_copy(incl_row[:], few[0:GR, 32:32 + NT]))
                    o.link(nc.vector.tensor_copy(base_row[:], few[0:GR, 96:96 + NT]))
                    o.link(TT(base_row[:], base_row[:], few[0:GR, 64:64 + NT], ALU.subtract))
                    spread = [GR, NB, NT]
                    o.link(TT(sel[:], step_f[:].unsqueeze(2).broadcast_to(spread), incl_row[:].unsqueeze(1).broadcast_to(spread), ALU.is_ge))
                    o.link(nc.vector.tensor_reduce(tile_f[:], sel[:], AX.X, ALU.add))
                    o.link(TT(sel[:], iota_row[0:GR, 0:NT].unsqueeze(1).broadcast_to(spread), tile_f[:].unsqueeze(2).broadcast_to(spread), ALU.is_equal))
                    o.link(TT(sel[:], sel[:], base_row[:].unsqueeze(1).broadcast_to(spread), ALU.mult))
                    o.link(nc.vector.tensor_reduce(chunk_f[:], sel[:], AX.X, ALU.add))
                    o.link(TT(chunk_f[:], chunk_f[:], step_f[:], ALU.add))
                    o.link(TS(chunk_f[:], chunk_f[:], float(CH - 1), None, ALU.min))
                    o.did(TS(tile_c[:], tile_f[:], float(NT - 1), None, ALU.min))
                    o.did(TS(tile_off[:], tile_f[:], float(P), None, ALU.mult))
                    o.link(nc.vector.tensor_copy(chunk_i[:], chunk_f[:]))
                    o.did(nc.vector.tensor_copy(table_i[:, 0, :], tile_c[:]))
                    o.link(TS(table_i[:, 1, :], chunk_f[:], float(P), None, ALU.mult))
                    dve.nop().then_inc(row_ready, 1)
                    dve.wait_ge(rows_in, 16 * 3 * NB)
                    flat = [GR, NB, P]
                    o.did(nc.vector.tensor_copy(src_f[:], srcrow[:]))
                    o.link(nc.vector.tensor_copy(seg_row[:], dstrow[:]))
                    o.link(TT(dl_row[:], seg_row[:], tile_off[:].unsqueeze(2).broadcast_to(flat), ALU.subtract))
                    dve.nop().then_inc(row_ready, 1)
                    dve.nop().then_inc(row_ready, 1)
                    o.did(TS(tile_off[:], tile_f[:], 4096.0, None, ALU.mult))
                    o.did(TS(v1[:], dl_row[:], 0.0, None, ALU.is_ge))
                    o.link(TS(v2[:], dl_row[:], float(P), None, ALU.is_lt))
                    o.did(TT(v1[:], v1[:], v2[:], ALU.mult))
                    o.did(nc.vector.memset(ends[:], -1.0))
                    o.link(nc.vector.scalar_tensor_tensor(key_row[:], src_f[:], float(NP), seg_row[:], ALU.mult, ALU.add))
                    own = iota_row[0:GR].unsqueeze(1).broadcast_to(flat)
                    o.link(TT(seg_row[:], seg_row[:], tile_off[:].unsqueeze(2).broadcast_to(flat), ALU.add))
                    o.link(TT(key_row[:], key_row[:], own, ALU.subtract))
                    o.link(nc.vector.scalar_tensor_tensor(key_row[:], key_row[:], -float(KD), v1[:], ALU.add, ALU.mult))
                    o.link(TT(key_row[:], key_row[:], own, ALU.add))
                    o.did(TS(key_row[:], key_row[:], float(KD), None, ALU.add))
                    o.link(TT(msg_row[:], src_f[:], own, ALU.subtract))
                    o.link(nc.vector.scalar_tensor_tensor(msg_row[:], msg_row[:], -float(NP), v1[:], ALU.add, ALU.mult))
                    o.link(nc.vector.scalar_tensor_tensor(msg_row[:], msg_row[:], float(NP), own, ALU.add, ALU.add))
                    dve.nop().then_inc(row_ready, 1)
                    dve.wait_ge(seg_in, 32)
                    o.did(TT(last_row[:], seg_row[:], after[:], ALU.not_equal))
                    o.link(TT(v1[:], seg_row[:], before[:], ALU.not_equal))
                    o.link(TS(v1[:], v1[:], -BIG, None, ALU.mult))
                    dve.nop().then_inc(row_ready, 1)
                    targets = (src_step[:], dl_step[:], key_step[:], last_step[:]) + tuple(attr4_step[:, :, c] for c in range(4))
                    for n, target in enumerate(targets):
                        dve.wait_ge(turned_ready, n + 1)
                        nc.vector.tensor_copy(target, turned[n % 4][:, 0:S]).then_inc(turned_used, 1)

        def norm_scales(name, source, t0=None):
            order, var_ready, root_ready = sem(name + "_order"), sem(name + "_var_ready"), sem(name + "_root_ready")
            mean, diff, var, root, half = (norm_small[:, i, :] for i in range(5))
            with nc.Block() as block:
                @block.vector
                def _(dve):
                    o = Order(dve, order)
                    o.begin(1)
                    with dve.Fori(0, NT) as t:
                        o.enter(t)
                        o.did(nc.vector.bn_stats(stats[:, bass.ds(t, 1), :].rearrange("p o s -> p (o s)"),
                                                 source[:, bass.ds(t, 1), :].rearrange("p o d -> p (o d)")))
                    o.leave(NT)
                    o.need(o.n)
                    o.did(nc.vector.tensor_tensor(mean, stats[:, :, 1], stats[:, :, 4], ALU.add))
                    o.did(nc.vector.tensor_tensor(diff, stats[:, :, 1], stats[:, :, 4], ALU.subtract))
                    o.link(nc.vector.tensor_tensor(var, stats[:, :, 2], stats[:, :, 5], ALU.add))
                    o.did(nc.vector.tensor_scalar(mean, mean, 0.5, None, ALU.mult))
                    o.did(nc.vector.tensor_scalar(var, var, 1.0 / D, EPS, ALU.mult, ALU.add))
                    o.link(nc.vector.tensor_tensor(half, diff, diff, ALU.mult))
                    o.link(nc.vector.scalar_tensor_tensor(var, half, 0.25, var, ALU.mult, ALU.add))
                    dve.nop().then_inc(var_ready, 1)
                    dve.wait_ge(root_ready, 1)
                    o.link(nc.vector.reciprocal(rstd[:], root))
                    o.link(nc.vector.scalar_tensor_tensor(shift[:], mean, -1.0, rstd[:], ALU.mult, ALU.mult))

                @block.scalar
                def _(act):
                    act.wait_ge(var_ready, 1)
                    nc.scalar.activation(root, var, ACT.Sqrt).then_inc(root_ready, 1)

        def norm_apply(name, source, target, func):
            with nc.Block() as block:
                @block.scalar
                def _(act):
                    with act.Fori(0, NT) as t:
                        nc.scalar.activation(target[:, bass.ds(t, 1), :].rearrange("p o d -> p (o d)"),
                                             source[:, bass.ds(t, 1), :].rearrange("p o d -> p (o d)"), func,
                                             bias=column(shift, t), scale=column(rstd, t))

        norm_scales("n0", x_sb)
        with ExitStack() as ctx:
            h0 = sb("h0", [P, NT, D], F32, ctx)
            wall = sb("wall", [P, 2, HD + 2 * HW], F32, ctx)
            arep = sb("arep", [P, 2, HD], F32, ctx)
            aprod = sb("aprod", [P, HD], F32, ctx)
            score_w = sb("score_w", [P, 2, 2, 12], F32, ctx)
            gb = sb("gb", [P, 2, 2], F32, ctx)
            bw = sb("bw", [1, HD + 2 * HW], F32, ctx)
            zs = sb("zs", [P, 5, D], F32, ctx)
            zT = sb("zT", [P, 5, 2, P], F32, ctx)
            orow = sb("orow", [P, 5, ROW], F32, ctx)
            srow = sb("srow", [P, 5, SROW], F32, ctx)
            dsmall = sb("dsmall", [P, 2, NT], F32, ctx)
            p_zT = [ps(f"p_zT{i}", [P, 2, P], F32, ctx) for i in range(2)]
            p_h = [ps(f"p_h{i}", [P, HD], F32, ctx) for i in range(2)]
            p_s = [ps(f"p_s{i}", [P, 2 * HW], F32, ctx) for i in range(2)]
            p_b = ps("p_b", [1, 1024], F32, ctx)
            norm_apply("n0", x_sb, h0, ACT.Relu)
            norm_scales("n1", h0)
            w_in, w_order, w_ready, bias_mm, bias_sb = sem("w_in"), sem("w_order"), sem("w_ready"), sem("bias_mm"), sem("bias_sb")
            dvar, droot = sem("dvar"), sem("droot")
            with nc.Block() as block:
                @block.sync
                def _(sp):
                    for k in range(2):
                        sp.dma_start(wall[:, k, 0:256], a["W1"][k * P:(k + 1) * P, :]).then_inc(w_in, 16)
                        sp.dma_start(wall[:, k, 256:512], a["W2"][k * P:(k + 1) * P, :]).then_inc(w_in, 16)
                    for n, (one, two) in enumerate((("a_src1", "a_src2"), ("a_dst1", "a_dst2"))):
                        for c, name in enumerate((one, two)):
                            row = a[name].rearrange("h c -> (h c)")
                            sp.dma_start(arep[:, n, c * 256:(c + 1) * 256], row.partition_broadcast(P)).then_inc(w_in, 16)
                    sp.dma_start(gb[:, :, 0], a["gamma"].rearrange("(k p) -> p k", k=2)).then_inc(w_in, 16)
                    sp.dma_start(gb[:, :, 1], a["beta"].rearrange("(k p) -> p k", k=2)).then_inc(w_in, 16)

                @block.vector
                def _(dve):
                    o = Order(dve, w_order)
                    dve.wait_ge(w_in, 160)
                    for k in range(2):
                        for n in range(2):
                            o.link(nc.vector.tensor_tensor(aprod[:], wall[:, k, 0:HD], arep[:, n, :], ALU.mult))
                            o.did(nc.vector.tensor_reduce(score_w[:, k, n, 0:4], aprod[:, 0:256].rearrange("p (h c) -> p h c", h=4), AX.X, ALU.add))
                            o.link(nc.vector.tensor_reduce(score_w[:, k, n, 4:12], aprod[:, 256:512].rearrange("p (h c) -> p h c", h=8), AX.X, ALU.add))
                            at = HD + n * HW
                            o.did(nc.vector.tensor_copy(wall[:, k, at:at + 8].rearrange("p (h o) -> p h o", o=2),
                                                        score_w[:, k, n, 0:4].unsqueeze(2).broadcast_to([P, 4, 2])))
                            o.link(nc.vector.tensor_copy(wall[:, k, at + 8:at + 16], score_w[:, k, n, 4:12]))
                    dve.nop().then_inc(w_ready, 1)
                    dve.wait_ge(bias_mm, 1)
                    nc.vector.tensor_copy(bw[:, 0:HD], p_b[:, 0:HD]).then_inc(bias_sb, 1)
                    nc.vector.tensor_copy(bw[:, HD:], p_b[:, 512:512 + 2 * HW]).then_inc(bias_sb, 1)
                    for k in range(2):
                        o.did(nc.vector.tensor_scalar(wall[:, k, :], wall[:, k, :], gb[:, k, 0:1], None, ALU.mult))
                    o.did(nc.vector.tensor_scalar(dsmall[:, 0, :], deg[:], 0.5, None, ALU.is_ge))
                    o.link(nc.vector.tensor_scalar(dsmall[:, 1, :], deg[:], 1.0, None, ALU.max))
                    dve.nop().then_inc(dvar, 1)
                    dve.wait_ge(droot, 1)
                    o.link(nc.vector.reciprocal(dinv[:], dinv[:]))
                    o.link(nc.vector.tensor_tensor(dinv[:], dinv[:], dsmall[:, 0, :], ALU.mult))

                @block.scalar
                def _(act):
                    act.wait_ge(dvar, 1)
                    nc.scalar.activation(dinv[:], dsmall[:, 1, :], ACT.Sqrt).then_inc(droot, 1)

                @block.tensor
                def _(pe):
                    pe.wait_ge(w_ready, 1)
                    for k in range(2):
                        nc.tensor.matmul(p_b[:, 0:HD], gb[:, k, 1:2], wall[:, k, 0:HD], start=(k == 0), stop=(k == 1))
                    for k in range(2):
                        m = nc.tensor.matmul(p_b[:, 512:512 + 2 * HW], gb[:, k, 1:2], wall[:, k, HD:], start=(k == 0), stop=(k == 1))
                    m.then_inc(bias_mm, 1)

            z_ready, zT_ps, zT_sb, tabs_ps, feat_out, score_out = (
                sem("z_ready"), sem("zT_ps"), sem("zT_sb"), sem("tabs_ps"), sem("feat_out"), sem("score_out"))
            row_out = [sem(f"row_out{u}") for u in range(5)]
            x_sum = sem("x_sum")
            R = NT // 5
            with nc.Block() as block:
                @block.scalar
                def _(act):
                    def round_of(i):
                        for u in range(5):
                            t = i * 5 + u
                            act.wait_ge(zT_ps, i * 5 + u + 1)
                            nc.scalar.activation(zs[:, u, :], h0[:, bass.ds(t, 1), :].rearrange("p o d -> p (o d)"), ACT.Identity,
                                                 bias=column(shift, t), scale=column(rstd, t)).then_inc(z_ready, 1)
                        for u in range(5):
                            act.wait_ge(tabs_ps, i * 5 + u + 1)
                            act.wait_ge(row_out[u], i * 32)
                            nc.scalar.copy(orow[:, u, 0:HD], p_h[u % 2][:]).then_inc(feat_out, 1)

                    looped(act, R, round_of)

                @block.tensor
                def _(pe):
                    pe.nop().then_inc(zT_ps, 5)
                    def round_of(i):
                        for u in range(5):
                            pe.wait_ge(z_ready, i * 5 + u + 1)
                            pe.wait_ge(zT_sb, i * 5 + u)
                            for k in range(2):
                                m = nc.tensor.transpose(p_zT[0][:, k, :], zs[:, u, k * P:(k + 1) * P], ident[:])
                            m.then_inc(zT_ps, 1)
                            pe.wait_ge(zT_sb, i * 5 + u + 1)
                            if u >= 2 or not is_first(i):
                                pe.wait_ge(feat_out, i * 5 + u - 1)
                                pe.wait_ge(score_out, i * 5 + u - 1)
                            for w, target in ((slice(0, HD), p_h[u % 2]), (slice(HD, HD + 2 * HW), p_s[u % 2])):
                                for k in range(2):
                                    nc.tensor.matmul(target[:], zT[:, u, k, :], wall[:, k, w], start=(k == 0), stop=False)
                                m = nc.tensor.matmul(target[:], ones[0:1, :], bw[:, w], start=False, stop=True)
                            m.then_inc(tabs_ps, 1)

                    looped(pe, R, round_of)

                @block.vector
                def _(dve):
                    def round_of(i):
                        for u in range(5):
                            t = i * 5 + u
                            dve.wait_ge(zT_ps, 5 + i * 5 + u + 1)
                            nc.vector.tensor_copy(zT[:, u], p_zT[0][:]).then_inc(zT_sb, 1)
                            dve.wait_ge(tabs_ps, i * 5 + u + 1)
                            dve.wait_ge(row_out[u], i * 32)
                            nc.vector.tensor_copy(orow[:, u, HD:], p_s[u % 2][:, 0:HW])
                            nc.vector.tensor_copy(srow[:, u, 0:HW], p_s[u % 2][:, 0:HW])
                            nc.vector.tensor_copy(srow[:, u, HW:SROW], column(dinv, t).broadcast_to([P, SROW - HW]))
                            nc.vector.tensor_copy(tab[:, bass.ds(t, 1), 0:HW].rearrange("p o h -> p (o h)"),
                                                  p_s[u % 2][:, HW:]).then_inc(score_out, 1)

                    looped(dve, R, round_of)
                    nc.vector.tensor_tensor(x_sb[:], x_sb[:], h0[:], ALU.add).then_inc(x_sum, 1)

                @block.sync
                def _(sp):
                    with sp.Fori(0, R) as i:
                        for u in range(5):
                            t = i * 5 + u
                            sp.wait_ge(feat_out, i * 5 + u + 1)
                            sp.wait_ge(score_out, i * 5 + u + 1)
                            sp.dma_start(att_dram[bass.ds(t * P, P), :], orow[:, u, :]).then_inc(row_out[u], 16)
                            sp.dma_start(score_dram[bass.ds(t * P, P), :], srow[:, u, :]).then_inc(row_out[u], 16)
                    for u in range(5):
                        sp.wait_ge(row_out[u], 32 * R)
        end_stage()

        G4 = S // 4
        place_all = sb("place_all", [P, S], I32, early)
        number_all = sb("number_all", [P, S], F32, early)

        def rounds(engine, work):
            work(0, 0, 0)
            work(1, 1, 0)
            with engine.Fori(1, G4 // 2 - 1) as i:
                work(i * 2, 0, i)
                work(i * 2 + 1, 1, i)
            work(G4 - 2, 0, G4 // 2 - 1)
            work(G4 - 1, 1, G4 // 2 - 1)

        def is_last(j, n=1):
            return isinstance(j, int) and j >= G4 - n

        with ExitStack() as ctx:
            top_acc = sb("top_acc", [P, NT, SROW], F32, ctx)
            idx = [sb(f"idx{q}", [P, 4], I32, ctx) for q in range(2)]
            score_g = [sb(f"score_g{q}", [P, 4, SROW], F32, ctx) for q in range(2)]
            pen = [sb(f"pen{q}", [HW, 4 * P], F32, ctx) for q in range(2)]
            run = [sb(f"run{q}", [HW, 4 * P], F32, ctx) for q in range(2)]
            hot = [sb(f"hot{q}", [P, 4, P], F32, ctx) for q in range(2)]
            rhs = [sb(f"rhs{q}", [P, 4, SROW], F32, ctx) for q in range(2)]
            key_rep = [sb(f"key_rep{q}", [P, 4, P], F32, ctx) for q in range(2)]
            same = sb("same", [P, 4, P], F32, ctx)
            earlier = sb("earlier", [P, 4, P], F32, ctx)
            prior = sb("prior", [P, 4], F32, ctx)
            place_f = sb("place_f", [P, 4], F32, ctx)
            no_edge = sb("no_edge", [P, NT], F32, ctx)
            number = [sb(f"number{q}", [P, 2], F32, ctx) for q in range(2)]
            place = [sb(f"place{q}", [P, 2], I32, ctx) for q in range(2)]
            own_place = sb("own_place", [P, 1], F32, ctx)
            p_in = [ps(f"p_in{q}", [HW, 4 * P], F32, ctx) for q in range(2)]
            p_run = [ps(f"p_run{q}", [P, 4, HW], F32, ctx) for q in range(2)]
            p_top = [ps(f"p_top{q}", [P, 4, SROW], F32, ctx) for q in range(2)]
            scores_in = [sem(f"a_scores_in{q}") for q in range(2)]
            rep_in = [sem(f"a_rep_in{q}") for q in range(2)]
            (idx_ready, turned_in, run_ready, run_turned, rhs_ready, tops, added, place_ready, slots_ready, placed, a_order, keys_used,
             places_free, self_in, loops) = (sem("a_" + x) for x in (
                 "idx_ready", "turned_in", "run_ready", "run_turned", "rhs_ready", "tops", "added", "place_ready", "slots_ready", "placed",
                 "order", "keys_used", "places_free", "self_in", "loops"))
            with nc.Block() as block:
                @block.sync
                def _(sp):
                    sp.dma_start(self_s[:], score_dram.rearrange("(t p) s -> p t s", p=P)[:, :, 0:HW]).then_inc(self_in, 16)
                    with sp.Fori(0, G4 // 2) as i:
                        for q in range(2):
                            g = i * 2 + q
                            sp.wait_ge(keys_used, g + 1)
                            sp.dma_start(pen[q][:], pen_dram[bass.ds(g * 4 * P, 4 * P)].partition_broadcast(HW)).then_inc(rep_in[q], 16)
                            sp.dma_start(key_rep[q][:].rearrange("p u e -> p (u e)"),
                                         key_dram[bass.ds(g * 4 * P, 4 * P)].partition_broadcast(P)).then_inc(rep_in[q], 16)

                @block.scalar
                def _(act):
                    def indices(g, q):
                        nc.scalar.copy(idx[q][:], src_step[:, bass.ds(g * 4, 4)]).then_inc(idx_ready, 1)

                    def work(j, q, i):
                        act.wait_ge(place_ready, j + 1)
                        act.wait_ge(places_free, j)
                        nc.scalar.copy(number[q][:], number_all[:, bass.ds(j * 4, 2)])
                        nc.scalar.copy(place[q][:], place_all[:, bass.ds(j * 4, 2)]).then_inc(slots_ready, 1)
                        if not is_last(j, 2):
                            act.wait_ge(rhs_ready, j + 1)
                            indices(j + 2, q)

                    indices(0, 0)
                    indices(1, 1)
                    rounds(act, work)
                    act.wait_ge(loops, 1)
                    nc.scalar.activation(self_s[:], self_s[:], ACT.Exp)

                @block.gpsimd
                def _(pool):
                    def gather(q, u):
                        nc.gpsimd.indirect_dma_start(
                            score_g[q][:, u, :], None, score_dram,
                            bass.IndirectOffsetOnAxis(ap=idx[q][:, u:u + 1].bitcast(U32), axis=0)).then_inc(scores_in[q], 16)

                    def work(j, q, i):
                        ahead = not is_last(j, 2)
                        if ahead:
                            pool.wait_ge(rhs_ready, j + 1)
                            pool.wait_ge(idx_ready, j + 3)
                            pool.nop().then_inc(waits_passed, 1)
                        for n in range(2):
                            if ahead:
                                gather(q, 2 * n)
                                gather(q, 2 * n + 1)
                            if n == 0:
                                pool.wait_ge(slots_ready, j + 1)
                            pool.wait_ge(placed, (j * 2 + n) * 16)
                            pool.nop().then_inc(places_free if n == 0 else waits_passed, 1)
                            nc.gpsimd.indirect_dma_start(
                                count_dram, bass.IndirectOffsetOnAxis(ap=place[q][:, n:n + 1].bitcast(U32), axis=0),
                                number[q][:, n:n + 1], None, compute_op=ALU.add).then_inc(placed, 16)

                    for q in range(2):
                        pool.wait_ge(idx_ready, q + 1)
                        for u in range(4):
                            gather(q, u)
                    pool.wait_ge(zeros_out, 16 * (NZ + 1))
                    rounds(pool, work)
                    pool.wait_ge(placed, G4 * 32)

                @block.tensor
                def _(pe):
                    def turn_scores(g, q, i):
                        pe.wait_ge(scores_in[q], i * 64 + 64)
                        for u in range(4):
                            m = nc.tensor.transpose(p_in[q][:, u * P:(u + 1) * P], score_g[q][:, u, 0:HW], ident[:])
                        m.then_inc(turned_in, 1)

                    def work(j, q, i):
                        if not is_last(j):
                            turn_scores(j + 1, 1 - q, i + q)
                        pe.wait_ge(run_ready, j + 1)
                        for u in range(4):
                            m = nc.tensor.matmul(p_run[q][:, u, :], run[q][:, u * P:(u + 1) * P], ident[0:HW, 0:HW], start=True, stop=True)
                        m.then_inc(run_turned, 1)
                        pe.wait_ge(rhs_ready, j + 1)
                        for u in range(4):
                            m = nc.tensor.matmul(p_top[q][:, u, :], hot[q][:, u, :], rhs[q][:, u, :], start=True, stop=True)
                        m.then_inc(tops, 1)

                    turn_scores(0, 0, 0)
                    rounds(pe, work)

                @block.vector
                def _(dve):
                    o = Order(dve, a_order)
                    TT, TS = nc.vector.tensor_tensor, nc.vector.tensor_scalar
                    dve.nop().then_inc(keys_used, 2)
                    o.did(nc.vector.memset(top_acc[:], 0.0))
                    o.did(nc.vector.memset(run[1][:], 0.0))
                    o.link(TS(own_place[:], pidx[:], float(KD), None, ALU.add))
                    spread = [P, 4, P]

                    def add_tops(g, q, tiles):
                        dve.wait_ge(tops, g + 1)
                        for u in range(4):
                            acc = top_acc[:, bass.ds(tiles[u], 1), :].rearrange("p o s -> p (o s)")
                            dve.wait_ge(added, g * 4 + u)
                            TT(acc, acc, p_top[q][:, u, :], ALU.add).then_inc(added, 1)

                    def work(j, q, i, tiles):
                        o.enter(j)
                        grp = bass.ds(j * 4, 4)
                        dve.wait_ge(rep_in[q], i * 32 + 32)
                        dve.wait_ge(turned_in, j + 1)
                        dve.wait_ge(run_ready, j)
                        nc.vector.tensor_tensor_scan(run[q][:], pen[q][:], p_in[q][:], run[1 - q][:, 4 * P - 1:4 * P],
                                                     ALU.add, ALU.max).then_inc(run_ready, 1)
                        here = key_step[:, grp]
                        o.link(TT(same[:], key_rep[q][:], here.unsqueeze(2).broadcast_to(spread), ALU.is_equal))
                        o.did(TT(earlier[:], same[:], lower[:].unsqueeze(1).broadcast_to(spread), ALU.mult))
                        nc.vector.tensor_reduce(number_all[:, grp], same[:], AX.X, ALU.add)
                        o.need(o.n)
                        o.link(nc.vector.tensor_reduce(prior[:], earlier[:], AX.X, ALU.add))
                        dve.wait_ge(run_ready, j + 1)
                        dve.nop().then_inc(keys_used, 1)
                        o.did(TS(prior[:], prior[:], 0.5, None, ALU.is_lt))
                        o.link(TT(place_f[:], here, own_place[:].broadcast_to([P, 4]), ALU.subtract))
                        o.link(TT(place_f[:], place_f[:], prior[:], ALU.mult))
                        TT(place_all[:, grp], place_f[:], own_place[:].broadcast_to([P, 4]), ALU.add).then_inc(place_ready, 1)
                        TT(hot[q][:], iota_row[:].unsqueeze(1).broadcast_to(spread),
                           dl_step[:, grp].unsqueeze(2).broadcast_to(spread), ALU.is_equal)
                        TT(rhs[q][:, :, HW:SROW], attr4_step[:, grp, :], score_g[q][:, :, HW:HW + 1].broadcast_to([P, 4, 4]), ALU.mult)
                        dve.wait_ge(run_turned, j + 1)
                        TT(rhs[q][:, :, 0:HW], p_run[q][:], last_step[:, grp].unsqueeze(2).broadcast_to([P, 4, HW]),
                           ALU.mult).then_inc(rhs_ready, 1)
                        if not is_first(j):
                            add_tops(j - 1, 1 - q, tiles)

                    o.begin(6)
                    tiles = read_registers(nc, step_table, 0, 4, ET.DVE, NT - 1)
                    work(0, 0, 0, None)
                    work(1, 1, 0, tiles)
                    with dve.Fori(1, G4 // 2) as i:
                        tiles = read_registers(nc, step_table, i * 8 - 4, 8, ET.DVE, NT - 1)
                        work(i * 2, 0, i, tiles[0:4])
                        work(i * 2 + 1, 1, i, tiles[4:8])
                    o.leave(G4)
                    add_tops(G4 - 1, 1, read_registers(nc, step_table, S - 4, 4, ET.DVE, NT - 1))
                    dve.wait_ge(added, S)
                    lo, hi = tab[:, :, 0:HW], tab[:, :, HW:]
                    every = [P, NT, HW]
                    dve.wait_ge(self_in, 16)
                    o.link(TS(no_edge[:], deg[:], 0.5, -BIG, ALU.is_lt, ALU.mult))
                    o.link(TT(hi, top_acc[:, :, 0:HW], no_edge[:].unsqueeze(2).broadcast_to(every), ALU.add))
                    o.link(TT(hi, hi, self_s[:], ALU.max))
                    o.did(TT(hi, hi, lo, ALU.add))
                    o.link(TT(self_s[:], self_s[:], lo, ALU.add))
                    o.did(nc.vector.scalar_tensor_tensor(self_s[:], self_s[:], 0.2, self_s[:], ALU.mult, ALU.max))
                    o.link(nc.vector.scalar_tensor_tensor(hi, hi, 0.2, hi, ALU.mult, ALU.max))
                    TT(self_s[:], self_s[:], hi, ALU.subtract).then_inc(loops, 1)
                    nc.vector.tensor_copy(F_sb[:], top_acc[:, :, HW:])
        end_stage()

        with ExitStack() as ctx:
            acc = sb("acc", [P, NT, ROW], F32, ctx)
            with ExitStack() as inner:
                idx = [sb(f"b_idx{q}", [P, 4], I32, inner) for q in range(2)]
                number = [sb(f"b_number{q}", [P, 2], F32, inner) for q in range(2)]
                place = [sb(f"b_place{q}", [P, 2], I32, inner) for q in range(2)]
                row_g = [sb(f"row_g{q}", [P, 4, ROW], F32, inner) for q in range(2)]
                hot = [sb(f"b_hot{q}", [P, 4, P], F32, inner) for q in range(2)]
                dl_rep = [sb(f"dl_rep{q}", [P, 4, P], F32, inner) for q in range(2)]
                hotT = [sb(f"b_hotT{q}", [P, 4, P], F32, inner) for q in range(2)]
                zz = sb("zz", [P, 4, HW], F32, inner)
                weight = [sb(f"weight{q}", [P, 4, HW], F32, inner) for q in range(2)]
                msg = [sb(f"msg{q}", [P, 4, HD], F32, inner) for q in range(2)]
                p_tab = ps("b_p_tab", [P, 4, 2 * HW], F32, inner)
                p_out = [ps(f"b_p_out{v}", [P, HD], F32, inner) for v in range(4)]
                p_den = [ps(f"b_p_den{q}", [P, 4, HW], F32, inner) for q in range(2)]
                rows_in = [sem(f"b_rows_in{q}") for q in range(2)]
                rep_in = [sem(f"b_rep_in{q}") for q in range(2)]
                (idx_ready, hotT_ready, hot_ready, tab_ready, arg_ready, weight_ready, msg_ready, sums_ready, added, b_order, own_in,
                 slots_ready, placed, places_free) = (sem("b_" + x) for x in (
                     "idx_ready", "hotT_ready", "hot_ready", "tab_ready", "arg_ready", "weight_ready", "msg_ready", "sums_ready", "added",
                     "order", "own_in", "slots_ready", "placed", "places_free"))
                with nc.Block() as block:
                    @block.sync
                    def _(sp):
                        sp.dma_start(acc[:], att_dram.rearrange("(t p) s -> p t s", p=P)).then_inc(own_in, 16)
                        with sp.Fori(0, G4 // 2) as i:
                            for q in range(2):
                                sp.wait_ge(hotT_ready, i * 2 + q + 1)
                                sp.nop().then_inc(waits_passed, 1)
                                sp.dma_start(dl_rep[q][:], pair_dram[bass.ds((i * 2 + q) * 4, 4), 0, :].partition_broadcast(P)).then_inc(rep_in[q], 16)

                    @block.scalar
                    def _(act):
                        def indices(g, q):
                            nc.scalar.copy(idx[q][:], src_step[:, bass.ds(g * 4, 4)]).then_inc(idx_ready, 1)

                        def slots(g, q):
                            nc.scalar.copy(number[q][:], number_all[:, bass.ds(g * 4 + 2, 2)])
                            nc.scalar.copy(place[q][:], place_all[:, bass.ds(g * 4 + 2, 2)]).then_inc(slots_ready, 1)

                        def work(j, q, i):
                            act.wait_ge(arg_ready, j + 1)
                            nc.scalar.activation(weight[q][:], zz[:], ACT.Exp).then_inc(weight_ready, 1)
                            if not is_last(j, 2):
                                indices(j + 2, q)
                            if not is_last(j):
                                act.wait_ge(places_free, j + 1)
                                slots(j + 1, 1 - q)

                        indices(0, 0)
                        indices(1, 1)
                        slots(0, 0)
                        rounds(act, work)

                    @block.gpsimd
                    def _(pool):
                        def gather(q, u):
                            nc.gpsimd.indirect_dma_start(
                                row_g[q][:, u, :], None, att_dram,
                                bass.IndirectOffsetOnAxis(ap=idx[q][:, u:u + 1].bitcast(U32), axis=0)).then_inc(rows_in[q], 16)

                        def work(j, q, i):
                            ahead = not is_last(j, 2)
                            if ahead:
                                pool.wait_ge(idx_ready, j + 3)
                            for n in range(2):
                                if ahead:
                                    for u in (2 * n, 2 * n + 1):
                                        pool.wait_ge(msg_ready, j * 4 + u + 1)
                                        pool.nop().then_inc(waits_passed, 1)
                                        gather(q, u)
                                if n == 0:
                                    pool.wait_ge(slots_ready, j + 1)
                                pool.wait_ge(placed, (j * 2 + n) * 16)
                                pool.nop().then_inc(places_free if n == 0 else waits_passed, 1)
                                nc.gpsimd.indirect_dma_start(
                                    count_dram, bass.IndirectOffsetOnAxis(ap=place[q][:, n:n + 1].bitcast(U32), axis=0),
                                    number[q][:, n:n + 1], None, compute_op=ALU.add).then_inc(placed, 16)

                        for q in range(2):
                            pool.wait_ge(idx_ready, q + 1)
                            for u in range(4):
                                gather(q, u)
                        rounds(pool, work)
                        pool.wait_ge(placed, G4 * 32)

                    @block.tensor
                    def _(pe):
                        def look_up(g, q, tiles):
                            pe.wait_ge(hotT_ready, g + 3)
                            for u in range(4):
                                m = nc.tensor.matmul(p_tab[:, u, :], hotT[q][:, u, :],
                                                     tab[:, bass.ds(tiles[u], 1), :].rearrange("p o h -> p (o h)"), start=True, stop=True)
                            m.then_inc(tab_ready, 1)

                        def work(j, q, i, tiles):
                            if not is_last(j):
                                pe.wait_ge(arg_ready, j + 1)
                                look_up(j + 1, 1 - q, tiles)
                            pe.wait_ge(hot_ready, j + 1)
                            for u in range(4):
                                pe.wait_ge(msg_ready, j * 4 + u + 1)
                                if not is_first(j):
                                    pe.wait_ge(added, j * 4 + u - 2)
                                nc.tensor.matmul(p_out[u][:], hot[q][:, u, :], msg[q][:, u, :], start=True, stop=True)
                                nc.tensor.matmul(p_den[q][:, u, :], hot[q][:, u, :], weight[q][:, u, :],
                                                 start=True, stop=True).then_inc(sums_ready, 1)

                        def pair_of(i, last):
                            tiles = read_registers(nc, step_table, i * 8 + 4, 4 if last else 8, ET.PE, NT - 1)
                            work(i * 2, 0, i, tiles[0:4])
                            work(i * 2 + 1, 1, i, tiles[4:8])

                        look_up(0, 0, read_registers(nc, step_table, 0, 4, ET.PE, NT - 1))
                        pair_of(0, False)
                        with pe.Fori(1, G4 // 2 - 1) as i:
                            pair_of(i, False)
                        pair_of(G4 // 2 - 1, True)

                    @block.vector
                    def _(dve):
                        o = Order(dve, b_order)
                        TT, TS = nc.vector.tensor_tensor, nc.vector.tensor_scalar
                        dve.nop().then_inc(hotT_ready, 2)
                        dve.wait_ge(own_in, 16)
                        for t in range(NT):
                            TT(acc[:, t, 0:HD].rearrange("p (h c) -> p h c", h=HW), acc[:, t, 0:HD].rearrange("p (h c) -> p h c", h=HW),
                               self_s[:, t, :].unsqueeze(2).broadcast_to([P, HW, HD // HW]), ALU.mult)
                        o.link(nc.vector.tensor_copy(acc[:, :, HD:], self_s[:]))
                        dve.nop().then_inc(added, 1)
                        spread = [P, 4, P]

                        def node_hot(g, q, i):
                            dve.wait_ge(rep_in[q], i * 16 + 16)
                            TS(hotT[q][:], dl_rep[q][:], pidx[:, 0:1], None, ALU.is_equal).then_inc(hotT_ready, 1)

                        def edge_hot(g, q):
                            TT(hot[q][:], iota_row[:].unsqueeze(1).broadcast_to(spread),
                               dl_step[:, bass.ds(g * 4, 4)].unsqueeze(2).broadcast_to(spread), ALU.is_equal).then_inc(hot_ready, 1)

                        def weigh(g, q, u):
                            TT(msg[q][:, u, :].rearrange("p (h c) -> p h c", h=HW), row_g[q][:, u, 0:HD].rearrange("p (h c) -> p h c", h=HW),
                               weight[q][:, u, :].unsqueeze(2).broadcast_to([P, HW, HD // HW]), ALU.mult).then_inc(msg_ready, 1)

                        def add_sums(g, q, u, tiles):
                            dve.wait_ge(sums_ready, g * 4 + u + 1)
                            dve.wait_ge(added, g * 4 + u + 1)
                            own = acc[:, bass.ds(tiles[u], 1), 0:HD].rearrange("p o s -> p (o s)")
                            TT(own, own, p_out[u][:], ALU.add).then_inc(added, 1)

                        def add_weights(g, q, tiles):
                            for u in range(4):
                                own = acc[:, bass.ds(tiles[u], 1), HD:].rearrange("p o s -> p (o s)")
                                o.link(TT(own, own, p_den[q][:, u, :], ALU.add))

                        def work(j, q, i, tiles):
                            if not is_first(j):
                                o.enter(j)
                            dve.wait_ge(rows_in[q], i * 64 + 64)
                            dve.wait_ge(tab_ready, j + 1)
                            o.link(TT(zz[:], p_tab[:, :, 0:HW], row_g[q][:, :, HD:], ALU.add))
                            o.link(nc.vector.scalar_tensor_tensor(zz[:], zz[:], 0.2, zz[:], ALU.mult, ALU.max))
                            o.link(TT(zz[:], zz[:], p_tab[:, :, HW:], ALU.subtract))
                            TS(zz[:], zz[:], 0.0, None, ALU.min).then_inc(arg_ready, 1)
                            if not is_last(j):
                                node_hot(j + 1, 1 - q, i + q)
                            before = not is_first(j)
                            if before:
                                add_sums(j - 1, 1 - q, 0, tiles)
                                add_sums(j - 1, 1 - q, 1, tiles)
                            dve.wait_ge(weight_ready, j + 1)
                            weigh(j, q, 0)
                            if before:
                                add_sums(j - 1, 1 - q, 2, tiles)
                            weigh(j, q, 1)
                            if before:
                                add_sums(j - 1, 1 - q, 3, tiles)
                                add_weights(j - 1, 1 - q, tiles)
                            if not is_last(j):
                                edge_hot(j + 1, 1 - q)
                            weigh(j, q, 2)
                            weigh(j, q, 3)

                        node_hot(0, 0, 0)
                        edge_hot(0, 0)
                        work(0, 0, 0, None)
                        o.begin(7, first=1)
                        work(1, 1, 0, read_registers(nc, step_table, 0, 4, ET.DVE, NT - 1))
                        with dve.Fori(1, G4 // 2 - 1) as i:
                            tiles = read_registers(nc, step_table, i * 8 - 4, 8, ET.DVE, NT - 1)
                            work(i * 2, 0, i, tiles[0:4])
                            work(i * 2 + 1, 1, i, tiles[4:8])
                        tiles = read_registers(nc, step_table, S - 12, 8, ET.DVE, NT - 1)
                        work(G4 - 2, 0, G4 // 2 - 1, tiles[0:4])
                        work(G4 - 1, 1, G4 // 2 - 1, tiles[4:8])
                        o.leave(G4)
                        tiles = read_registers(nc, step_table, S - 4, 4, ET.DVE, NT - 1)
                        for u in range(4):
                            add_sums(G4 - 1, 1, u, tiles)
                        add_weights(G4 - 1, 1, tiles)
            with ExitStack() as inner:
                wu = sb("wu", [P, 4, D], F32, inner)
                brow = sb("brow", [P, HD + D], F32, inner)
                den = sb("den", [P, NT, HW], F32, inner)
                val = sb("val", [P, 5, HD], F32, inner)
                neg = sb("neg", [P, 5, HD], F32, inner)
                valT = sb("valT", [P, 5, 4, P], F32, inner)
                p_val = [ps(f"p_val{v}", [P, 4, P], F32, inner) for v in range(2)]
                p_uni = [ps(f"p_uni{v}", [P, D], F32, inner) for v in range(2)]
                c_in, c_order, neg_ready, exp_ready, elu_ready, val_turned, valT_ready, uni_ready, x_added = (
                    sem("c_in"), sem("c_order"), sem("neg_ready"), sem("exp_ready"), sem("elu_ready"), sem("val_turned"),
                    sem("valT_ready"), sem("uni_ready"), sem("x_added"))
                with nc.Block() as block:
                    @block.sync
                    def _(sp):
                        sp.dma_start(wu[:], a["Wu"].rearrange("(k p) d -> p k d", k=4)).then_inc(c_in, 16)
                        for name, w in (("b1", slice(0, 256)), ("b2", slice(256, HD)), ("bu", slice(HD, HD + D))):
                            sp.dma_start(brow[:, w], a[name].partition_broadcast(P)).then_inc(c_in, 16)

                    @block.vector
                    def _(dve):
                        o = Order(dve, c_order)
                        TT = nc.vector.tensor_tensor
                        o.link(nc.vector.tensor_scalar(den[:], acc[:, :, HD:], 1e-16, None, ALU.add))
                        o.link(nc.vector.reciprocal(den[:], den[:]))
                        dve.wait_ge(c_in, 64)
                        o.begin(5 * 3)
                        with dve.Fori(0, R) as i:
                            o.enter(i)
                            for u in range(5):
                                t = i * 5 + u
                                dve.wait_ge(val_turned, i * 5 + u + 1)
                                o.link(TT(val[:, u, :].rearrange("p (h c) -> p h c", h=HW),
                                          acc[:, bass.ds(t, 1), 0:HD].rearrange("p o (h c) -> p (o h) c", h=HW),
                                          den[:, bass.ds(t, 1), :].rearrange("p o h -> p (o h)").unsqueeze(2).broadcast_to([P, HW, HD // HW]), ALU.mult))
                                o.link(TT(val[:, u, :], val[:, u, :], brow[:, 0:HD], ALU.add))
                                nc.vector.tensor_scalar(neg[:, u, :], val[:, u, :], 0.0, None, ALU.min).then_inc(neg_ready, 1)
                                o.link(nc.vector.tensor_scalar(val[:, u, :], val[:, u, :], 0.0, -1.0, ALU.max, ALU.add))
                                dve.wait_ge(exp_ready, t + 1)
                                TT(val[:, u, :], val[:, u, :], neg[:, u, :], ALU.add).then_inc(elu_ready, 1)
                            for u in range(5):
                                t = i * 5 + u
                                dve.wait_ge(uni_ready, t + 1)
                                own = x_sb[:, bass.ds(t, 1), :].rearrange("p o d -> p (o d)")
                                TT(own, own, p_uni[u % 2][:], ALU.add).then_inc(x_added, 1)
                        o.leave(R)
                        dve.wait_ge(x_added, NT)
                        o.link(TT(x_sb[:], x_sb[:], brow[:, HD:].unsqueeze(1).broadcast_to([P, NT, D]), ALU.add))

                    @block.scalar
                    def _(act):
                        with act.Fori(0, R) as i:
                            for u in range(5):
                                act.wait_ge(neg_ready, i * 5 + u + 1)
                                nc.scalar.activation(neg[:, u, :], neg[:, u, :], ACT.Exp).then_inc(exp_ready, 1)
                            for u in range(5):
                                act.wait_ge(val_turned, 5 + i * 5 + u + 1)
                                nc.scalar.copy(valT[:, u], p_val[u % 2][:]).then_inc(valT_ready, 1)

                    @block.tensor
                    def _(pe):
                        pe.nop().then_inc(val_turned, 5)
                        def round_of(i):
                            for u in range(5):
                                t = i * 5 + u
                                pe.wait_ge(elu_ready, t + 1)
                                if u >= 2 or not is_first(i):
                                    pe.wait_ge(valT_ready, t - 1)
                                for k in range(4):
                                    m = nc.tensor.transpose(p_val[u % 2][:, k, :], val[:, u, k * P:(k + 1) * P], ident[:])
                                m.then_inc(val_turned, 1)
                                pe.wait_ge(valT_ready, t + 1)
                                if u >= 2 or not is_first(i):
                                    pe.wait_ge(x_added, t - 1)
                                for k in range(4):
                                    m = nc.tensor.matmul(p_uni[u % 2][:], valT[:, u, k, :], wu[:, k, :], start=(k == 0), stop=(k == 3))
                                m.then_inc(uni_ready, 1)

                        looped(pe, R, round_of)
        early.close()

        by_src = dram("by_src", [NP, NP], F16)
        by_dst = dram("by_dst", [NP, NP], F16)
        with ExitStack() as ctx:
            cnt = [sb(f"cnt{q}", [P, NP], F32, ctx) for q in range(2)]
            half = [sb(f"half{q}", [P, NP], F16, ctx) for q in range(2)]
            halfT = [sb(f"halfT{q}", [P, NT, P], F16, ctx) for q in range(2)]
            p_t = [ps(f"cv_p{v}", [P, 5, P], F16, ctx) for v in range(2)]
            cnt_in = [sem(f"cnt_in{q}") for q in range(2)]
            halves, blocks, blocks_out, blocks_free = sem("halves"), sem("blocks"), sem("blocks_out"), sem("blocks_free")
            stored = [sem(f"stored{q}") for q in range(2)]
            with nc.Block() as block:
                def tile_of(i, q):
                    return i * 2 + q

                @block.sync
                def _(sp):
                    def load(t, q):
                        sp.wait_ge(halves, t + 1)
                        sp.nop().then_inc(waits_passed, 1)
                        sp.dma_start(cnt[q][:], count_dram[bass.ds(t * (P * NP), P * NP), :].rearrange("(p f) o -> p (f o)", p=P)).then_inc(cnt_in[q], 16)

                    def store(t, q):
                        sp.wait_ge(halves, t + 3)
                        sp.nop().then_inc(waits_passed, 1)
                        sp.dma_start(by_src[bass.ds(t * P, P), :], half[q][:]).then_inc(stored[q], 16)
                        sp.wait_ge(blocks_out, t * 5 + 5)
                        sp.nop().then_inc(waits_passed, 1)
                        sp.dma_start(by_dst.rearrange("(k p) s -> p k s", p=P)[:, :, bass.ds(t * P, P)], halfT[q][:]).then_inc(stored[q], 16)

                    load(0, 0)
                    with sp.Fori(0, NT // 2) as i:
                        for q in range(2):
                            load(i * 2 + q + 1, 1 - q)
                            store(i * 2 + q, q)
                    store(NT - 1, 0)
                    sp.wait_ge(stored[0], 32 * (NT // 2 + 1))
                    sp.wait_ge(stored[1], 32 * (NT // 2))

                @block.scalar
                def _(act):
                    act.nop().then_inc(halves, 2)

                    def convert(t, q, i):
                        act.wait_ge(cnt_in[q], i * 16 + 16)
                        act.wait_ge(stored[q], i * 32)
                        nc.scalar.activation(half[q][:], cnt[q][:], ACT.Copy, accum_out=column(degsrc, t)).then_inc(halves, 1)

                    def round_of(i):
                        for q in range(2):
                            convert(i * 2 + q, q, i)

                    looped(act, NT // 2, round_of)
                    convert(NT - 1, 0, NT // 2)

                @block.tensor
                def _(pe):
                    def turn(t, q):
                        pe.wait_ge(halves, t + 3)
                        for b in range(5):
                            pe.wait_ge(blocks_free, t * 5 + b + 1)
                            for k in range(5):
                                m = nc.tensor.transpose(p_t[(b + q) % 2][:, k, :], half[q][:, (b * 5 + k) * P:(b * 5 + k + 1) * P], ident16[:])
                            m.then_inc(blocks, 1)

                    with pe.Fori(0, NT // 2) as i:
                        for q in range(2):
                            turn(i * 2 + q, q)
                    turn(NT - 1, 0)

                @block.vector
                def _(dve):
                    dve.nop().then_inc(blocks_free, 2)

                    def take(t, q, i):
                        for b in range(5):
                            if b == 0:
                                dve.wait_ge(stored[q], i * 32)
                            dve.wait_ge(blocks, t * 5 + b + 1)
                            nc.vector.tensor_copy(halfT[q][:, b * 5:b * 5 + 5, :], p_t[(b + q) % 2][:]).then_inc(blocks_out, 1)
                            dve.wait_ge(blocks_out, t * 5 + b + 1)
                            dve.nop().then_inc(blocks_free, 1)

                    def round_of(i):
                        for q in range(2):
                            take(i * 2 + q, q, i)

                    looped(dve, NT // 2, round_of)
                    take(NT - 1, 0, NT // 2)
        end_stage()

        with ExitStack() as ctx:
            hT = sb("hT", [P, 2, NP], F32, ctx)
            aggT = sb("aggT", [P, 2, NP], F32, ctx)
            parts = sb("parts", [P, NT, 2, 2, P], F16, ctx)
            cbuf = [sb(f"cbuf{q}", [P, NT, W], F16, ctx) for q in range(2)]
            wslot = sb("wslot", [P, 4, D], F32, ctx)
            ewslot = sb("ewslot", [4, D], F32, ctx)
            FT = sb("FT", [4, NP], F32, ctx)
            dinv_rep = sb("dinv_rep", [P, NP], F32, ctx)
            low_sb = [sb(f"low_sb{m}", [P, W], F32, ctx) for m in range(2)]
            rest = [sb(f"rest{v}", [P, 2, P], F32, ctx) for v in range(2)]
            bn_tab = sb("bn_tab", [P, LAYERS, 3, 2], F32, ctx)
            floor = sb("floor", [P, LAYERS], F32, ctx)
            bn_raw = sb("bn_raw", [P, 2, NC, 6], F32, ctx)
            bn_mv = sb("bn_mv", [P, 2, 2], F32, ctx)
            bn_rs = sb("bn_rs", [P, 4, 2], F32, ctx)
            dinv_dram = dram("dinv_dram", [NP], F32)
            p_hi = [ps(f"p_hi{m}", [P, W], F32, ctx) for m in range(2)]
            p_lo = [ps(f"p_lo{m}", [P, W], F32, ctx) for m in range(2)]
            p_new = [ps(f"p_new{m}", [P, W], F32, ctx) for m in range(2)]
            p_turn = [ps(f"l_p_turn{v}", [P, 2, P], F32, ctx) for v in range(2)]

            h1 = aggT[:].rearrange("p m n -> p (m n)").rearrange("p (t d) -> p t d", d=D)
            norm_scales("n2", x_sb)
            norm_apply("n2", x_sb, h1, ACT.Relu)
            s_turned, s_taken, s_in, s_dv = sem("s_turned"), sem("s_taken"), sem("s_in"), sem("s_dv")
            with nc.Block() as block:
                @block.sync
                def _(sp):
                    sp.dma_start(dinv_dram.rearrange("(t p) -> p t", p=P), dinv[:]).then_inc(s_in, 16)
                    sp.wait_ge(s_in, 16)
                    sp.dma_start(dinv_rep[:], dinv_dram.partition_broadcast(P)).then_inc(s_in, 16)
                    for n, name in enumerate(("mlp_b", "bn_g", "bn_b")):
                        for m in range(2):
                            sp.dma_start(bn_tab[:, :, n, m], a[name].rearrange("l (m p) -> m p l", m=2)[m]).then_inc(s_in, 16)
                    sp.wait_ge(s_in, 16 * 8)

                @block.tensor
                def _(pe):
                    for t in range(NT):
                        if t >= 2:
                            pe.wait_ge(s_taken, t - 1)
                        for m in range(2):
                            k = nc.tensor.transpose(p_turn[t % 2][:, m, :], h1[:, t, m * P:(m + 1) * P], ident[:])
                        k.then_inc(s_turned, 1)
                    for t in range(NT):
                        pe.wait_ge(s_taken, NT + t - 1 if t else NT)
                        nc.tensor.transpose(p_turn[t % 2][0:4, 0, :], F_sb[:, t, :], ident[:]).then_inc(s_turned, 1)

                @block.vector
                def _(dve):
                    nc.vector.memset(floor[:], 0.0).then_inc(s_dv, 1)
                    dve.wait_ge(s_dv, 1)
                    nc.vector.memset(floor[:, LAYERS - 1:], -3.0e38)
                    nc.vector.memset(ewslot[:], 0.0)
                    for t in range(NT):
                        dve.wait_ge(s_turned, t + 1)
                        nc.vector.tensor_copy(hT[:, :, t * P:(t + 1) * P], p_turn[t % 2][:]).then_inc(s_taken, 1)
                    for t in range(NT):
                        dve.wait_ge(s_turned, NT + t + 1)
                        nc.vector.tensor_copy(FT[:, t * P:(t + 1) * P], p_turn[t % 2][0:4, 0, :]).then_inc(s_taken, 1)

            (turned, rest_ready, high_ready, low_ready, sums, low_out, agg_ready, news, new_ready, chunk_used, layer_done,
             var_ready, root_ready, bn_order, scaled, w_loaded, w_used) = (sem("l_" + x) for x in (
                 "turned", "rest_ready", "high_ready", "low_ready", "sums", "low_out", "agg_ready", "news", "new_ready", "chunk_used",
                 "layer_done", "var_ready", "root_ready", "bn_order", "scaled", "w_loaded", "w_used"))
            halfway, halfway2 = sem("l_halfway"), sem("l_halfway2")
            chunk_in = [sem(f"l_chunk_in{q}") for q in range(2)]

            def load_chunk(sp, matrix, l, i, q):
                sp.wait_ge(chunk_used, l * NC + i * 2 + q + 1)
                sp.nop().then_inc(waits_passed, 1)
                sp.dma_start(cbuf[q][:], matrix.rearrange("(k p) n -> p k n", p=P)[:, :, bass.ds((i * 2 + q) * W, W)]).then_inc(chunk_in[q], 16)

            def aggregate(pe, l, c, q, edge_term):
                pe.wait_ge(chunk_in[q], l * (16 * NC // 2) + (c - q) * 8 + 16)
                for m in range(2):
                    pe.wait_ge(agg_ready, l * (2 * NC) + c * 2 + m + 1)
                    for k in range(NT):
                        nc.tensor.matmul(p_lo[m][:], parts[:, k, m, 1, :], cbuf[q][:, k, :], start=(k == 0), stop=(k == NT - 1))
                        last = nc.tensor.matmul(p_hi[m][:], parts[:, k, m, 0, :], cbuf[q][:, k, :], start=(k == 0),
                                                stop=(k == NT - 1 and not edge_term))
                    if edge_term:
                        last = nc.tensor.matmul(p_hi[m][:], ewslot[:, m * P:(m + 1) * P], FT[:, bass.ds(c * W, W)], start=False, stop=True)
                    last.then_inc(sums, 1)
                pe.wait_ge(sums, l * (2 * NC) + c * 2 + 2)
                pe.nop().then_inc(chunk_used, 1)

            def take_low(act, l, c):
                for m in range(2):
                    act.wait_ge(sums, l * (2 * NC) + c * 2 + m + 1)
                    act.wait_ge(agg_ready, l * (2 * NC) + c * 2 + m + 1)
                    nc.scalar.mul(low_sb[m][:], p_lo[m][:], 1.0 / LO).then_inc(low_out, 1)

            def sum_up(dve, l, c, by_degree):
                for m in range(2):
                    dve.wait_ge(low_out, l * (2 * NC) + c * 2 + m + 1)
                    part = aggT[:, m, bass.ds(c * W, W)]
                    whole = nc.vector.tensor_tensor(part, p_hi[m][:], low_sb[m][:], ALU.add)
                    if by_degree:
                        whole.then_inc(halfway, 1)
                        dve.wait_ge(halfway, l * (2 * NC) + c * 2 + m + 1)
                        whole = nc.vector.tensor_tensor(part, part, dinv_rep[:, bass.ds(c * W, W)], ALU.mult)
                    whole.then_inc(agg_ready, 1)

            with nc.Block() as block:
                @block.sync
                def _(sp):
                    with sp.Fori(0, LAYERS) as l:
                        sp.wait_ge(w_used, l + 1)
                        sp.nop().then_inc(waits_passed, 1)
                        sp.dma_start(wslot[:], a["mlp_w"][bass.ds(l, 1)].rearrange("l (k p) d -> p (l k) d", p=P)).then_inc(w_loaded, 16)
                        sp.dma_start(ewslot[0:3, P:D], a["ew2"][bass.ds(l, 1)].rearrange("l c d -> (l c) d")).then_inc(w_loaded, 16)
                        sp.dma_start(ewslot[3:4, 0:P], a["ew1"][bass.ds(l, 1)].rearrange("l c d -> (l c) d")).then_inc(w_loaded, 16)
                        with sp.Fori(0, NC // 2) as i:
                            for q in range(2):
                                load_chunk(sp, by_src, l, i, q)

                @block.tensor
                def _(pe):
                    pe.nop().then_inc(chunk_used, 2)

                    def layer_product(l, c):
                        pe.wait_ge(agg_ready, l * (2 * NC) + c * 2 + 4)
                        for m in range(2):
                            pe.wait_ge(new_ready, l * (2 * NC) + c * 2 + m + 1)
                            for k in range(4):
                                state = (hT if k < 2 else aggT)[:, k % 2, bass.ds(c * W, W)]
                                r = nc.tensor.matmul(p_new[m][:], wslot[:, k, m * P:(m + 1) * P], state, start=(k == 0), stop=(k == 3))
                            r.then_inc(news, 1)

                    with pe.Fori(0, LAYERS) as l:
                        pe.wait_ge(layer_done, l + 1)
                        for t in range(NT):
                            pe.wait_ge(rest_ready, l * NT + t + 1)
                            for m in range(2):
                                r = nc.tensor.transpose(p_turn[t % 2][:, m, :], hT[:, m, t * P:(t + 1) * P], ident[:])
                            r.then_inc(turned, 1)
                        pe.wait_ge(w_loaded, l * 48 + 48)
                        pe.wait_ge(low_ready, (l + 1) * NT)
                        aggregate(pe, l, 0, 0, True)
                        with pe.Fori(0, NC // 2 - 1) as i:
                            for q in (1, 0):
                                c = i * 2 + (1 if q else 2)
                                aggregate(pe, l, c, q, True)
                                layer_product(l, c - 1)
                        aggregate(pe, l, NC - 1, 1, True)
                        layer_product(l, NC - 2)
                        layer_product(l, NC - 1)

                @block.scalar
                def _(act):
                    act.nop().then_inc(new_ready, 2)

                    def take_new(l, c):
                        act.wait_ge(news, l * (2 * NC) + c * 2 + 2)
                        act.nop().then_inc(waits_passed, 1)
                        for m in range(2):
                            nc.scalar.activation(hT[:, m, bass.ds(c * W, W)], p_new[m][:], ACT.Relu,
                                                 bias=bn_tab[:, bass.ds(l, 1), 0, m]).then_inc(new_ready, 1)

                    with act.Fori(0, LAYERS) as l:
                        for t in range(NT + 1):
                            if t < NT:
                                act.wait_ge(turned, l * NT + t + 1)
                                nc.scalar.activation(parts[:, t, :, 0, :], p_turn[t % 2][:], ACT.Copy, scale=dinv[:, t:t + 1]).then_inc(high_ready, 1)
                            if t > 0:
                                act.wait_ge(rest_ready, l * NT + t + 2)
                                nc.scalar.mul(parts[:, t - 1, :, 1, :], rest[(t - 1) % 2][:], LO).then_inc(low_ready, 1)
                        take_low(act, l, 0)
                        with act.Fori(0, NC // 2 - 1) as i:
                            for q in (1, 0):
                                c = i * 2 + (1 if q else 2)
                                take_low(act, l, c)
                                take_new(l, c - 1)
                        take_low(act, l, NC - 1)
                        take_new(l, NC - 2)
                        take_new(l, NC - 1)
                        act.wait_ge(var_ready, l + 1)
                        nc.scalar.activation(bn_rs[:, 0, :], bn_rs[:, 3, :], ACT.Sqrt).then_inc(root_ready, 1)
                        act.wait_ge(bn_order, l * 6 + 5)
                        for m in range(2):
                            nc.scalar.activation(hT[:, m, :], hT[:, m, :], ACT.Identity, bias=bn_rs[:, 2, m:m + 1],
                                                 scale=bn_rs[:, 1, m:m + 1]).then_inc(scaled, 1)

                @block.vector
                def _(dve):
                    TT, TS, STT = nc.vector.tensor_tensor, nc.vector.tensor_scalar, nc.vector.scalar_tensor_tensor
                    dve.nop().then_inc(rest_ready, 2)
                    dve.nop().then_inc(w_used, 1)
                    dve.nop().then_inc(layer_done, 1)
                    dve.nop().then_inc(agg_ready, 2)
                    o = Order(dve, bn_order)

                    o.begin(6)
                    with dve.Fori(0, LAYERS) as l:
                        o.enter(l)
                        for t in range(NT):
                            dve.wait_ge(high_ready, l * NT + t + 1)
                            if t >= 2:
                                dve.wait_ge(low_ready, l * NT + t - 1)
                            STT(rest[t % 2][:], p_turn[t % 2][:], dinv[:, t:t + 1], parts[:, t, :, 0, :], ALU.mult, ALU.subtract).then_inc(rest_ready, 1)
                        with dve.Fori(0, NC) as c:
                            sum_up(dve, l, c, True)
                        for c in range(NC):
                            for m in range(2):
                                if c % 2 == 0:
                                    dve.wait_ge(new_ready, l * (2 * NC) + c * 2 + 2 + 4) if m == 0 else None
                                n = min(W, N - c * W)
                                k = nc.vector.bn_stats(bn_raw[:, m, c, :], hT[:, m, c * W:c * W + n])
                        o.link(k)
                        dve.nop().then_inc(waits_passed, 1)
                        for m in range(2):
                            k = nc.vector.bn_aggr(bn_mv[:, m, :], bn_raw[:, m].rearrange("p c s -> p (c s)"))
                        o.link(k)
                        o.link(TS(bn_rs[:, 3, :], bn_mv[:, :, 1], EPS, None, ALU.add))
                        dve.nop().then_inc(var_ready, 1)
                        dve.wait_ge(root_ready, l + 1)
                        gain, offset = (bn_tab[:, bass.ds(l, 1), n, :].rearrange("p o m -> p (o m)") for n in (1, 2))
                        nc.vector.reciprocal(bn_rs[:, 1, :], bn_rs[:, 0, :]).then_inc(halfway2, 1)
                        dve.wait_ge(halfway2, l * 3 + 1)
                        TT(bn_rs[:, 1, :], bn_rs[:, 1, :], gain, ALU.mult).then_inc(halfway2, 1)
                        dve.wait_ge(halfway2, l * 3 + 2)
                        TT(bn_rs[:, 2, :], bn_mv[:, :, 0], bn_rs[:, 1, :], ALU.mult).then_inc(halfway2, 1)
                        dve.wait_ge(halfway2, l * 3 + 3)
                        o.link(TT(bn_rs[:, 2, :], offset, bn_rs[:, 2, :], ALU.subtract))
                        dve.nop().then_inc(w_used, 1)
                        dve.nop().then_inc(bn_order, 1)
                        for m in range(2):
                            dve.wait_ge(scaled, l * 2 + m + 1)
                            k = TS(hT[:, m, :], hT[:, m, :], column(floor, l), None, ALU.max)
                        k.then_inc(bn_order, 1)
                        dve.wait_ge(bn_order, l * 6 + 6)
                        dve.nop().then_inc(layer_done, 1)

            with nc.Block() as block:
                @block.tensor
                def _(pe):
                    for t in range(NT):
                        if t >= 2:
                            pe.wait_ge(s_taken, 2 * NT + t - 1)
                        for m in range(2):
                            k = nc.tensor.transpose(p_turn[t % 2][:, m, :], hT[:, m, t * P:(t + 1) * P], ident[:])
                        k.then_inc(s_turned, 1)

                @block.vector
                def _(dve):
                    for t in range(NT):
                        dve.wait_ge(s_turned, 2 * NT + t + 1)
                        nc.vector.tensor_tensor(x_sb[:, t, :].rearrange("p (m d) -> p m d", m=2), x_sb[:, t, :].rearrange("p (m d) -> p m d", m=2),
                                                p_turn[t % 2][:], ALU.add).then_inc(s_taken, 1)
            norm_scales("n3", x_sb)
            norm_apply("n3", x_sb, h1, ACT.Relu)
            split, g_in, g_order = sem("g_split"), sem("g_in"), sem("g_order")
            with ExitStack() as inner:
                gw = sb("gw", [P, 2, D], F32, inner)
                g_brow = sb("g_brow", [P, D], F32, inner)
                inv_deg = sb("inv_deg", [P, NT], F32, inner)
                has_deg = sb("has_deg", [P, NT], F32, inner)
                with nc.Block() as block:
                    @block.sync
                    def _(sp):
                        sp.dma_start(gw[:], a["L2_W"].rearrange("(k p) d -> p k d", k=2)).then_inc(g_in, 16)
                        sp.dma_start(g_brow[:], a["L2_b"].partition_broadcast(P)).then_inc(g_in, 16)
                        sp.wait_ge(g_in, 32)

                    @block.scalar
                    def _(act):
                        h_parts = h1.rearrange("p t (m d) -> p t m d", m=2)
                        nc.scalar.copy(parts[:, :, :, 0, :], h_parts).then_inc(split, 1)
                        act.wait_ge(split, 2)
                        nc.scalar.mul(parts[:, :, :, 1, :], h_parts, LO)

                    @block.vector
                    def _(dve):
                        o = Order(dve, g_order)
                        h_parts = h1.rearrange("p t (m d) -> p t m d", m=2)
                        o.did(nc.vector.tensor_scalar(has_deg[:], degsrc[:], 0.5, None, ALU.is_ge))
                        o.link(nc.vector.tensor_scalar(inv_deg[:], degsrc[:], 1.0, None, ALU.max))
                        o.link(nc.vector.reciprocal(inv_deg[:], inv_deg[:]))
                        o.link(nc.vector.tensor_tensor(inv_deg[:], inv_deg[:], has_deg[:], ALU.mult))
                        dve.wait_ge(split, 1)
                        nc.vector.tensor_tensor(h_parts, h_parts, parts[:, :, :, 0, :], ALU.subtract).then_inc(split, 1)

                with nc.Block() as block:
                    @block.sync
                    def _(sp):
                        with sp.Fori(0, NC // 2) as i:
                            for q in range(2):
                                load_chunk(sp, by_dst, LAYERS, i, q)

                    @block.tensor
                    def _(pe):
                        with pe.Fori(0, NC // 2) as i:
                            for q in range(2):
                                aggregate(pe, LAYERS, i * 2 + q, q, False)

                    @block.scalar
                    def _(act):
                        with act.Fori(0, NC) as c:
                            take_low(act, LAYERS, c)

                    @block.vector
                    def _(dve):
                        with dve.Fori(0, NC) as c:
                            sum_up(dve, LAYERS, c, False)

                p_conv, conv_ready, conv_taken = p_turn, sem("conv_ready"), sem("conv_taken")
                with nc.Block() as block:
                    @block.tensor
                    def _(pe):
                        for t in range(NT):
                            if t >= 2:
                                pe.wait_ge(conv_taken, t - 1)
                            for k in range(2):
                                r = nc.tensor.matmul(p_conv[t % 2][:].rearrange("p m d -> p (m d)"), aggT[:, k, t * P:(t + 1) * P], gw[:, k, :],
                                                     start=(k == 0), stop=(k == 1))
                            r.then_inc(conv_ready, 1)

                    @block.vector
                    def _(dve):
                        STT = nc.vector.scalar_tensor_tensor
                        for t in range(NT):
                            STT(x_sb[:, t, :], g_brow[:], has_deg[:, t:t + 1], x_sb[:, t, :], ALU.mult, ALU.add).then_inc(g_order, 1)
                        for t in range(NT):
                            dve.wait_ge(conv_ready, t + 1)
                            dve.wait_ge(g_order, 4 + t + 1)
                            STT(x_sb[:, t, :], p_conv[t % 2][:].rearrange("p m d -> p (m d)"), inv_deg[:, t:t + 1], x_sb[:, t, :],
                                ALU.mult, ALU.add).then_inc(conv_taken, 1)
        end_stage()

        with ExitStack() as ctx:
            h3 = sb("h3", [P, NT, D], F32, ctx)
            h3T = sb("h3T", [P, 2, NP], F32, ctx)
            m_in = sem("m_in")
            norm_scales("n4", x_sb)
            norm_apply("n4", x_sb, h3, ACT.Relu)

            src_dram = dram("src_dram", [NP, D], F32)
            with ExitStack() as inner:
                dst_part = sb("dst_part", [P, NT, D], F32, inner)
                attr_w = sb("attr_w", [ED, D], F32, inner)
                with ExitStack() as inmost:
                    node_w = sb("node_w", [P, 4, D], F32, inmost)
                    m_brow = sb("m_brow", [P, D], F32, inmost)
                    src_part = sb("src_part", [P, NT, D], F32, inmost)
                    p_turn = [ps(f"m_p_turn{v}", [P, 2, P], F32, inmost) for v in range(2)]
                    p_parts = [[ps(f"m_p_parts{v}{n}", [P, D], F32, inmost) for n in range(2)] for v in range(2)]
                    turned, taken, products, src_ready, dst_ready, src_out = (
                        sem("m_" + x) for x in ("turned", "taken", "products", "src_ready", "dst_ready", "src_out"))
                    with nc.Block() as block:
                        @block.sync
                        def _(sp):
                            sp.dma_start(node_w[:], a["m_W1T"][0:2 * D].rearrange("(k p) d -> p k d", p=P)).then_inc(m_in, 16)
                            sp.dma_start(attr_w[:], a["m_W1T"][2 * D:]).then_inc(m_in, 16)
                            sp.dma_start(m_brow[:], a["m_b1"].partition_broadcast(P)).then_inc(m_in, 16)
                            for part in range(5):
                                sp.wait_ge(src_ready, (part + 1) * 5)
                                sp.dma_start(src_dram.rearrange("(t p) d -> p t d", p=P)[:, part * 5:part * 5 + 5, :],
                                             src_part[:, part * 5:part * 5 + 5, :]).then_inc(src_out, 16)
                            sp.wait_ge(src_out, 80)

                        @block.tensor
                        def _(pe):
                            def turn(t):
                                if t >= 2:
                                    pe.wait_ge(taken, t - 1)
                                for m in range(2):
                                    k = nc.tensor.transpose(p_turn[t % 2][:, m, :], h3[:, t, m * P:(m + 1) * P], ident[:])
                                k.then_inc(turned, 1)

                            turn(0)
                            pe.wait_ge(m_in, 48)
                            for t in range(NT):
                                if t + 1 < NT:
                                    turn(t + 1)
                                pe.wait_ge(taken, t + 1)
                                if t >= 2:
                                    pe.wait_ge(src_ready, t - 1)
                                    pe.wait_ge(dst_ready, t - 1)
                                for n in range(2):
                                    for k in range(2):
                                        r = nc.tensor.matmul(p_parts[t % 2][n][:], h3T[:, k, t * P:(t + 1) * P], node_w[:, 2 * n + k, :],
                                                             start=(k == 0), stop=(k == 1))
                                r.then_inc(products, 1)

                        @block.scalar
                        def _(act):
                            for t in range(NT):
                                act.wait_ge(products, t + 1)
                                nc.scalar.copy(dst_part[:, t, :], p_parts[t % 2][1][:]).then_inc(dst_ready, 1)

                        @block.vector
                        def _(dve):
                            def take(t):
                                dve.wait_ge(turned, t + 1)
                                nc.vector.tensor_copy(h3T[:, :, t * P:(t + 1) * P], p_turn[t % 2][:]).then_inc(taken, 1)

                            take(0)
                            dve.wait_ge(m_in, 48)
                            for t in range(NT):
                                if t + 1 < NT:
                                    take(t + 1)
                                dve.wait_ge(products, t + 1)
                                nc.vector.tensor_tensor(src_part[:, t, :], p_parts[t % 2][0][:], m_brow[:], ALU.add).then_inc(src_ready, 1)

                msg_step = sb("msg_step", [P, S], F32, inner)
                own_row = sb("own_row", [P, 1], F32, inner)
                idx = [sb(f"m_idx{q}", [P, 4], I32, inner) for q in range(2)]
                src_rows = [sb(f"src_rows{q}", [P, 4, D], F32, inner) for q in range(2)]
                msg = [sb(f"m_msg{q}", [P, 4, D], F32, inner) for q in range(2)]
                attrT = [sb(f"attrT{q}", [ED, 4, P], F32, inner) for q in range(2)]
                pair = [sb(f"pair{q}", [P, 4, 2, P], F32, inner) for q in range(2)]
                hotT = [sb(f"m_hotT{q}", [P, 4, P], F32, inner) for q in range(2)]
                same = [sb(f"m_same{q}", [P, 4, P], F32, inner) for q in range(2)]
                earlier = sb("m_earlier", [P, 4, P], F32, inner)
                prior = sb("m_prior", [P, 4], F32, inner)
                place_f = sb("m_place_f", [P, 4], F32, inner)
                place = [sb(f"m_place{q}", [P, 4], I32, inner) for q in range(2)]
                merged = [sb(f"merged{q}", [P, 4, D], F32, inner) for q in range(2)]
                valid = sb("m_valid", [P, S], F32, inner)
                p_pre = [ps(f"p_pre{q}", [P, 4, D], F32, inner) for q in range(2)]
                p_merged = [ps(f"p_merged{q}", [P, 4, D], F32, inner) for q in range(2)]
                (m_order, loop_order, idx_ready, hot_ready, place_ready, pair_used, pre_done, pre_added, msg_ready, merge_done, out_ready,
                 places_free) = (sem("e_" + x) for x in (
                     "order", "loop_order", "idx_ready", "hot_ready", "place_ready", "pair_used", "pre_done", "pre_added", "msg_ready", "merge_done",
                     "out_ready", "places_free"))
                rows_in = [sem(f"e_rows_in{q}") for q in range(2)]
                edges_in = [sem(f"e_edges_in{q}") for q in range(2)]
                landed = [sem(f"e_landed{n}") for n in range(RS)]
                with nc.Block() as block:
                    @block.vector
                    def _(dve):
                        o = Order(dve, m_order)
                        TS, STT = nc.vector.tensor_scalar, nc.vector.scalar_tensor_tensor
                        o.did(TS(own_row[:], pidx[:], float(NP), None, ALU.add))
                        o.did(TS(valid[:], dl_step[:], 0.0, None, ALU.is_ge))
                        o.link(nc.vector.tensor_copy(msg_step[:], src_step[:]))
                        o.link(STT(valid[:], dl_step[:], float(P), valid[:], ALU.is_lt, ALU.mult))
                        o.link(TS(msg_step[:], msg_step[:], own_row[:, 0:1], None, ALU.subtract))
                        o.link(nc.vector.tensor_tensor(msg_step[:], msg_step[:], valid[:], ALU.mult))
                        TS(msg_step[:], msg_step[:], own_row[:, 0:1], None, ALU.add)

                with nc.Block() as block:
                    def groups(engine, work):
                        def pair_of(i):
                            work(i * 2, 0, i)
                            work(i * 2 + 1, 1, i)
                        looped(engine, G4 // 2 - 1, pair_of)

                    @block.sync
                    def _(sp):
                        def load_pair(i):
                            first = read_registers(nc, step_table, i * 8 + S, 8, ET.SP, (CH - 1) * P)
                            for q in range(2):
                                g = i * 2 + q
                                sp.wait_ge(pre_done, g + 1)
                                sp.wait_ge(pair_used, g + 1)
                                sp.nop().then_inc(waits_passed, 1)
                                sp.dma_start(pair[q][:].rearrange("p u n e -> p (u n e)"),
                                             pair_dram[bass.ds(g * 4, 4)].rearrange("s n e -> (s n e)").partition_broadcast(P)).then_inc(edges_in[q], 16)
                                for u in range(4):
                                    sp.dma_start(attrT[q][:, u, :], a["attr64T"][:, bass.ds(first[q * 4 + u], P)]).then_inc(edges_in[q], 16)

                        looped(sp, G4 // 2, load_pair)

                    @block.gpsimd
                    def _(pool):
                        def gather(g, q):
                            pool.wait_ge(idx_ready, g + 1)
                            pool.nop().then_inc(waits_passed, 1)
                            for u in range(4):
                                nc.gpsimd.indirect_dma_start(
                                    src_rows[q][:, u, :], None, src_dram,
                                    bass.IndirectOffsetOnAxis(ap=idx[q][:, u:u + 1].bitcast(U32), axis=0)).then_inc(rows_in[q], 16)

                        def scatter(g, q):
                            pool.wait_ge(place_ready, g + 1)
                            pool.wait_ge(out_ready, g + 3)
                            pool.nop().then_inc(waits_passed, 1)
                            for u in range(4):
                                nc.gpsimd.indirect_dma_start(
                                    sums_dram[u], bass.IndirectOffsetOnAxis(ap=place[q][:, u:u + 1].bitcast(U32), axis=0),
                                    merged[q][:, u, :], None, compute_op=ALU.add).then_inc(landed[u], 16)

                        def work(g, q, i):
                            pool.wait_ge(pre_added, g + 3)
                            gather(g + 2, q)
                            for n in range(RS):
                                pool.wait_ge(landed[n], g * 16)
                            pool.nop().then_inc(places_free, 1)
                            scatter(g, q)

                        gather(0, 0)
                        gather(1, 1)
                        pool.wait_ge(sums_zeroed, 16 * RS)
                        groups(pool, work)
                        for g, q in ((G4 - 2, 0), (G4 - 1, 1)):
                            for n in range(RS):
                                pool.wait_ge(landed[n], g * 16)
                            pool.nop().then_inc(places_free, 1)
                            scatter(g, q)
                        for n in range(RS):
                            pool.wait_ge(landed[n], G4 * 16)

                    @block.scalar
                    def _(act):
                        act.nop().then_inc(out_ready, 2)

                        def indices(g, q):
                            nc.scalar.copy(idx[q][:], src_step[:, bass.ds(g * 4, 4)]).then_inc(idx_ready, 1)

                        def finish(g, q, ahead):
                            act.wait_ge(pre_added, g + 3)
                            if ahead:
                                indices(g + 2, q)
                            nc.scalar.activation(msg[q][:], msg[q][:], ACT.Relu).then_inc(msg_ready, 1)
                            act.wait_ge(merge_done, g + 3)
                            act.wait_ge(places_free, g)
                            nc.scalar.copy(merged[q][:], p_merged[q][:]).then_inc(out_ready, 1)

                        indices(0, 0)
                        indices(1, 1)
                        groups(act, lambda g, q, i: finish(g, q, True))
                        finish(G4 - 2, 0, False)
                        finish(G4 - 1, 1, False)

                    @block.tensor
                    def _(pe):
                        pe.nop().then_inc(pre_done, 2)
                        pe.nop().then_inc(merge_done, 2)

                        def products(g, q, i, tiles):
                            pe.wait_ge(edges_in[q], i * 80 + 80)
                            pe.wait_ge(hot_ready, g + 1)
                            pe.wait_ge(pre_added, g + 1)
                            for u in range(4):
                                nc.tensor.matmul(p_pre[q][:, u, :], hotT[q][:, u, :],
                                                 dst_part[:, bass.ds(tiles[u], 1), :].rearrange("p o d -> p (o d)"), start=True, stop=False)
                                r = nc.tensor.matmul(p_pre[q][:, u, :], attrT[q][:, u, :], attr_w[:], start=False, stop=True)
                            r.then_inc(pre_done, 1)

                        def merge(g, q):
                            pe.wait_ge(msg_ready, g + 1)
                            pe.wait_ge(place_ready, g + 1)
                            pe.wait_ge(out_ready, g + 1)
                            for u in range(4):
                                r = nc.tensor.matmul(p_merged[q][:, u, :], same[q][:, u, :], msg[q][:, u, :], start=True, stop=True)
                            r.then_inc(merge_done, 1)

                        def pair_of(i):
                            tiles = read_registers(nc, step_table, i * 8 + 4, 8, ET.PE, NT - 1)
                            products(i * 2 + 1, 1, i, tiles[0:4])
                            merge(i * 2, 0)
                            products(i * 2 + 2, 0, i + 1, tiles[4:8])
                            merge(i * 2 + 1, 1)

                        products(0, 0, 0, read_registers(nc, step_table, 0, 4, ET.PE, NT - 1))
                        looped(pe, G4 // 2 - 1, pair_of)
                        products(G4 - 1, 1, G4 // 2 - 1, read_registers(nc, step_table, S - 4, 4, ET.PE, NT - 1))
                        merge(G4 - 2, 0)
                        merge(G4 - 1, 1)

                    @block.vector
                    def _(dve):
                        TT, TS = nc.vector.tensor_tensor, nc.vector.tensor_scalar
                        o = Order(dve, loop_order)
                        dve.nop().then_inc(pair_used, 2)
                        dve.nop().then_inc(pre_added, 2)
                        spread = [P, 4, P]

                        def choose(g, q, i):
                            dve.wait_ge(edges_in[q], i * 80 + 80)
                            dve.wait_ge(pre_done, g + 1)
                            TS(hotT[q][:], pair[q][:, :, 0, :], pidx[:, 0:1], None, ALU.is_equal).then_inc(hot_ready, 1)
                            here = msg_step[:, bass.ds(g * 4, 4)]
                            dve.wait_ge(merge_done, g + 1)
                            o.link(TT(same[q][:], pair[q][:, :, 1, :], here.unsqueeze(2).broadcast_to(spread), ALU.is_equal))
                            dve.nop().then_inc(pair_used, 1)
                            o.link(TT(earlier[:], same[q][:], lower[:].unsqueeze(1).broadcast_to(spread), ALU.mult))
                            o.link(nc.vector.tensor_reduce(prior[:], earlier[:], AX.X, ALU.add))
                            o.link(TS(prior[:], prior[:], 0.5, None, ALU.is_lt))
                            o.link(TT(place_f[:], here, own_row[:].broadcast_to([P, 4]), ALU.subtract))
                            o.link(TT(place_f[:], place_f[:], prior[:], ALU.mult))

                        def choose_place(g, q):
                            dve.wait_ge(places_free, g)
                            TT(place[q][:], place_f[:], own_row[:].broadcast_to([P, 4]), ALU.add).then_inc(place_ready, 1)

                        def sum_parts(g, q, i):
                            dve.wait_ge(rows_in[q], i * 64 + 64)
                            dve.wait_ge(pre_done, g + 3)
                            dve.wait_ge(merge_done, g + 1)
                            for v in range(2):
                                k = TT(msg[q][:, 2 * v:2 * v + 2, :], src_rows[q][:, 2 * v:2 * v + 2, :], p_pre[q][:, 2 * v:2 * v + 2, :], ALU.add)
                            k.then_inc(pre_added, 1)

                        def work(g, q, i):
                            o.enter(g)
                            choose(g + 1, 1 - q, i + q)
                            sum_parts(g, q, i)
                            choose_place(g + 1, 1 - q)

                        choose(0, 0, 0)
                        choose_place(0, 0)
                        o.begin(6)
                        groups(dve, work)
                        o.leave(G4 - 2)
                        choose(G4 - 1, 1, G4 // 2 - 1)
                        sum_parts(G4 - 2, 0, G4 // 2 - 1)
                        choose_place(G4 - 1, 1)
                        sum_parts(G4 - 1, 1, G4 // 2 - 1)
            w2 = sb("m_w2", [P, 2, D], F32, ctx)
            wi = sb("m_wi", [P, 2, 3 * D], F32, ctx)
            wh = sb("m_wh", [P, 2, 3 * D], F32, ctx)
            b2 = sb("m_b2row", [P, D], F32, ctx)
            bi = sb("m_bi", [P, 3 * D], F32, ctx)
            bh = sb("m_bh", [P, 3 * D], F32, ctx)
            parts_in = [sb(f"parts_in{q}", [P, RS, D], F32, ctx) for q in range(2)]
            agg = [sb(f"u_agg{q}", [P, D], F32, ctx) for q in range(2)]
            aggT = [sb(f"u_aggT{q}", [P, 2, P], F32, ctx) for q in range(2)]
            agg2 = [sb(f"u_agg2{q}", [P, D], F32, ctx) for q in range(2)]
            agg2T = [sb(f"u_agg2T{q}", [P, 2, P], F32, ctx) for q in range(2)]
            hslot = [sb(f"u_hslot{q}", [P, 2, P], F32, ctx) for q in range(2)]
            gates = [sb(f"gates{q}", [P, 2 * D], F32, ctx) for q in range(2)]
            cand = [sb(f"cand{q}", [P, 2 * D], F32, ctx) for q in range(2)]
            p_t = [ps(f"u_p_t{q}", [P, 2, P], F32, ctx) for q in range(2)]
            p_2 = [ps(f"u_p_2{q}", [P, D], F32, ctx) for q in range(2)]
            p_rz = [ps(f"u_p_rz{q}", [P, 2 * D], F32, ctx) for q in range(2)]
            p_n = [ps(f"u_p_n{q}", [P, 2 * D], F32, ctx) for q in range(2)]
            (u_in, u_order, bias_ready, agg_ready, turns, copies, second, agg2_ready, slot_ready, gates_ps, rz_ready, rz_done, tanh_in,
             tanh_done, rows_ready, parts_free) = (sem("u_" + x) for x in (
                 "in", "order", "bias_ready", "agg_ready", "turns", "copies", "second", "agg2_ready", "slot_ready", "gates_ps", "rz_ready",
                 "rz_done", "tanh_in", "tanh_done", "rows_ready", "parts_free"))
            u_parts = [sem(f"u_parts{q}") for q in range(2)]
            stored = sem("stored")

            def each_tile(engine, work):
                def tiles_of(i):
                    for q in range(2):
                        work(i * 2 + q, q, i)
                looped(engine, NT // 2, tiles_of)
                work(NT - 1, 0, NT // 2)

            with nc.Block() as block:
                @block.sync
                def _(sp):
                    sp.dma_start(w2[:], a["m_W2T"].rearrange("(k p) d -> p k d", k=2)).then_inc(u_in, 16)
                    sp.dma_start(wi[:], a["m_W_ihT"].rearrange("(k p) d -> p k d", k=2)).then_inc(u_in, 16)
                    sp.dma_start(wh[:], a["m_W_hhT"].rearrange("(k p) d -> p k d", k=2)).then_inc(u_in, 16)
                    for name, row in (("m_b2", b2), ("m_b_ih", bi), ("m_b_hh", bh)):
                        sp.dma_start(row[:], a[name].partition_broadcast(P)).then_inc(u_in, 16)

                    def load(t, q, i):
                        sp.wait_ge(parts_free, t)
                        sp.nop().then_inc(waits_passed, 1)
                        for n in range(RS):
                            sp.dma_start(parts_in[q][:, n, :], sums_dram[n][bass.ds(t * P, P), :]).then_inc(u_parts[q], 16)

                    each_tile(sp, load)

                @block.gpsimd
                def _(pool):
                    def store(t, q, i):
                        pool.wait_ge(rows_ready, t + 1)
                        pool.nop().then_inc(waits_passed, 1)
                        pool.dma_start(out[bass.ds(t * P, P), :], x_sb[:, bass.ds(t, 1), :].rearrange("p o d -> p (o d)")).then_inc(stored, 16)

                    with pool.Fori(0, NT - 1) as t:
                        store(t, 0, 0)
                    pool.wait_ge(rows_ready, NT)
                    pool.dma_start(out[(NT - 1) * P:N, :], x_sb[0:N - (NT - 1) * P, NT - 1, :]).then_inc(stored, 16)
                    pool.wait_ge(stored, 16 * NT)

                @block.tensor
                def _(pe):
                    pe.wait_ge(u_in, 96)

                    def work(t, q, i):
                        pe.wait_ge(agg_ready, t + 1)
                        pe.wait_ge(copies, t * 2)
                        for m in range(2):
                            r = nc.tensor.transpose(p_t[0][:, m, :], agg[q][:, m * P:(m + 1) * P], ident[:])
                        r.then_inc(turns, 1)
                        pe.wait_ge(slot_ready, t + 1)
                        pe.wait_ge(rz_ready, t)
                        pe.wait_ge(tanh_in, t)
                        for k in range(2):
                            nc.tensor.matmul(p_rz[q][:], hslot[q][:, k, :], wh[:, k, 0:2 * D], start=(k == 0), stop=False)
                        for k in range(2):
                            nc.tensor.matmul(p_n[q][:, D:], hslot[q][:, k, :], wh[:, k, 2 * D:], start=(k == 0), stop=(k == 1))
                        pe.wait_ge(copies, t * 2 + 1)
                        pe.wait_ge(agg2_ready, t)
                        for k in range(2):
                            r = nc.tensor.matmul(p_2[q][:], aggT[q][:, k, :], w2[:, k, :], start=(k == 0), stop=(k == 1))
                        r.then_inc(second, 1)
                        pe.wait_ge(agg2_ready, t + 2)
                        for m in range(2):
                            r = nc.tensor.transpose(p_t[1][:, m, :], agg2[q][:, m * P:(m + 1) * P], ident[:])
                        r.then_inc(turns, 1)
                        pe.wait_ge(copies, t * 2 + 2)
                        for k in range(2):
                            nc.tensor.matmul(p_rz[q][:], agg2T[q][:, k, :], wi[:, k, 0:2 * D], start=False, stop=(k == 1))
                        for k in range(2):
                            r = nc.tensor.matmul(p_n[q][:, 0:D], agg2T[q][:, k, :], wi[:, k, 2 * D:], start=(k == 0), stop=(k == 1))
                        r.then_inc(gates_ps, 1)

                    each_tile(pe, work)

                @block.scalar
                def _(act):
                    act.nop().then_inc(gates_ps, 1)

                    def work(t, q, i):
                        act.wait_ge(gates_ps, t)
                        nc.scalar.copy(hslot[q][:], h3T[:, :, bass.ds(t * P, P)]).then_inc(slot_ready, 1)
                        act.wait_ge(turns, t * 2 + 1)
                        nc.scalar.copy(aggT[q][:], p_t[0][:]).then_inc(copies, 1)
                        act.wait_ge(turns, t * 2 + 2)
                        nc.scalar.copy(agg2T[q][:], p_t[1][:]).then_inc(copies, 1)
                        act.wait_ge(rz_ready, t + 2)
                        nc.scalar.activation(gates[q][:], gates[q][:], ACT.Sigmoid).then_inc(rz_done, 1)
                        act.wait_ge(tanh_in, t + 2)
                        nc.scalar.activation(cand[q][:, 0:D], cand[q][:, 0:D], ACT.Tanh).then_inc(tanh_done, 1)

                    each_tile(act, work)

                @block.vector
                def _(dve):
                    TT, STT = nc.vector.tensor_tensor, nc.vector.scalar_tensor_tensor
                    o = Order(dve, u_order)
                    for s in (parts_free, agg2_ready, rz_ready, tanh_in):
                        dve.nop().then_inc(s, 1)
                    dve.wait_ge(u_in, 96)
                    o.link(TT(bh[:, 0:2 * D], bh[:, 0:2 * D], bi[:, 0:2 * D], ALU.add))

                    def work(t, q, i):
                        o.enter(t)
                        dve.wait_ge(u_parts[q], i * (16 * RS) + 16 * RS)
                        o.link(TT(parts_in[q][:, 0:2, :], parts_in[q][:, 0:2, :], parts_in[q][:, 2:4, :], ALU.add))
                        TT(agg[q][:], parts_in[q][:, 0, :], parts_in[q][:, 1, :], ALU.add).then_inc(agg_ready, 1)
                        dve.wait_ge(agg_ready, t + 1)
                        dve.nop().then_inc(parts_free, 1)
                        dve.wait_ge(second, t + 1)
                        STT(agg2[q][:], b2[:], column(degsrc, t), p_2[q][:], ALU.mult, ALU.add).then_inc(agg2_ready, 1)
                        dve.wait_ge(gates_ps, t + 2)
                        TT(gates[q][:], p_rz[q][:], bh[:, 0:2 * D], ALU.add).then_inc(rz_ready, 1)
                        TT(cand[q][:, 0:D], p_n[q][:, 0:D], bi[:, 2 * D:], ALU.add)
                        o.link(TT(cand[q][:, D:], p_n[q][:, D:], bh[:, 2 * D:], ALU.add))
                        dve.wait_ge(rz_done, t + 1)
                        o.link(TT(cand[q][:, D:], cand[q][:, D:], gates[q][:, 0:D], ALU.mult))
                        TT(cand[q][:, 0:D], cand[q][:, 0:D], cand[q][:, D:], ALU.add).then_inc(tanh_in, 1)
                        dve.wait_ge(tanh_done, t + 1)
                        own = x_sb[:, bass.ds(t, 1), :].rearrange("p o d -> p (o d)")
                        o.did(TT(own, own, cand[q][:, 0:D], ALU.add))
                        o.link(TT(cand[q][:, D:], h3[:, bass.ds(t, 1), :].rearrange("p o d -> p (o d)"), cand[q][:, 0:D], ALU.subtract))
                        o.link(TT(cand[q][:, D:], cand[q][:, D:], gates[q][:, D:], ALU.mult))
                        TT(own, own, cand[q][:, D:], ALU.add).then_inc(rows_ready, 1)

                    o.begin(6)
                    each_tile(dve, work)
                    o.leave(NT)


NAMES = {
    "gamma": "L0_gnn_gamma", "beta": "L0_gnn_beta", "W1": "L0_gnn_W1", "a_src1": "L0_gnn_a_src1", "a_dst1": "L0_gnn_a_dst1",
    "b1": "L0_gnn_b1", "W2": "L0_gnn_W2", "a_src2": "L0_gnn_a_src2", "a_dst2": "L0_gnn_a_dst2", "b2": "L0_gnn_b2",
    "Wu": "L0_gnn_Wu", "bu": "L0_gnn_bu",
    "mlp_w": "L1_gnn_mlp_w", "mlp_b": "L1_gnn_mlp_b", "ew1": "L1_gnn_ew1", "ew2": "L1_gnn_ew2", "bn_g": "L1_gnn_bn_g", "bn_b": "L1_gnn_bn_b",
    "L2_W": "L2_gnn_W", "L2_b": "L2_gnn_b",
    "m_b1": "L3_gnn_b1", "m_b2": "L3_gnn_b2", "m_b_ih": "L3_gnn_b_ih", "m_b_hh": "L3_gnn_b_hh",
}
TURNED = {"m_W1T": "L3_gnn_W1", "m_W2T": "L3_gnn_W2", "m_W_ihT": "L3_gnn_W_ih", "m_W_hhT": "L3_gnn_W_hh"}


def kernel(**inputs):
    import concourse.bacc as bacc
    from concourse.bass_utils import run_bass_kernel_spmd

    given = {name: np.asarray(value) for name, value in inputs.items()}

    def padded(array, rows, fill=0):
        whole = np.full((rows,) + array.shape[1:], fill, array.dtype)
        whole[:array.shape[0]] = array
        return whole

    arrays = {
        "x": padded(given["x"], NP),
        "src": padded(given["src"], EP),
        "dst": padded(given["dst"], EP, PADDST),
        "attr4": padded(given["edge_attr_4"], EP),
        "attr64T": np.ascontiguousarray(padded(given["edge_attr_64"], EP).T),
    }
    arrays.update({short: np.ascontiguousarray(given[name]) for short, name in NAMES.items()})
    arrays.update({short: np.ascontiguousarray(given[name].T) for short, name in TURNED.items()})

    nc = bacc.Bacc("TRN2", target_bir_lowering=False, num_devices=1)
    a = {name: nc.dram_tensor("in_" + name, array.shape, mybir.dt.from_np(array.dtype), kind="ExternalInput").ap()
         for name, array in arrays.items()}
    out = nc.dram_tensor("out", [N, D], F32, kind="ExternalOutput").ap()
    program(nc, a, out)
    result = run_bass_kernel_spmd(nc, [{"in_" + name: array for name, array in arrays.items()}], core_ids=[0])
    return result.results[0]["out"]
```

```python
from contextlib import ExitStack

import numpy as np
import concourse.bass as bass
from concourse import mybir

F32 = mybir.dt.float32
F16 = mybir.dt.float16
BF16 = mybir.dt.bfloat16
I32 = mybir.dt.int32
U32 = mybir.dt.uint32
ALU = mybir.AluOpType
ACT = mybir.ActivationFunctionType
AX = mybir.AxisListType
ET = mybir.EngineType

P = 128
N = 3125
NT = -(-N // P)
NP = NT * P
D = 256
E = 53125
CH = -(-E // P)
EP = CH * P
GR = 110
NB = 4
S = GR * NB
assert S >= CH + NT - 1
HJ = 425
HP = E // HJ
HB = 17
HW = 16
HD = 512
ROW = HD + HW
SROW = 20
KD = NP * NP
ZF = 2000
PLAN_CHUNKS = 15
RS = 4
ED = 64
PADDST = 4095
BIG = 1.0e30
EPS = 1e-5
LAYERS = 5
W = 400
NC = NP // W
assert NC * W == NP and NC % 2 == 0
PIECES = (NP + P) // P // 2
PT = 5
LAG = 3
HALF = NP // 2
LO = 2048.0
assert HP * HJ == E and HJ % HB == 0


class Order:

    def __init__(self, engine, semaphore):
        self.engine, self.semaphore, self.base, self.n = engine, semaphore, 0, 0

    def did(self, instruction):
        instruction.then_inc(self.semaphore, 1)
        self.n += 1
        return self.n

    def need(self, n):
        self.engine.wait_ge(self.semaphore, self.base + n)

    def link(self, instruction):
        self.need(self.did(instruction))

    def begin(self, per, first=0):
        self.start, self.per = self.base + self.n - first * per, per

    def enter(self, i):
        self.base, self.n = self.start + i * self.per, 0

    def leave(self, rounds):
        assert self.n == self.per, (self.n, self.per)
        self.base, self.n = self.start + rounds * self.per, 0


def looped(engine, rounds, work):
    work(0)
    with engine.Fori(1, rounds) as i:
        work(i)


def column(ap, k):
    return ap[:, bass.ds(k, 1)]


def read_registers(nc, table, at, count, engine, top):
    _, values = nc.values_load_multi_w_load_instructions(
        table[0:1, bass.ds(at, count)], engines=[engine], min_val=0, max_val=top,
        skip_runtime_bounds_check_because="the table is clamped to this range when it is made")
    return values


def program(nc, a, out):
    top = ExitStack()
    with top:
        def sb(name, shape, dt, ctx=top):
            return ctx.enter_context(nc.sbuf_tensor(name, shape, dt))

        def ps(name, shape, dt, ctx):
            return ctx.enter_context(nc.psum_tensor(name, shape, dt))

        def sem(name, over_stages=False):
            handle = nc.alloc_semaphore(name=name)
            (lasting if over_stages else of_stage).append(handle)
            return handle

        def end_stage():
            nc.clear_and_free_semaphores(of_stage)
            of_stage.clear()
            nc.all_engine_barrier()


        def is_first(j):
            return isinstance(j, int) and j == 0

        def dram(name, shape, dt):
            return nc.dram_tensor(name, shape, dt, kind="Internal").ap()

        lasting, of_stage = [], []
        top.enter_context(nc.allow_non_contiguous_dma(reason="small tables and columns, once"))
        x_sb = sb("x_sb", [P, NT, D], F32)
        iota_row = sb("iota_row", [P, P], F32)
        pidx = sb("pidx", [P, 1], F32)
        ident = sb("ident", [P, P], F32)
        ident16 = sb("ident16", [P, P], F16)
        lower = sb("lower", [P, P], F32)
        ones = sb("ones", [P, P], F32)
        deg = sb("deg", [P, NT], F32)
        dinv = sb("dinv", [P, NT], F32)
        step_table = sb("step_table", [1, 2 * S], I32)
        src_step = sb("src_step", [P, S], I32)
        dl_step = sb("dl_step", [P, S], F32)
        F_sb = sb("F_sb", [P, NT, 4], F32)
        degsrc = sb("degsrc", [P, NT], F32)
        rstd = sb("rstd", [P, NT], F32)
        shift = sb("shift", [P, NT], F32)
        stats = sb("stats", [P, NT, 6], F32)
        norm_small = sb("norm_small", [P, 5, NT], F32)
        tab = sb("tab", [P, NT, 2 * HW], F32)
        early = top.enter_context(ExitStack())
        zeros = sb("zeros", [P, ZF], F32, early)
        waits_passed = sem("waits_passed", True)
        key_step = sb("key_step", [P, S], F32, early)
        last_step = sb("last_step", [P, S], F32, early)
        attr4_step = sb("attr4_step", [P, S, 4], F32, early)
        self_s = sb("self_s", [P, NT, HW], F32, early)

        step_dram = dram("step_dram", [2 * S], I32)
        pen_dram = dram("pen_dram", [S * P], F32)
        key_dram = dram("key_dram", [S * P], F32)
        pair_dram = dram("pair_dram", [S, 2, P], F32)
        sums_dram = [dram(f"sums_dram{n}", [NP + P, D], F32) for n in range(RS)]
        seg_dram = dram("seg_dram", [S * P + 2], F32)
        att_dram = dram("att_dram", [NP, ROW], F32)
        score_dram = dram("score_dram", [NP, SROW], F32)
        count_dram = dram("count_dram", [KD + P, 1], F32)
        by_src = dram("by_src", [NP, NP], F16)

        with ExitStack() as ctx:
            iota_i = sb("iota_i", [P, P], I32, ctx)
            pidx_i = sb("pidx_i", [P, 1], I32, ctx)
            dst_i = sb("dst_i", [HP, HJ], I32, ctx)
            lo_i = sb("lo_i", [HP, HJ], I32, ctx)
            hi_i = sb("hi_i", [HP, HJ], I32, ctx)
            lo_f = sb("lo_f", [HP, HJ], BF16, ctx)
            hi_f = sb("hi_f", [HP, HJ], BF16, ctx)
            iota_bf = sb("iota_bf", [P, P], BF16, ctx)
            lo_hot = sb("lo_hot", [HP, 2, HB, P], BF16, ctx)
            hi_hot = sb("hi_hot", [HP, 2, HB, NT], BF16, ctx)
            hist = ps("hist", [P, NT], F32, ctx)
            dst_in, x_in, iota_made = sem("dst_in"), sem("x_in"), sem("iota_made")
            count_order, hots_ready, hots_used = sem("count_order"), sem("hots_ready"), sem("hots_used")
            zeros_ready, zeros_out, hist_zero = sem("zeros_ready"), sem("zeros_out", True), sem("hist_zero")
            NZ = KD // (P * ZF)
            with nc.Block() as block:
                @block.sync
                def _(sp):
                    sp.dma_start(dst_i[:], a["dst"][0:E].rearrange("(p j) -> p j", p=HP)).then_inc(dst_in, 16)
                    sp.dma_start(x_sb[:], a["x"].rearrange("(t p) d -> p t d", p=P)).then_inc(x_in, 16)
                    sp.wait_ge(zeros_ready, 1)
                    whole = count_dram[0:KD, :].rearrange("(z p f) o -> z p (f o)", z=NZ, p=P)
                    with sp.Fori(0, NZ) as z:
                        sp.dma_start(whole[bass.ds(z, 1)].rearrange("z p f -> (z p) f"), zeros[:]).then_inc(zeros_out, 16)
                    sp.dma_start(count_dram[KD:KD + P, :], zeros[:, 0:1]).then_inc(zeros_out, 16)
                    sp.wait_ge(x_in, 16)

                @block.gpsimd
                def _(pool):
                    nc.gpsimd.memset(zeros[:], 0.0).then_inc(zeros_ready, 1)
                    nc.gpsimd.iota(iota_i[:], pattern=[[1, P]], base=0, channel_multiplier=0).then_inc(iota_made, 1)
                    nc.gpsimd.iota(pidx_i[:], pattern=[[0, 1]], base=0, channel_multiplier=1).then_inc(iota_made, 1)

                @block.vector
                def _(dve):
                    o = Order(dve, count_order)
                    nc.vector.memset(hist[:], 0.0).then_inc(hist_zero, 1)
                    dve.wait_ge(iota_made, 2)
                    o.did(nc.vector.tensor_copy(iota_row[:], iota_i[:]))
                    o.did(nc.vector.tensor_copy(iota_bf[:], iota_i[:]))
                    o.did(nc.vector.memset(ones[:], 1.0))
                    o.link(nc.vector.tensor_copy(pidx[:], pidx_i[:]))
                    o.did(nc.vector.tensor_scalar(ident[:], iota_row[:], pidx[:, 0:1], None, ALU.is_equal))
                    o.did(nc.vector.tensor_scalar(ident16[:], iota_row[:], pidx[:, 0:1], None, ALU.is_equal))
                    o.did(nc.vector.tensor_scalar(lower[:], iota_row[:], pidx[:, 0:1], None, ALU.is_lt))
                    dve.wait_ge(dst_in, 16)
                    o.did(nc.vector.tensor_scalar(lo_i[:], dst_i[:], P - 1, None, ALU.bitwise_and))
                    o.link(nc.vector.tensor_scalar(hi_i[:], dst_i[:], 7, None, ALU.logical_shift_right))
                    o.did(nc.vector.tensor_copy(lo_f[:], lo_i[:]))
                    o.link(nc.vector.tensor_copy(hi_f[:], hi_i[:]))
                    with dve.Fori(0, HJ // HB) as b:
                        with_slot = bass.ds(b % 2, 1)
                        dve.wait_ge(hots_used, b + 1)
                        nc.vector.tensor_tensor(
                            lo_hot[:, with_slot].rearrange("p o j n -> p (o j) n"),
                            iota_bf[0:HP].unsqueeze(1).broadcast_to([HP, HB, P]),
                            lo_f[:, bass.ds(b * HB, HB)].unsqueeze(2).broadcast_to([HP, HB, P]), ALU.is_equal)
                        nc.vector.tensor_tensor(
                            hi_hot[:, with_slot].rearrange("p o j n -> p (o j) n"),
                            iota_bf[0:HP, 0:NT].unsqueeze(1).broadcast_to([HP, HB, NT]),
                            hi_f[:, bass.ds(b * HB, HB)].unsqueeze(2).broadcast_to([HP, HB, NT]),
                            ALU.is_equal).then_inc(hots_ready, 1)
                    dve.wait_ge(hots_used, HJ // HB + 2)
                    nc.vector.tensor_copy(deg[:], hist[:])

                @block.tensor
                def _(pe):
                    pe.wait_ge(hist_zero, 1)
                    pe.nop().then_inc(hots_used, 2)
                    with pe.Fori(0, HJ // HB) as b:
                        pe.wait_ge(hots_ready, b + 1)
                        for j in range(HB):
                            last = nc.tensor.matmul(
                                hist[:], lo_hot[:, bass.ds(b % 2, 1), j, :].rearrange("p o n -> p (o n)"),
                                hi_hot[:, bass.ds(b % 2, 1), j, :].rearrange("p o n -> p (o n)"),
                                start=False, stop=True, skip_group_check=True)
                        last.then_inc(hots_used, 1)

        def norm_vector(dve, name, source):
            order, var_ready, root_ready, scales_ready = (sem(name + x) for x in ("_order", "_var_ready", "_root_ready", "_scales_ready"))
            mean, diff, var, root, half = (norm_small[:, i, :] for i in range(5))
            o = Order(dve, order)
            o.begin(1)
            with dve.Fori(0, NT // 5) as i:
                o.enter(i)
                for u in range(5):
                    t = i * 5 + u
                    k = nc.vector.bn_stats(stats[:, bass.ds(t, 1), :].rearrange("p o s -> p (o s)"),
                                           source[:, bass.ds(t, 1), :].rearrange("p o d -> p (o d)"))
                o.did(k)
            o.leave(NT // 5)
            o.need(o.n)
            o.did(nc.vector.tensor_tensor(mean, stats[:, :, 1], stats[:, :, 4], ALU.add))
            o.did(nc.vector.tensor_tensor(diff, stats[:, :, 1], stats[:, :, 4], ALU.subtract))
            o.link(nc.vector.tensor_tensor(var, stats[:, :, 2], stats[:, :, 5], ALU.add))
            o.did(nc.vector.tensor_scalar(mean, mean, 0.5, None, ALU.mult))
            o.did(nc.vector.tensor_scalar(var, var, 1.0 / D, EPS, ALU.mult, ALU.add))
            o.link(nc.vector.tensor_tensor(half, diff, diff, ALU.mult))
            o.link(nc.vector.scalar_tensor_tensor(var, half, 0.25, var, ALU.mult, ALU.add))
            dve.nop().then_inc(var_ready, 1)
            dve.wait_ge(root_ready, 1)
            o.link(nc.vector.reciprocal(rstd[:], root))
            o.link(nc.vector.scalar_tensor_tensor(shift[:], mean, -1.0, rstd[:], ALU.mult, ALU.mult))
            dve.nop().then_inc(scales_ready, 1)
            return var_ready, root_ready, scales_ready

        def norm_root(act, var_ready, root_ready, scales_ready):
            act.wait_ge(var_ready, 1)
            nc.scalar.activation(norm_small[:, 3, :], norm_small[:, 2, :], ACT.Sqrt).then_inc(root_ready, 1)
            act.wait_ge(scales_ready, 1)

        def norm_scales(name, source):
            with nc.Block() as block:
                made = []

                @block.vector
                def _(dve):
                    made.extend(norm_vector(dve, name, source))

                @block.scalar
                def _(act):
                    norm_root(act, *made)

        def apply_tiles(source, target, ready):
            for t in range(NT):
                nc.scalar.activation(target[:, t, :], source[:, t, :], ACT.Relu, bias=shift[:, t:t + 1], scale=rstd[:, t:t + 1]).then_inc(ready, 1)

        with_h0 = top.enter_context(ExitStack())
        h0 = sb("h0", [P, NT, D], F32, with_h0)
        h0_ready = sem("h0_ready")
        with ExitStack() as ctx:
            col = sb("col", [NT, 8], F32, ctx)
            col_i = sb("col_i", [NT, 4], I32, ctx)
            chunks_bc = sb("chunks_bc", [NT, P], F32, ctx)
            first_bc = sb("first_bc", [NT, P], F32, ctx)
            tri_ex = sb("tri_ex", [NT, NT], F32, ctx)
            tri_in = sb("tri_in", [NT, NT], F32, ctx)
            base_row = sb("base_row", [GR, NT], F32, ctx)
            incl_row = sb("incl_row", [GR, NT], F32, ctx)
            step_i = sb("step_i", [GR, NB], I32, ctx)
            step_f = sb("step_f", [GR, NB], F32, ctx)
            sel = sb("sel", [GR, NB, NT], F32, ctx)
            tile_f = sb("tile_f", [GR, NB], F32, ctx)
            tile_c = sb("tile_c", [GR, NB], F32, ctx)
            chunk_f = sb("chunk_f", [GR, NB], F32, ctx)
            chunk_i = sb("chunk_i", [GR, NB], I32, ctx)
            table_i = sb("table_i", [GR, 2, NB], I32, ctx)
            srcrow = sb("srcrow", [GR, NB, P], I32, ctx)
            dstrow = sb("dstrow", [GR, NB, P], I32, ctx)
            attrrow = sb("attrrow", [GR, NB, P, 4], F32, ctx)
            src_f = sb("src_f", [GR, NB, P], F32, ctx)
            dl_row = sb("dl_row", [GR, NB, P], F32, ctx)
            seg_row = sb("seg_row", [GR, NB, P], F32, ctx)
            key_row = sb("key_row", [GR, NB, P], F32, ctx)
            v1 = sb("v1", [GR, NB, P], F32, ctx)
            v2 = sb("v2", [GR, NB, P], F32, ctx)
            before = sb("before", [GR, NB, P], F32, ctx)
            after = sb("after", [GR, NB, P], F32, ctx)
            last_row = sb("last_row", [GR, NB, P], F32, ctx)
            msg_row = sb("msg_row", [GR, NB, P], F32, ctx)
            ends = sb("ends", [1, 2], F32, ctx)
            tile_off = sb("tile_off", [GR, NB], F32, ctx)
            few = ps("few", [P, 512], F32, ctx)
            turned = [ps(f"turned{i}", [P, 512], F32, ctx) for i in range(4)]
            plan = sem("plan")
            pe_few, rows_in, table_out, table_in = sem("pe_few"), sem("rows_in"), sem("table_out"), sem("table_in")
            seg_out, seg_in, pen_out, turned_ready, turned_used = (
                sem("seg_out"), sem("seg_in"), sem("pen_out"), sem("turned_ready"), sem("turned_used"))
            steps_made = sem("steps_made")
            row_ready = sem("row_ready")
            COUNT, START, END, CHUNKS, FIRST, SOME = range(6)
            norms = []
            with nc.Block() as block:
                @block.gpsimd
                def _(pool):
                    nc.gpsimd.iota(step_i[:], pattern=[[GR, NB]], base=0, channel_multiplier=1).then_inc(steps_made, 1)
                    pool.wait_ge(row_ready, 1)
                    for b in range(NB):
                        for rows, name in ((srcrow[:, b, :], "src"), (dstrow[:, b, :], "dst"),
                                           (attrrow[:, b].rearrange("p e c -> p (e c)"), "attr4")):
                            table = a[name].rearrange("(c e) -> c e", c=CH) if name != "attr4" else \
                                a[name].rearrange("(c e) f -> c (e f)", c=CH)
                            nc.gpsimd.indirect_dma_start(
                                rows, None, table, bass.IndirectOffsetOnAxis(ap=chunk_i[:, b:b + 1].bitcast(U32), axis=0)
                            ).then_inc(rows_in, 16)

                @block.tensor
                def _(pe):
                    nc.tensor.matmul(few[0:NT, 0:1], deg[:], ones[:, 0:1], start=True, stop=True).then_inc(pe_few, 1)
                    pe.wait_ge(plan, 3)
                    nc.tensor.matmul(few[0:NT, 1:2], tri_ex[:], col[:, COUNT:COUNT + 1], start=True, stop=True).then_inc(pe_few, 1)
                    pe.wait_ge(plan, PLAN_CHUNKS)
                    nc.tensor.matmul(few[0:GR, 32:32 + NT], chunks_bc[:, 0:GR], tri_in[:], start=True, stop=True)
                    nc.tensor.matmul(few[0:GR, 64:64 + NT], chunks_bc[:, 0:GR], tri_ex[:], start=True, stop=True)
                    nc.tensor.matmul(few[0:GR, 96:96 + NT], first_bc[:, 0:GR], ident[0:NT, 0:NT], start=True, stop=True).then_inc(pe_few, 1)
                    n = 0
                    for what, rows in (("src", src_f), ("dl", dl_row), ("key", key_row), ("last", last_row)):
                        pe.wait_ge(row_ready, 2 + n)
                        for b in range(NB):
                            t = nc.tensor.transpose(turned[n % 4][:, b * GR:(b + 1) * GR], rows[:, b, :], ident[0:GR, 0:GR])
                        t.then_inc(turned_ready, 1)
                        n += 1
                    for c in range(4):
                        pe.wait_ge(turned_used, n - 3)
                        for b in range(NB):
                            t = nc.tensor.transpose(turned[n % 4][:, b * GR:(b + 1) * GR], attrrow[:, b, :, c], ident[0:GR, 0:GR])
                        t.then_inc(turned_ready, 1)
                        n += 1

                @block.sync
                def _(sp):
                    sp.wait_ge(row_ready, 1)
                    for r in range(2):
                        sp.dma_start(step_dram[r * S:(r + 1) * S].rearrange("(b p) -> p b", b=NB), table_i[:, r, :]).then_inc(table_out, 16)
                    sp.wait_ge(table_out, 32)
                    sp.dma_start(step_table[:], step_dram.rearrange("(o s) -> o s", o=1)).then_inc(table_in, 16)
                    sp.wait_ge(row_ready, 4)
                    sp.dma_start(seg_dram[1:S * P + 1].rearrange("(b p e) -> p b e", b=NB, p=GR), seg_row[:]).then_inc(seg_out, 16)
                    sp.dma_start(seg_dram[0:1].rearrange("(o s) -> o s", o=1), ends[:, 0:1]).then_inc(seg_out, 16)
                    sp.dma_start(seg_dram[S * P + 1:S * P + 2].rearrange("(o s) -> o s", o=1), ends[:, 1:2]).then_inc(seg_out, 16)
                    sp.wait_ge(seg_out, 48)
                    sp.dma_start(before[:], seg_dram[0:S * P].rearrange("(b p e) -> p b e", b=NB, p=GR)).then_inc(seg_in, 16)
                    sp.dma_start(after[:], seg_dram[2:S * P + 2].rearrange("(b p e) -> p b e", b=NB, p=GR)).then_inc(seg_in, 16)
                    sp.dma_start(key_dram.rearrange("(b p e) -> p b e", b=NB, p=GR), key_row[:]).then_inc(pen_out, 16)
                    sp.wait_ge(row_ready, 5)
                    sp.dma_start(pen_dram.rearrange("(b p e) -> p b e", b=NB, p=GR), v1[:]).then_inc(pen_out, 16)
                    for n, rows in enumerate((dl_row, msg_row)):
                        sp.dma_start(pair_dram.rearrange("(b p) n e -> n p b e", b=NB)[n], rows[:]).then_inc(pen_out, 16)
                    sp.wait_ge(pen_out, 64)
                    sp.wait_ge(table_in, 16)

                @block.vector
                def _(dve):
                    o = Order(dve, plan)
                    TT, TS = nc.vector.tensor_tensor, nc.vector.tensor_scalar
                    o.did(TS(tri_ex[:], iota_row[0:NT, 0:NT], pidx[0:NT, 0:1], None, ALU.is_gt))
                    o.did(TS(tri_in[:], iota_row[0:NT, 0:NT], pidx[0:NT, 0:1], None, ALU.is_ge))
                    dve.wait_ge(pe_few, 1)
                    o.link(nc.vector.tensor_copy(col[:, COUNT:COUNT + 1], few[0:NT, 0:1]))
                    dve.wait_ge(pe_few, 2)
                    o.did(nc.vector.tensor_copy(col_i[:, 0:1], few[0:NT, 1:2]))
                    o.link(nc.vector.tensor_copy(col[:, START:START + 1], few[0:NT, 1:2]))
                    o.did(TS(col[:, SOME:SOME + 1], col[:, COUNT:COUNT + 1], 0.5, None, ALU.is_ge))
                    o.link(TT(col[:, END:END + 1], col[:, START:START + 1], col[:, COUNT:COUNT + 1], ALU.add))
                    o.link(TS(col[:, END:END + 1], col[:, END:END + 1], -1.0, 0.0, ALU.add, ALU.max))
                    o.link(nc.vector.tensor_copy(col_i[:, 1:2], col[:, END:END + 1]))
                    o.link(TS(col_i[:, 2:4], col_i[:, 0:2], 7, None, ALU.logical_shift_right))
                    o.link(nc.vector.tensor_copy(col[:, 6:8], col_i[:, 2:4]))
                    o.did(TS(first_bc[:], ones[0:NT, :], col[:, 6:7], None, ALU.mult))
                    o.link(TT(col[:, CHUNKS:CHUNKS + 1], col[:, 7:8], col[:, 6:7], ALU.subtract))
                    o.link(TS(col[:, CHUNKS:CHUNKS + 1], col[:, CHUNKS:CHUNKS + 1], 1.0, col[:, SOME:SOME + 1], ALU.add, ALU.mult))
                    o.link(TS(chunks_bc[:], ones[0:NT, :], col[:, CHUNKS:CHUNKS + 1], None, ALU.mult))
                    assert o.n == PLAN_CHUNKS
                    dve.wait_ge(steps_made, 1)
                    o.did(nc.vector.tensor_copy(step_f[:], step_i[:]))
                    dve.wait_ge(pe_few, 3)
                    o.did(nc.vector.tensor_copy(incl_row[:], few[0:GR, 32:32 + NT]))
                    o.link(nc.vector.tensor_copy(base_row[:], few[0:GR, 96:96 + NT]))
                    o.link(TT(base_row[:], base_row[:], few[0:GR, 64:64 + NT], ALU.subtract))
                    spread = [GR, NB, NT]
                    o.link(TT(sel[:], step_f[:].unsqueeze(2).broadcast_to(spread), incl_row[:].unsqueeze(1).broadcast_to(spread), ALU.is_ge))
                    o.link(nc.vector.tensor_reduce(tile_f[:], sel[:], AX.X, ALU.add))
                    o.link(TT(sel[:], iota_row[0:GR, 0:NT].unsqueeze(1).broadcast_to(spread), tile_f[:].unsqueeze(2).broadcast_to(spread), ALU.is_equal))
                    o.link(TT(sel[:], sel[:], base_row[:].unsqueeze(1).broadcast_to(spread), ALU.mult))
                    o.link(nc.vector.tensor_reduce(chunk_f[:], sel[:], AX.X, ALU.add))
                    o.link(TT(chunk_f[:], chunk_f[:], step_f[:], ALU.add))
                    o.link(TS(chunk_f[:], chunk_f[:], float(CH - 1), None, ALU.min))
                    o.did(TS(tile_c[:], tile_f[:], float(NT - 1), None, ALU.min))
                    o.did(TS(tile_off[:], tile_f[:], float(P), None, ALU.mult))
                    o.link(nc.vector.tensor_copy(chunk_i[:], chunk_f[:]))
                    o.did(nc.vector.tensor_copy(table_i[:, 0, :], tile_c[:]))
                    o.link(TS(table_i[:, 1, :], chunk_f[:], float(P), None, ALU.mult))
                    dve.nop().then_inc(row_ready, 1)
                    norms.append(norm_vector(dve, "n0", x_sb))
                    dve.wait_ge(h0_ready, NT)
                    norms.append(norm_vector(dve, "n1", h0))
                    dve.wait_ge(rows_in, 16 * 3 * NB)
                    flat = [GR, NB, P]
                    o.did(nc.vector.tensor_copy(src_f[:], srcrow[:]))
                    o.link(nc.vector.tensor_copy(seg_row[:], dstrow[:]))
                    o.link(TT(dl_row[:], seg_row[:], tile_off[:].unsqueeze(2).broadcast_to(flat), ALU.subtract))
                    dve.nop().then_inc(row_ready, 1)
                    dve.nop().then_inc(row_ready, 1)
                    o.did(TS(tile_off[:], tile_f[:], 4096.0, None, ALU.mult))
                    o.did(TS(v1[:], dl_row[:], 0.0, None, ALU.is_ge))
                    o.link(TS(v2[:], dl_row[:], float(P), None, ALU.is_lt))
                    o.did(TT(v1[:], v1[:], v2[:], ALU.mult))
                    o.did(nc.vector.memset(ends[:], -1.0))
                    o.link(nc.vector.scalar_tensor_tensor(key_row[:], src_f[:], float(NP), seg_row[:], ALU.mult, ALU.add))
                    own = iota_row[0:GR].unsqueeze(1).broadcast_to(flat)
                    o.link(TT(seg_row[:], seg_row[:], tile_off[:].unsqueeze(2).broadcast_to(flat), ALU.add))
                    o.link(TT(key_row[:], key_row[:], own, ALU.subtract))
                    o.link(nc.vector.scalar_tensor_tensor(key_row[:], key_row[:], -float(KD), v1[:], ALU.add, ALU.mult))
                    o.link(TT(key_row[:], key_row[:], own, ALU.add))
                    o.did(TS(key_row[:], key_row[:], float(KD), None, ALU.add))
                    o.link(TT(msg_row[:], src_f[:], own, ALU.subtract))
                    o.link(nc.vector.scalar_tensor_tensor(msg_row[:], msg_row[:], -float(NP), v1[:], ALU.add, ALU.mult))
                    o.link(nc.vector.scalar_tensor_tensor(msg_row[:], msg_row[:], float(NP), own, ALU.add, ALU.add))
                    dve.nop().then_inc(row_ready, 1)
                    dve.wait_ge(seg_in, 32)
                    o.did(TT(last_row[:], seg_row[:], after[:], ALU.not_equal))
                    o.link(TT(v1[:], seg_row[:], before[:], ALU.not_equal))
                    o.link(TS(v1[:], v1[:], -BIG, None, ALU.mult))
                    dve.nop().then_inc(row_ready, 1)
                    targets = (src_step[:], dl_step[:], key_step[:], last_step[:]) + tuple(attr4_step[:, :, c] for c in range(4))
                    for n, target in enumerate(targets):
                        dve.wait_ge(turned_ready, n + 1)
                        nc.vector.tensor_copy(target, turned[n % 4][:, 0:S]).then_inc(turned_used, 1)

                @block.scalar
                def _(act):
                    norm_root(act, *norms[0])
                    apply_tiles(x_sb, h0, h0_ready)
                    norm_root(act, *norms[1])

        with ExitStack() as ctx:
            wall = sb("wall", [P, 2, HD + 2 * HW], F32, ctx)
            arep = sb("arep", [P, 2, HD], F32, ctx)
            aprod = sb("aprod", [P, HD], F32, ctx)
            score_w = sb("score_w", [P, 2, 2, 12], F32, ctx)
            gb = sb("gb", [P, 2, 2], F32, ctx)
            bw = sb("bw", [1, HD + 2 * HW], F32, ctx)
            bw_rep = sb("bw_rep", [P, HD + 2 * HW], F32, ctx)
            bias_rep = sem("bias_rep")
            zs = sb("zs", [P, 2, D], F32, ctx)
            zT = sb("zT", [P, 2, 2, P], F32, ctx)
            orow = sb("orow", [P, 5, ROW], F32, ctx)
            srow = sb("srow", [P, 5, SROW], F32, ctx)
            dsmall = sb("dsmall", [P, 2, NT], F32, ctx)
            p_zT = [ps(f"p_zT{i}", [P, 2, P], F32, ctx) for i in range(2)]
            p_h = [ps(f"p_h{i}", [P, HD], F32, ctx) for i in range(2)]
            p_s = [ps(f"p_s{i}", [P, 2 * HW], F32, ctx) for i in range(2)]
            p_b = ps("p_b", [1, 1024], F32, ctx)
            w_in, w_order, w_ready, bias_mm, bias_sb = sem("w_in"), sem("w_order"), sem("w_ready"), sem("bias_mm"), sem("bias_sb")
            dvar, droot = sem("dvar"), sem("droot")
            with nc.Block() as block:
                @block.sync
                def _(sp):
                    for k in range(2):
                        sp.dma_start(wall[:, k, 0:256], a["W1"][k * P:(k + 1) * P, :]).then_inc(w_in, 16)
                        sp.dma_start(wall[:, k, 256:512], a["W2"][k * P:(k + 1) * P, :]).then_inc(w_in, 16)
                    for n, (one, two) in enumerate((("a_src1", "a_src2"), ("a_dst1", "a_dst2"))):
                        for c, name in enumerate((one, two)):
                            row = a[name].rearrange("h c -> (h c)")
                            sp.dma_start(arep[:, n, c * 256:(c + 1) * 256], row.partition_broadcast(P)).then_inc(w_in, 16)
                    sp.dma_start(gb[:, :, 0], a["gamma"].rearrange("(k p) -> p k", k=2)).then_inc(w_in, 16)
                    sp.dma_start(gb[:, :, 1], a["beta"].rearrange("(k p) -> p k", k=2)).then_inc(w_in, 16)

                @block.vector
                def _(dve):
                    o = Order(dve, w_order)
                    dve.wait_ge(w_in, 160)
                    for k in range(2):
                        for n in range(2):
                            o.link(nc.vector.tensor_tensor(aprod[:], wall[:, k, 0:HD], arep[:, n, :], ALU.mult))
                            o.did(nc.vector.tensor_reduce(score_w[:, k, n, 0:4], aprod[:, 0:256].rearrange("p (h c) -> p h c", h=4), AX.X, ALU.add))
                            o.link(nc.vector.tensor_reduce(score_w[:, k, n, 4:12], aprod[:, 256:512].rearrange("p (h c) -> p h c", h=8), AX.X, ALU.add))
                            at = HD + n * HW
                            o.did(nc.vector.tensor_copy(wall[:, k, at:at + 8].rearrange("p (h o) -> p h o", o=2),
                                                        score_w[:, k, n, 0:4].unsqueeze(2).broadcast_to([P, 4, 2])))
                            o.link(nc.vector.tensor_copy(wall[:, k, at + 8:at + 16], score_w[:, k, n, 4:12]))
                    dve.nop().then_inc(w_ready, 1)
                    dve.wait_ge(bias_mm, 1)
                    nc.vector.tensor_copy(bw[:, 0:HD], p_b[:, 0:HD]).then_inc(bias_sb, 1)
                    nc.vector.tensor_copy(bw[:, HD:], p_b[:, 512:512 + 2 * HW]).then_inc(bias_sb, 1)
                    dve.wait_ge(bias_rep, 1)
                    nc.vector.tensor_copy(bw_rep[:, 0:HD], p_h[0][:])
                    nc.vector.tensor_copy(bw_rep[:, HD:], p_s[0][:])
                    for k in range(2):
                        o.did(nc.vector.tensor_scalar(wall[:, k, :], wall[:, k, :], gb[:, k, 0:1], None, ALU.mult))
                    o.did(nc.vector.tensor_scalar(dsmall[:, 0, :], deg[:], 0.5, None, ALU.is_ge))
                    o.link(nc.vector.tensor_scalar(dsmall[:, 1, :], deg[:], 1.0, None, ALU.max))
                    dve.nop().then_inc(dvar, 1)
                    dve.wait_ge(droot, 1)
                    o.link(nc.vector.reciprocal(dinv[:], dinv[:]))
                    o.link(nc.vector.tensor_tensor(dinv[:], dinv[:], dsmall[:, 0, :], ALU.mult))

                @block.scalar
                def _(act):
                    act.wait_ge(dvar, 1)
                    nc.scalar.activation(dinv[:], dsmall[:, 1, :], ACT.Sqrt).then_inc(droot, 1)

                @block.tensor
                def _(pe):
                    pe.wait_ge(w_ready, 1)
                    for k in range(2):
                        nc.tensor.matmul(p_b[:, 0:HD], gb[:, k, 1:2], wall[:, k, 0:HD], start=(k == 0), stop=(k == 1))
                    for k in range(2):
                        m = nc.tensor.matmul(p_b[:, 512:512 + 2 * HW], gb[:, k, 1:2], wall[:, k, HD:], start=(k == 0), stop=(k == 1))
                    m.then_inc(bias_mm, 1)
                    pe.wait_ge(bias_sb, 2)
                    nc.tensor.matmul(p_h[0][:], ones[0:1, :], bw[:, 0:HD], start=True, stop=True)
                    nc.tensor.matmul(p_s[0][:], ones[0:1, :], bw[:, HD:], start=True, stop=True).then_inc(bias_rep, 1)

            z_ready, zT_ps, zT_sb, tabs_ps, score_out = (
                sem("z_ready"), sem("zT_ps"), sem("zT_sb"), sem("tabs_ps"), sem("score_out"))
            row_out = [sem(f"row_out{u}") for u in range(5)]
            x_sum = sem("x_sum")
            R = NT // 5
            with nc.Block() as block:
                @block.scalar
                def _(act):
                    for t in range(NT):
                        if t >= 2:
                            act.wait_ge(zT_ps, t - 1)
                        nc.scalar.activation(zs[:, t % 2, :], h0[:, t, :], ACT.Identity, bias=shift[:, t:t + 1],
                                             scale=rstd[:, t:t + 1]).then_inc(z_ready, 1)

                @block.tensor
                def _(pe):
                    def turn(t):
                        pe.wait_ge(z_ready, t + 1)
                        if t >= 2:
                            pe.wait_ge(zT_sb, t - 1)
                        for k in range(2):
                            m = nc.tensor.transpose(p_zT[t % 2][:, k, :], zs[:, t % 2, k * P:(k + 1) * P], ident[:])
                        m.then_inc(zT_ps, 1)

                    turn(0)
                    for t in range(NT):
                        if t + 1 < NT:
                            turn(t + 1)
                        pe.wait_ge(zT_sb, t + 1)
                        if t >= 2:
                            pe.wait_ge(score_out, t - 1)
                        for w, target in ((slice(0, HD), p_h[t % 2]), (slice(HD, HD + 2 * HW), p_s[t % 2])):
                            for k in range(2):
                                m = nc.tensor.matmul(target[:], zT[:, t % 2, k, :], wall[:, k, w], start=(k == 0), stop=(k == 1))
                        m.then_inc(tabs_ps, 1)

                @block.vector
                def _(dve):
                    def take(t):
                        dve.wait_ge(zT_ps, t + 1)
                        nc.vector.tensor_copy(zT[:, t % 2], p_zT[t % 2][:]).then_inc(zT_sb, 1)

                    take(0)
                    for t in range(NT):
                        if t + 1 < NT:
                            take(t + 1)
                        u = t % 5
                        dve.wait_ge(tabs_ps, t + 1)
                        dve.wait_ge(row_out[u], t // 5 * 32)
                        nc.vector.tensor_tensor(orow[:, u, 0:HD], p_h[t % 2][:], bw_rep[:, 0:HD], ALU.add)
                        nc.vector.tensor_tensor(orow[:, u, HD:], p_s[t % 2][:, 0:HW], bw_rep[:, HD:HD + HW], ALU.add)
                        nc.vector.tensor_tensor(srow[:, u, 0:HW], p_s[t % 2][:, 0:HW], bw_rep[:, HD:HD + HW], ALU.add)
                        nc.vector.tensor_copy(srow[:, u, HW:SROW], dinv[:, t:t + 1].broadcast_to([P, SROW - HW]))
                        nc.vector.tensor_tensor(tab[:, t, 0:HW], p_s[t % 2][:, HW:], bw_rep[:, HD + HW:], ALU.add).then_inc(score_out, 1)
                    nc.vector.tensor_tensor(x_sb[:], x_sb[:], h0[:], ALU.add).then_inc(x_sum, 1)

                @block.sync
                def _(sp):
                    for t in range(NT):
                        u = t % 5
                        sp.wait_ge(score_out, t + 1)
                        sp.dma_start(att_dram[t * P:(t + 1) * P, :], orow[:, u, :]).then_inc(row_out[u], 16)
                        sp.dma_start(score_dram[t * P:(t + 1) * P, :], srow[:, u, :]).then_inc(row_out[u], 16)
                    for u in range(5):
                        sp.wait_ge(row_out[u], 32 * R)
        with_h0.close()
        end_stage()

        G4 = S // 4
        place_all = sb("place_all", [P, S], I32, early)
        number_all = sb("number_all", [P, S], F32, early)

        def rounds(engine, work):
            work(0, 0, 0)
            work(1, 1, 0)
            with engine.Fori(1, G4 // 2 - 1) as i:
                work(i * 2, 0, i)
                work(i * 2 + 1, 1, i)
            work(G4 - 2, 0, G4 // 2 - 1)
            work(G4 - 1, 1, G4 // 2 - 1)

        def is_last(j, n=1):
            return isinstance(j, int) and j >= G4 - n

        with_acc = top.enter_context(ExitStack())
        acc = sb("acc", [P, NT, ROW], F32, with_acc)
        with ExitStack() as ctx:
            top_acc = sb("top_acc", [P, NT, SROW], F32, ctx)
            idx = [sb(f"idx{q}", [P, 4], I32, ctx) for q in range(2)]
            score_g = [sb(f"score_g{q}", [P, 4, SROW], F32, ctx) for q in range(2)]
            pen = [sb(f"pen{q}", [HW, 4 * P], F32, ctx) for q in range(2)]
            run = [sb(f"run{q}", [HW, 4 * P], F32, ctx) for q in range(2)]
            hot = [sb(f"hot{q}", [P, 4, P], F32, ctx) for q in range(2)]
            rhs = [sb(f"rhs{q}", [P, 4, SROW], F32, ctx) for q in range(2)]
            key_rep = [sb(f"key_rep{q}", [P, 4, P], F32, ctx) for q in range(2)]
            same = sb("same", [P, 4, P], F32, ctx)
            earlier = sb("earlier", [P, 4, P], F32, ctx)
            prior = sb("prior", [P, 4], F32, ctx)
            place_f = sb("place_f", [P, 4], F32, ctx)
            no_edge = sb("no_edge", [P, NT], F32, ctx)
            number = [sb(f"number{q}", [P, 2], F32, ctx) for q in range(2)]
            place = [sb(f"place{q}", [P, 2], I32, ctx) for q in range(2)]
            own_place = sb("own_place", [P, 1], F32, ctx)
            p_in = [ps(f"p_in{q}", [HW, 4 * P], F32, ctx) for q in range(2)]
            p_run = [ps(f"p_run{q}", [P, 4, HW], F32, ctx) for q in range(2)]
            p_top = [ps(f"p_top{q}", [P, 4, SROW], F32, ctx) for q in range(2)]
            scores_in = [sem(f"a_scores_in{q}") for q in range(2)]
            rep_in = [sem(f"a_rep_in{q}") for q in range(2)]
            (idx_ready, turned_in, run_ready, run_turned, rhs_ready, tops, added, place_ready, slots_ready, placed, a_order, keys_used,
             places_free, self_in, own_in, loops) = (sem("a_" + x) for x in (
                 "idx_ready", "turned_in", "run_ready", "run_turned", "rhs_ready", "tops", "added", "place_ready", "slots_ready", "placed",
                 "order", "keys_used", "places_free", "self_in", "own_in", "loops"))
            with nc.Block() as block:
                @block.sync
                def _(sp):
                    sp.dma_start(self_s[:], score_dram.rearrange("(t p) s -> p t s", p=P)[:, :, 0:HW]).then_inc(self_in, 16)

                    def load_pair(i):
                        for q in range(2):
                            g = i * 2 + q
                            sp.wait_ge(keys_used, g + 1)
                            sp.dma_start(pen[q][:], pen_dram[bass.ds(g * 4 * P, 4 * P)].partition_broadcast(HW)).then_inc(rep_in[q], 16)
                            sp.dma_start(key_rep[q][:].rearrange("p u e -> p (u e)"),
                                         key_dram[bass.ds(g * 4 * P, 4 * P)].partition_broadcast(P)).then_inc(rep_in[q], 16)

                    with sp.Fori(0, NT) as t:
                        load_pair(t)
                        sp.dma_start(acc[:, bass.ds(t, 1), :].rearrange("p o s -> p (o s)"), att_dram[bass.ds(t * P, P), :]).then_inc(own_in, 16)
                    with sp.Fori(NT, G4 // 2) as i:
                        load_pair(i)
                    sp.wait_ge(own_in, 16 * NT)

                @block.scalar
                def _(act):
                    def indices(g, q):
                        nc.scalar.copy(idx[q][:], src_step[:, bass.ds(g * 4, 4)]).then_inc(idx_ready, 1)

                    def work(j, q, i):
                        act.wait_ge(place_ready, j + 1)
                        act.wait_ge(places_free, j)
                        nc.scalar.copy(number[q][:], number_all[:, bass.ds(j * 4, 2)])
                        nc.scalar.copy(place[q][:], place_all[:, bass.ds(j * 4, 2)]).then_inc(slots_ready, 1)
                        if not is_last(j, 2):
                            act.wait_ge(rhs_ready, j + 1)
                            indices(j + 2, q)

                    indices(0, 0)
                    indices(1, 1)
                    rounds(act, work)
                    act.wait_ge(loops, 1)
                    nc.scalar.activation(self_s[:], self_s[:], ACT.Exp)

                @block.gpsimd
                def _(pool):
                    def gather(q, u):
                        nc.gpsimd.indirect_dma_start(
                            score_g[q][:, u, :], None, score_dram,
                            bass.IndirectOffsetOnAxis(ap=idx[q][:, u:u + 1].bitcast(U32), axis=0)).then_inc(scores_in[q], 16)

                    def work(j, q, i):
                        ahead = not is_last(j, 2)
                        if ahead:
                            pool.wait_ge(rhs_ready, j + 1)
                            pool.wait_ge(idx_ready, j + 3)
                            pool.nop().then_inc(waits_passed, 1)
                        for n in range(2):
                            if ahead:
                                gather(q, 2 * n)
                                gather(q, 2 * n + 1)
                            if n == 0:
                                pool.wait_ge(slots_ready, j + 1)
                            pool.wait_ge(placed, (j * 2 + n) * 16)
                            pool.nop().then_inc(places_free if n == 0 else waits_passed, 1)
                            nc.gpsimd.indirect_dma_start(
                                count_dram, bass.IndirectOffsetOnAxis(ap=place[q][:, n:n + 1].bitcast(U32), axis=0),
                                number[q][:, n:n + 1], None, compute_op=ALU.add).then_inc(placed, 16)

                    for q in range(2):
                        pool.wait_ge(idx_ready, q + 1)
                        for u in range(4):
                            gather(q, u)
                    pool.wait_ge(zeros_out, 16 * (NZ + 1))
                    rounds(pool, work)
                    pool.wait_ge(placed, G4 * 32)

                @block.tensor
                def _(pe):
                    def turn_scores(g, q, i):
                        pe.wait_ge(scores_in[q], i * 64 + 64)
                        for u in range(4):
                            m = nc.tensor.transpose(p_in[q][:, u * P:(u + 1) * P], score_g[q][:, u, 0:HW], ident[:])
                        m.then_inc(turned_in, 1)

                    def work(j, q, i):
                        pe.wait_ge(run_ready, j + 1)
                        for u in range(4):
                            m = nc.tensor.matmul(p_run[q][:, u, :], run[q][:, u * P:(u + 1) * P], ident[0:HW, 0:HW], start=True, stop=True)
                        m.then_inc(run_turned, 1)
                        if not is_last(j):
                            turn_scores(j + 1, 1 - q, i + q)
                        pe.wait_ge(rhs_ready, j + 1)
                        for u in range(4):
                            m = nc.tensor.matmul(p_top[q][:, u, :], hot[q][:, u, :], rhs[q][:, u, :], start=True, stop=True)
                        m.then_inc(tops, 1)

                    turn_scores(0, 0, 0)
                    rounds(pe, work)

                @block.vector
                def _(dve):
                    o = Order(dve, a_order)
                    TT, TS = nc.vector.tensor_tensor, nc.vector.tensor_scalar
                    dve.nop().then_inc(keys_used, 2)
                    o.did(nc.vector.memset(top_acc[:], 0.0))
                    o.did(nc.vector.memset(run[1][:], 0.0))
                    o.link(TS(own_place[:], pidx[:], float(KD), None, ALU.add))
                    spread = [P, 4, P]

                    def add_tops(g, q, tiles):
                        dve.wait_ge(tops, g + 1)
                        for u in range(4):
                            acc = top_acc[:, bass.ds(tiles[u], 1), :].rearrange("p o s -> p (o s)")
                            dve.wait_ge(added, g * 4 + u)
                            TT(acc, acc, p_top[q][:, u, :], ALU.add).then_inc(added, 1)

                    def work(j, q, i, tiles):
                        o.enter(j)
                        grp = bass.ds(j * 4, 4)
                        dve.wait_ge(rep_in[q], i * 32 + 32)
                        dve.wait_ge(turned_in, j + 1)
                        dve.wait_ge(run_ready, j)
                        nc.vector.tensor_tensor_scan(run[q][:], pen[q][:], p_in[q][:], run[1 - q][:, 4 * P - 1:4 * P],
                                                     ALU.add, ALU.max).then_inc(run_ready, 1)
                        here = key_step[:, grp]
                        o.link(TT(same[:], key_rep[q][:], here.unsqueeze(2).broadcast_to(spread), ALU.is_equal))
                        o.did(TT(earlier[:], same[:], lower[:].unsqueeze(1).broadcast_to(spread), ALU.mult))
                        nc.vector.tensor_reduce(number_all[:, grp], same[:], AX.X, ALU.add)
                        o.need(o.n)
                        o.link(nc.vector.tensor_reduce(prior[:], earlier[:], AX.X, ALU.add))
                        dve.wait_ge(run_ready, j + 1)
                        dve.nop().then_inc(keys_used, 1)
                        o.did(TS(prior[:], prior[:], 0.5, None, ALU.is_lt))
                        o.link(TT(place_f[:], here, own_place[:].broadcast_to([P, 4]), ALU.subtract))
                        o.link(TT(place_f[:], place_f[:], prior[:], ALU.mult))
                        TT(place_all[:, grp], place_f[:], own_place[:].broadcast_to([P, 4]), ALU.add).then_inc(place_ready, 1)
                        TT(hot[q][:], iota_row[:].unsqueeze(1).broadcast_to(spread),
                           dl_step[:, grp].unsqueeze(2).broadcast_to(spread), ALU.is_equal)
                        TT(rhs[q][:, :, HW:SROW], attr4_step[:, grp, :], score_g[q][:, :, HW:HW + 1].broadcast_to([P, 4, 4]), ALU.mult)
                        dve.wait_ge(run_turned, j + 1)
                        TT(rhs[q][:, :, 0:HW], p_run[q][:], last_step[:, grp].unsqueeze(2).broadcast_to([P, 4, HW]),
                           ALU.mult).then_inc(rhs_ready, 1)
                        if not is_first(j):
                            add_tops(j - 1, 1 - q, tiles)

                    o.begin(6)
                    tiles = read_registers(nc, step_table, 0, 4, ET.DVE, NT - 1)
                    work(0, 0, 0, None)
                    work(1, 1, 0, tiles)
                    with dve.Fori(1, G4 // 2) as i:
                        tiles = read_registers(nc, step_table, i * 8 - 4, 8, ET.DVE, NT - 1)
                        work(i * 2, 0, i, tiles[0:4])
                        work(i * 2 + 1, 1, i, tiles[4:8])
                    o.leave(G4)
                    add_tops(G4 - 1, 1, read_registers(nc, step_table, S - 4, 4, ET.DVE, NT - 1))
                    dve.wait_ge(added, S)
                    lo, hi = tab[:, :, 0:HW], tab[:, :, HW:]
                    every = [P, NT, HW]
                    dve.wait_ge(self_in, 16)
                    o.link(TS(no_edge[:], deg[:], 0.5, -BIG, ALU.is_lt, ALU.mult))
                    o.link(TT(hi, top_acc[:, :, 0:HW], no_edge[:].unsqueeze(2).broadcast_to(every), ALU.add))
                    o.link(TT(hi, hi, self_s[:], ALU.max))
                    o.did(TT(hi, hi, lo, ALU.add))
                    o.link(TT(self_s[:], self_s[:], lo, ALU.add))
                    o.did(nc.vector.scalar_tensor_tensor(self_s[:], self_s[:], 0.2, self_s[:], ALU.mult, ALU.max))
                    o.link(nc.vector.scalar_tensor_tensor(hi, hi, 0.2, hi, ALU.mult, ALU.max))
                    TT(self_s[:], self_s[:], hi, ALU.subtract).then_inc(loops, 1)
                    nc.vector.tensor_copy(F_sb[:], top_acc[:, :, HW:])
        end_stage()

        with ExitStack() as ctx:
            with ExitStack() as inner:
                idx = [sb(f"b_idx{q}", [P, 4], I32, inner) for q in range(2)]
                number = [sb(f"b_number{q}", [P, 2], F32, inner) for q in range(2)]
                place = [sb(f"b_place{q}", [P, 2], I32, inner) for q in range(2)]
                row_g = [sb(f"row_g{q}", [P, 4, ROW], F32, inner) for q in range(2)]
                hot = [sb(f"b_hot{q}", [P, 4, P], F32, inner) for q in range(2)]
                away = sb("away", [P, 4, P], F32, inner)
                dl_rep = [sb(f"dl_rep{q}", [P, 4, P], F32, inner) for q in range(2)]
                hotT = [sb(f"b_hotT{q}", [P, 4, P], F32, inner) for q in range(2)]
                zz = sb("zz", [P, 4, HW], F32, inner)
                weight = [sb(f"weight{q}", [P, 4, HW], F32, inner) for q in range(2)]
                msg = [sb(f"msg{q}", [P, 4, HD], F32, inner) for q in range(2)]
                p_tab = ps("b_p_tab", [P, 4, 2 * HW], F32, inner)
                p_out = [ps(f"b_p_out{v}", [P, HD], F32, inner) for v in range(4)]
                p_den = [ps(f"b_p_den{q}", [P, 4, HW], F32, inner) for q in range(2)]
                rows_in = [sem(f"b_rows_in{q}") for q in range(2)]
                rep_in = [sem(f"b_rep_in{q}") for q in range(2)]
                (idx_ready, hotT_ready, hot_ready, tab_ready, arg_ready, weight_ready, msg_ready, sums_ready, added, b_order,
                 slots_ready, placed, places_free, away_ready, hots_used) = (sem("b_" + x) for x in (
                     "idx_ready", "hotT_ready", "hot_ready", "tab_ready", "arg_ready", "weight_ready", "msg_ready", "sums_ready", "added",
                     "order", "slots_ready", "placed", "places_free", "away_ready", "hots_used"))
                with nc.Block() as block:
                    @block.sync
                    def _(sp):
                        with sp.Fori(0, G4 // 2) as i:
                            for q in range(2):
                                sp.wait_ge(hotT_ready, i * 2 + q + 1)
                                sp.nop().then_inc(waits_passed, 1)
                                sp.dma_start(dl_rep[q][:], pair_dram[bass.ds((i * 2 + q) * 4, 4), 0, :].partition_broadcast(P)).then_inc(rep_in[q], 16)

                    @block.scalar
                    def _(act):
                        def indices(g, q):
                            nc.scalar.copy(idx[q][:], src_step[:, bass.ds(g * 4, 4)]).then_inc(idx_ready, 1)

                        def slots(g, q):
                            nc.scalar.copy(number[q][:], number_all[:, bass.ds(g * 4 + 2, 2)])
                            nc.scalar.copy(place[q][:], place_all[:, bass.ds(g * 4 + 2, 2)]).then_inc(slots_ready, 1)

                        def edge_hot(g, q):
                            for u in range(4):
                                r = nc.scalar.activation(away[:, u, :], iota_row[:], ACT.Abs, bias=column(dl_step, g * 4 + u), scale=-1.0)
                            r.then_inc(away_ready, 1)
                            act.wait_ge(away_ready, g + 1)
                            nc.scalar.activation(hot[q][:], away[:], ACT.Relu, bias=1.0, scale=-1.0).then_inc(hot_ready, 1)

                        def work(j, q, i):
                            act.wait_ge(arg_ready, j + 1)
                            nc.scalar.activation(weight[q][:], zz[:], ACT.Exp).then_inc(weight_ready, 1)
                            if not is_last(j, 2):
                                indices(j + 2, q)
                            if not is_last(j):
                                act.wait_ge(places_free, j + 1)
                                slots(j + 1, 1 - q)
                                if not is_first(j):
                                    act.wait_ge(hots_used, j)
                                edge_hot(j + 1, 1 - q)

                        indices(0, 0)
                        indices(1, 1)
                        edge_hot(0, 0)
                        slots(0, 0)
                        rounds(act, work)

                    @block.gpsimd
                    def _(pool):
                        def gather(q, u):
                            nc.gpsimd.indirect_dma_start(
                                row_g[q][:, u, :], None, att_dram,
                                bass.IndirectOffsetOnAxis(ap=idx[q][:, u:u + 1].bitcast(U32), axis=0)).then_inc(rows_in[q], 16)

                        def work(j, q, i):
                            ahead = not is_last(j, 2)
                            if ahead:
                                pool.wait_ge(idx_ready, j + 3)
                            for n in range(2):
                                if ahead:
                                    for u in (2 * n, 2 * n + 1):
                                        pool.wait_ge(msg_ready, j * 4 + u + 1)
                                        pool.nop().then_inc(waits_passed, 1)
                                        gather(q, u)
                                if n == 0:
                                    pool.wait_ge(slots_ready, j + 1)
                                pool.wait_ge(placed, (j * 2 + n) * 16)
                                pool.nop().then_inc(places_free if n == 0 else waits_passed, 1)
                                nc.gpsimd.indirect_dma_start(
                                    count_dram, bass.IndirectOffsetOnAxis(ap=place[q][:, n:n + 1].bitcast(U32), axis=0),
                                    number[q][:, n:n + 1], None, compute_op=ALU.add).then_inc(placed, 16)

                        for q in range(2):
                            pool.wait_ge(idx_ready, q + 1)
                            for u in range(4):
                                gather(q, u)
                        rounds(pool, work)
                        pool.wait_ge(placed, G4 * 32)

                    @block.tensor
                    def _(pe):
                        def look_up(g, q, tiles):
                            pe.wait_ge(hotT_ready, g + 3)
                            for u in range(4):
                                m = nc.tensor.matmul(p_tab[:, u, :], hotT[q][:, u, :],
                                                     tab[:, bass.ds(tiles[u], 1), :].rearrange("p o h -> p (o h)"), start=True, stop=True)
                            m.then_inc(tab_ready, 1)

                        def work(j, q, i, tiles):
                            if not is_last(j):
                                pe.wait_ge(arg_ready, j + 1)
                                look_up(j + 1, 1 - q, tiles)
                            pe.wait_ge(hot_ready, j + 1)
                            for u in range(4):
                                pe.wait_ge(msg_ready, j * 4 + u + 1)
                                if not is_first(j):
                                    pe.wait_ge(added, j * 4 + u - 2)
                                nc.tensor.matmul(p_out[u][:], hot[q][:, u, :], msg[q][:, u, :], start=True, stop=True)
                                nc.tensor.matmul(p_den[q][:, u, :], hot[q][:, u, :], weight[q][:, u, :],
                                                 start=True, stop=True).then_inc(sums_ready, 1)

                        def pair_of(i, last):
                            tiles = read_registers(nc, step_table, i * 8 + 4, 4 if last else 8, ET.PE, NT - 1)
                            work(i * 2, 0, i, tiles[0:4])
                            work(i * 2 + 1, 1, i, tiles[4:8])

                        look_up(0, 0, read_registers(nc, step_table, 0, 4, ET.PE, NT - 1))
                        pair_of(0, False)
                        with pe.Fori(1, G4 // 2 - 1) as i:
                            pair_of(i, False)
                        pair_of(G4 // 2 - 1, True)

                    @block.vector
                    def _(dve):
                        o = Order(dve, b_order)
                        TT, TS = nc.vector.tensor_tensor, nc.vector.tensor_scalar
                        dve.nop().then_inc(hotT_ready, 2)
                        for t in range(NT):
                            TT(acc[:, t, 0:HD].rearrange("p (h c) -> p h c", h=HW), acc[:, t, 0:HD].rearrange("p (h c) -> p h c", h=HW),
                               self_s[:, t, :].unsqueeze(2).broadcast_to([P, HW, HD // HW]), ALU.mult)
                        o.link(nc.vector.tensor_copy(acc[:, :, HD:], self_s[:]))
                        dve.nop().then_inc(added, 1)
                        spread = [P, 4, P]

                        def node_hot(q, u):
                            return TS(hotT[q][:, u, :], dl_rep[q][:, u, :], pidx[:, 0:1], None, ALU.is_equal)

                        def weigh(g, q, u):
                            TT(msg[q][:, u, :].rearrange("p (h c) -> p h c", h=HW), row_g[q][:, u, 0:HD].rearrange("p (h c) -> p h c", h=HW),
                               weight[q][:, u, :].unsqueeze(2).broadcast_to([P, HW, HD // HW]), ALU.mult).then_inc(msg_ready, 1)

                        def add_sums(g, q, u, tiles):
                            dve.wait_ge(sums_ready, g * 4 + u + 1)
                            dve.wait_ge(added, g * 4 + u + 1)
                            own = acc[:, bass.ds(tiles[u], 1), 0:HD].rearrange("p o s -> p (o s)")
                            TT(own, own, p_out[u][:], ALU.add).then_inc(added, 1)

                        def add_weights(g, q, u, tiles):
                            own = acc[:, bass.ds(tiles[u], 1), HD:].rearrange("p o s -> p (o s)")
                            o.did(TT(own, own, p_den[q][:, u, :], ALU.add))

                        def work(j, q, i, tiles):
                            if not is_first(j):
                                o.enter(j)
                            before, after = not is_first(j), not is_last(j)
                            dve.wait_ge(rows_in[q], i * 64 + 64)
                            dve.wait_ge(tab_ready, j + 1)
                            o.did(TT(zz[:], p_tab[:, :, 0:HW], row_g[q][:, :, HD:], ALU.add))
                            if after:
                                dve.wait_ge(rep_in[1 - q], (i + q) * 16 + 16)
                                node_hot(1 - q, 0)
                            o.need(1 if before else o.n)
                            o.did(nc.vector.scalar_tensor_tensor(zz[:], zz[:], 0.2, zz[:], ALU.mult, ALU.max))
                            if after:
                                node_hot(1 - q, 1)
                            o.need(2 if before else o.n)
                            o.did(TT(zz[:], zz[:], p_tab[:, :, HW:], ALU.subtract))
                            if after:
                                node_hot(1 - q, 2)
                            o.need(3 if before else o.n)
                            TS(zz[:], zz[:], 0.0, None, ALU.min).then_inc(arg_ready, 1)
                            if before:
                                add_sums(j - 1, 1 - q, 0, tiles)
                            if after:
                                node_hot(1 - q, 3).then_inc(hotT_ready, 1)
                            if before:
                                add_sums(j - 1, 1 - q, 1, tiles)
                            dve.wait_ge(weight_ready, j + 1)
                            weigh(j, q, 0)
                            if before:
                                add_sums(j - 1, 1 - q, 2, tiles)
                            weigh(j, q, 1)
                            if before:
                                add_sums(j - 1, 1 - q, 3, tiles)
                                add_weights(j - 1, 1 - q, 0, tiles)
                            if before:
                                dve.nop().then_inc(hots_used, 1)
                                o.need(4)
                                add_weights(j - 1, 1 - q, 1, tiles)
                            weigh(j, q, 2)
                            if before:
                                o.need(5)
                                add_weights(j - 1, 1 - q, 2, tiles)
                            weigh(j, q, 3)
                            if before:
                                o.need(6)
                                add_weights(j - 1, 1 - q, 3, tiles)

                        dve.wait_ge(rep_in[0], 16)
                        for u in range(4):
                            k = node_hot(0, u)
                        k.then_inc(hotT_ready, 1)
                        work(0, 0, 0, None)
                        o.begin(7, first=1)
                        work(1, 1, 0, read_registers(nc, step_table, 0, 4, ET.DVE, NT - 1))
                        with dve.Fori(1, G4 // 2 - 1) as i:
                            tiles = read_registers(nc, step_table, i * 8 - 4, 8, ET.DVE, NT - 1)
                            work(i * 2, 0, i, tiles[0:4])
                            work(i * 2 + 1, 1, i, tiles[4:8])
                        tiles = read_registers(nc, step_table, S - 12, 8, ET.DVE, NT - 1)
                        work(G4 - 2, 0, G4 // 2 - 1, tiles[0:4])
                        work(G4 - 1, 1, G4 // 2 - 1, tiles[4:8])
                        o.leave(G4)
                        tiles = read_registers(nc, step_table, S - 4, 4, ET.DVE, NT - 1)
                        for u in range(4):
                            add_sums(G4 - 1, 1, u, tiles)
                        o.need(o.n)
                        for u in range(4):
                            add_weights(G4 - 1, 1, u, tiles)
                            o.need(o.n)
            with ExitStack() as inner:
                wu = sb("wu", [P, 4, D], F32, inner)
                brow = sb("brow", [P, HD + D], F32, inner)
                den = sb("den", [P, NT, HW], F32, inner)
                val = sb("val", [P, 5, HD], F32, inner)
                neg = sb("neg", [P, 5, HD], F32, inner)
                valT = sb("valT", [P, 5, 4, P], F32, inner)
                cnt = [sb(f"cnt{q}", [P, HALF], F32, inner) for q in range(2)]
                half = [sb(f"half{q}", [P, HALF], F16, inner) for q in range(2)]
                deg_half = sb("deg_half", [P, 2, NT], F32, inner)
                cnt_in, stored = [[sem(f"c_{x}{q}") for q in range(2)] for x in ("cnt_in", "stored")]
                halves = [sem(f"c_halves{q}") for q in range(2)]
                p_val = [ps(f"p_val{v}", [P, 4, P], F32, inner) for v in range(2)]
                p_uni = [ps(f"p_uni{v}", [P, D], F32, inner) for v in range(2)]
                c_in, c_order, neg_ready, exp_ready, elu_ready, val_turned, valT_ready, uni_ready, x_added = (
                    sem("c_in"), sem("c_order"), sem("neg_ready"), sem("exp_ready"), sem("elu_ready"), sem("val_turned"),
                    sem("valT_ready"), sem("uni_ready"), sem("x_added"))
                with nc.Block() as block:
                    @block.sync
                    def _(sp):
                        sp.dma_start(wu[:], a["Wu"].rearrange("(k p) d -> p k d", k=4)).then_inc(c_in, 16)
                        for name, w in (("b1", slice(0, 256)), ("b2", slice(256, HD)), ("bu", slice(HD, HD + D))):
                            sp.dma_start(brow[:, w], a[name].partition_broadcast(P)).then_inc(c_in, 16)

                        def load(t, q):
                            rows = count_dram[bass.ds(t * (P * NP), P * NP), :].rearrange("(p f) o -> p (f o)", p=P)
                            sp.dma_start(cnt[q][:], rows[:, q * HALF:(q + 1) * HALF]).then_inc(cnt_in[q], 16)

                        def store(t, q):
                            sp.wait_ge(halves[q], t + 1)
                            sp.nop().then_inc(waits_passed, 1)
                            sp.dma_start(by_src[bass.ds(t * P, P), q * HALF:(q + 1) * HALF], half[q][:]).then_inc(stored[q], 16)

                        for q in range(2):
                            load(0, q)
                        with sp.Fori(0, NT - 1) as t:
                            for q in range(2):
                                store(t, q)
                                load(t + 1, q)
                        for q in range(2):
                            store(NT - 1, q)
                        for q in range(2):
                            sp.wait_ge(stored[q], 16 * NT)

                    @block.vector
                    def _(dve):
                        o = Order(dve, c_order)
                        TT = nc.vector.tensor_tensor
                        o.link(nc.vector.tensor_scalar(den[:], acc[:, :, HD:], 1e-16, None, ALU.add))
                        o.link(nc.vector.reciprocal(den[:], den[:]))
                        dve.wait_ge(c_in, 64)
                        o.begin(5 * 3)
                        with dve.Fori(0, R) as i:
                            o.enter(i)
                            for u in range(5):
                                t = i * 5 + u
                                dve.wait_ge(val_turned, i * 5 + u + 1)
                                o.link(TT(val[:, u, :].rearrange("p (h c) -> p h c", h=HW),
                                          acc[:, bass.ds(t, 1), 0:HD].rearrange("p o (h c) -> p (o h) c", h=HW),
                                          den[:, bass.ds(t, 1), :].rearrange("p o h -> p (o h)").unsqueeze(2).broadcast_to([P, HW, HD // HW]), ALU.mult))
                                o.link(TT(val[:, u, :], val[:, u, :], brow[:, 0:HD], ALU.add))
                                nc.vector.tensor_scalar(neg[:, u, :], val[:, u, :], 0.0, None, ALU.min).then_inc(neg_ready, 1)
                                o.link(nc.vector.tensor_scalar(val[:, u, :], val[:, u, :], 0.0, -1.0, ALU.max, ALU.add))
                                dve.wait_ge(exp_ready, t + 1)
                                TT(val[:, u, :], val[:, u, :], neg[:, u, :], ALU.add).then_inc(elu_ready, 1)
                            for u in range(5):
                                t = i * 5 + u
                                dve.wait_ge(uni_ready, t + 1)
                                own = x_sb[:, bass.ds(t, 1), :].rearrange("p o d -> p (o d)")
                                TT(own, own, p_uni[u % 2][:], ALU.add).then_inc(x_added, 1)
                        o.leave(R)
                        for q in range(2):
                            dve.wait_ge(halves[q], NT)
                        nc.vector.tensor_tensor(degsrc[:], deg_half[:, 0, :], deg_half[:, 1, :], ALU.add)
                        dve.wait_ge(x_added, NT)
                        o.link(TT(x_sb[:], x_sb[:], brow[:, HD:].unsqueeze(1).broadcast_to([P, NT, D]), ALU.add))

                    @block.scalar
                    def _(act):
                        def round_counts(t, q):
                            act.wait_ge(cnt_in[q], t * 16 + 16)
                            act.wait_ge(stored[q], t * 16)
                            nc.scalar.activation(half[q][:], cnt[q][:], ACT.Copy, accum_out=column(deg_half[:, q, :], t)).then_inc(halves[q], 1)

                        def round_of(i):
                            for u in range(5):
                                act.wait_ge(neg_ready, i * 5 + u + 1)
                                nc.scalar.activation(neg[:, u, :], neg[:, u, :], ACT.Exp).then_inc(exp_ready, 1)
                                round_counts(i * 5 + u // 2, u % 2)
                            for u in range(5):
                                act.wait_ge(val_turned, 5 + i * 5 + u + 1)
                                nc.scalar.copy(valT[:, u], p_val[u % 2][:]).then_inc(valT_ready, 1)
                                round_counts(i * 5 + (u + 5) // 2, (u + 5) % 2)

                        looped(act, R, round_of)

                    @block.tensor
                    def _(pe):
                        pe.nop().then_inc(val_turned, 5)
                        def round_of(i):
                            for u in range(5):
                                t = i * 5 + u
                                pe.wait_ge(elu_ready, t + 1)
                                if u >= 2 or not is_first(i):
                                    pe.wait_ge(valT_ready, t - 1)
                                for k in range(4):
                                    m = nc.tensor.transpose(p_val[u % 2][:, k, :], val[:, u, k * P:(k + 1) * P], ident[:])
                                m.then_inc(val_turned, 1)
                                pe.wait_ge(valT_ready, t + 1)
                                if u >= 2 or not is_first(i):
                                    pe.wait_ge(x_added, t - 1)
                                for k in range(4):
                                    m = nc.tensor.matmul(p_uni[u % 2][:], valT[:, u, k, :], wu[:, k, :], start=(k == 0), stop=(k == 3))
                                m.then_inc(uni_ready, 1)

                        looped(pe, R, round_of)
        with_acc.close()
        early.close()

        end_stage()

        with ExitStack() as ctx:
            hT = sb("hT", [P, 2, NP], F32, ctx)
            aggT = sb("aggT", [P, 2, NP], F32, ctx)
            parts = sb("parts", [P, NT, 2, 2, P], F16, ctx)
            cbuf = [sb(f"cbuf{q}", [P, NT, W], F16, ctx) for q in range(2)]
            wslot = sb("wslot", [P, 4, D], F32, ctx)
            ewslot = sb("ewslot", [4, D], F32, ctx)
            FT = sb("FT", [4, NP], F32, ctx)
            dinv_rep = sb("dinv_rep", [P, NP], F32, ctx)
            zero_rows = sb("zero_rows", [P, 2 * D], F32, ctx)
            low_sb = [sb(f"low_sb{m}", [P, W], F32, ctx) for m in range(2)]
            rest = [sb(f"rest{v}", [P, 2, P], F32, ctx) for v in range(2)]
            bn_tab = sb("bn_tab", [P, LAYERS, 3, 2], F32, ctx)
            bn_raw = sb("bn_raw", [P, 2, NC, 6], F32, ctx)
            bn_mv = sb("bn_mv", [P, 2, 2], F32, ctx)
            bn_rs = sb("bn_rs", [P, 4, 2], F32, ctx)
            dinv_dram = dram("dinv_dram", [NP], F32)
            p_hi = [ps(f"p_hi{m}", [P, W], F32, ctx) for m in range(2)]
            p_lo = [ps(f"p_lo{m}", [P, W], F32, ctx) for m in range(2)]
            p_new = [ps(f"p_new{m}", [P, W], F32, ctx) for m in range(2)]
            p_turn = [ps(f"l_p_turn{v}", [P, 2, P], F32, ctx) for v in range(2)]

            h1 = aggT[:].rearrange("p m n -> p (m n)").rearrange("p (t d) -> p t d", d=D)
            norm_scales("n2", x_sb)
            s_turned, s_taken, s_in, s_applied = sem("s_turned"), sem("s_taken"), sem("s_in"), sem("s_applied")
            with nc.Block() as block:
                @block.scalar
                def _(act):
                    apply_tiles(x_sb, h1, s_applied)

                @block.sync
                def _(sp):
                    sp.dma_start(dinv_dram.rearrange("(t p) -> p t", p=P), dinv[:]).then_inc(s_in, 16)
                    sp.wait_ge(s_in, 16)
                    sp.dma_start(dinv_rep[:], dinv_dram.partition_broadcast(P)).then_inc(s_in, 16)
                    for n, name in enumerate(("mlp_b", "bn_g", "bn_b")):
                        for m in range(2):
                            sp.dma_start(bn_tab[:, :, n, m], a[name].rearrange("l (m p) -> m p l", m=2)[m]).then_inc(s_in, 16)
                    sp.wait_ge(s_in, 16 * 8)

                @block.tensor
                def _(pe):
                    for t in range(NT):
                        if t >= 2:
                            pe.wait_ge(s_taken, t - 1)
                        pe.wait_ge(s_applied, t + 1)
                        for m in range(2):
                            k = nc.tensor.transpose(p_turn[t % 2][:, m, :], h1[:, t, m * P:(m + 1) * P], ident[:])
                        k.then_inc(s_turned, 1)
                    for t in range(NT):
                        pe.wait_ge(s_taken, NT + t - 1 if t else NT)
                        nc.tensor.transpose(p_turn[t % 2][0:4, 0, :], F_sb[:, t, :], ident[:]).then_inc(s_turned, 1)

                @block.vector
                def _(dve):
                    nc.vector.memset(zero_rows[:], 0.0)
                    nc.vector.memset(bn_rs[:, 1, :], 1.0)
                    nc.vector.memset(bn_rs[:, 2, :], 0.0)
                    nc.vector.memset(ewslot[:], 0.0)
                    for t in range(NT):
                        dve.wait_ge(s_turned, t + 1)
                        nc.vector.tensor_copy(hT[:, :, t * P:(t + 1) * P], p_turn[t % 2][:]).then_inc(s_taken, 1)
                    for t in range(NT):
                        dve.wait_ge(s_turned, NT + t + 1)
                        nc.vector.tensor_copy(FT[:, t * P:(t + 1) * P], p_turn[t % 2][0:4, 0, :]).then_inc(s_taken, 1)

            (turned, rest_ready, high_ready, low_ready, sums, low_out, agg_ready, news, new_ready, chunk_used, scales_ready,
             var_ready, root_ready, bn_order, scaled, w_loaded, w_used) = (sem("l_" + x) for x in (
                 "turned", "rest_ready", "high_ready", "low_ready", "sums", "low_out", "agg_ready", "news", "new_ready", "chunk_used",
                 "scales_ready", "var_ready", "root_ready", "bn_order", "scaled", "w_loaded", "w_used"))
            halfway, halfway2, sums_zeroed = sem("l_halfway"), sem("l_halfway2"), sem("l_sums_zeroed")
            chunk_in = [sem(f"l_chunk_in{q}") for q in range(2)]

            def load_chunk(sp, l, i, q):
                sp.wait_ge(chunk_used, l * NC + i * 2 + q + 1)
                sp.nop().then_inc(waits_passed, 1)
                sp.dma_start(cbuf[q][:], by_src.rearrange("(k p) n -> p k n", p=P)[:, :, bass.ds((i * 2 + q) * W, W)]).then_inc(chunk_in[q], 16)

            def aggregate(pe, l, c, q):
                pe.wait_ge(chunk_in[q], l * (16 * NC // 2) + (c - q) * 8 + 16)
                for m in range(2):
                    pe.wait_ge(agg_ready, l * (2 * NC) + c * 2 + m + 1)
                    for k in range(NT):
                        nc.tensor.matmul(p_lo[m][:], parts[:, k, m, 1, :], cbuf[q][:, k, :], start=(k == 0), stop=(k == NT - 1))
                        nc.tensor.matmul(p_hi[m][:], parts[:, k, m, 0, :], cbuf[q][:, k, :], start=(k == 0), stop=False)
                    nc.tensor.matmul(p_hi[m][:], ewslot[:, m * P:(m + 1) * P], FT[:, bass.ds(c * W, W)],
                                     start=False, stop=True).then_inc(sums, 1)

            def take_low(act, l, c):
                for m in range(2):
                    act.wait_ge(sums, l * (2 * NC) + c * 2 + m + 1)
                    act.wait_ge(agg_ready, l * (2 * NC) + c * 2 + m + 1)
                    nc.scalar.mul(low_sb[m][:], p_lo[m][:], 1.0 / LO).then_inc(low_out, 1)
                act.nop().then_inc(chunk_used, 1)

            def sum_up(dve, l, c):
                for m in range(2):
                    dve.wait_ge(low_out, l * (2 * NC) + c * 2 + m + 1)
                    part = aggT[:, m, bass.ds(c * W, W)]
                    nc.vector.tensor_tensor(part, p_hi[m][:], low_sb[m][:], ALU.add).then_inc(halfway, 1)
                    dve.wait_ge(halfway, l * (2 * NC) + c * 2 + m + 1)
                    nc.vector.tensor_tensor(part, part, dinv_rep[:, bass.ds(c * W, W)], ALU.mult).then_inc(agg_ready, 1)

            with nc.Block() as block:
                @block.sync
                def _(sp):
                    with sp.Fori(0, LAYERS) as l:
                        for q in range(2):
                            load_chunk(sp, l, 0, q)
                        sp.wait_ge(w_used, l + 1)
                        sp.nop().then_inc(waits_passed, 1)
                        sp.dma_start(wslot[:], a["mlp_w"][bass.ds(l, 1)].rearrange("l (k p) d -> p (l k) d", p=P)).then_inc(w_loaded, 16)
                        sp.dma_start(ewslot[0:3, P:D], a["ew2"][bass.ds(l, 1)].rearrange("l c d -> (l c) d")).then_inc(w_loaded, 16)
                        sp.dma_start(ewslot[3:4, 0:P], a["ew1"][bass.ds(l, 1)].rearrange("l c d -> (l c) d")).then_inc(w_loaded, 16)
                        with sp.Fori(1, NC // 2) as i:
                            for q in range(2):
                                load_chunk(sp, l, i, q)

                @block.gpsimd
                def _(pool):
                    for n in range(RS):
                        rows = sums_dram[n].rearrange("(p r) d -> p (r d)", p=P)
                        for piece in range(PIECES):
                            pool.dma_start(rows[:, piece * 2 * D:(piece + 1) * 2 * D], zero_rows[:]).then_inc(sums_zeroed, 16)
                    pool.wait_ge(sums_zeroed, 16 * RS * PIECES)

                @block.tensor
                def _(pe):
                    pe.nop().then_inc(chunk_used, 2)

                    def layer_product(l, c):
                        pe.wait_ge(agg_ready, l * (2 * NC) + c * 2 + 4)
                        for m in range(2):
                            pe.wait_ge(new_ready, l * (2 * NC) + c * 2 + m + 1)
                            for k in range(4):
                                state = (hT if k < 2 else aggT)[:, k % 2, bass.ds(c * W, W)]
                                r = nc.tensor.matmul(p_new[m][:], wslot[:, k, m * P:(m + 1) * P], state, start=(k == 0), stop=(k == 3))
                            r.then_inc(news, 1)

                    with pe.Fori(0, LAYERS) as l:
                        for t in range(NT + LAG):
                            if t < NT:
                                if t % PT == 0:
                                    pe.wait_ge(scaled, l * (NT // PT) + t // PT + 1)
                                pe.wait_ge(rest_ready, l * NT + t + 1)
                                for m in range(2):
                                    r = nc.tensor.transpose(p_turn[t % 2][:, m, :], hT[:, m, t * P:(t + 1) * P], ident[:])
                                r.then_inc(turned, 1)
                            k = t - LAG
                            if k == 0:
                                pe.wait_ge(chunk_in[0], l * (16 * NC // 2) + 16)
                                pe.wait_ge(agg_ready, l * (2 * NC) + 2)
                            if k >= 0:
                                pe.wait_ge(low_ready, l * NT + k + 1)
                                for m in range(2):
                                    nc.tensor.matmul(p_lo[m][:], parts[:, k, m, 1, :], cbuf[0][:, k, :], start=(k == 0), stop=(k == NT - 1))
                                    nc.tensor.matmul(p_hi[m][:], parts[:, k, m, 0, :], cbuf[0][:, k, :], start=(k == 0), stop=False)
                        pe.wait_ge(w_loaded, l * 48 + 48)
                        for m in range(2):
                            nc.tensor.matmul(p_hi[m][:], ewslot[:, m * P:(m + 1) * P], FT[:, 0:W], start=False, stop=True).then_inc(sums, 1)
                        with pe.Fori(0, NC // 2 - 1) as i:
                            for q in (1, 0):
                                c = i * 2 + (1 if q else 2)
                                aggregate(pe, l, c, q)
                                layer_product(l, c - 1)
                        aggregate(pe, l, NC - 1, 1)
                        layer_product(l, NC - 2)
                        layer_product(l, NC - 1)

                @block.scalar
                def _(act):
                    act.nop().then_inc(new_ready, 2)

                    def take_new(l, c):
                        act.wait_ge(news, l * (2 * NC) + c * 2 + 2)
                        act.nop().then_inc(waits_passed, 1)
                        for m in range(2):
                            nc.scalar.activation(hT[:, m, bass.ds(c * W, W)], p_new[m][:], ACT.Relu,
                                                 bias=bn_tab[:, bass.ds(l, 1), 0, m]).then_inc(new_ready, 1)

                    def norm_piece(piece):
                        own = slice(piece * PT * P, (piece + 1) * PT * P)
                        for m in range(2):
                            r = nc.scalar.activation(hT[:, m, own], hT[:, m, own], ACT.Relu, bias=bn_rs[:, 2, m:m + 1],
                                                     scale=bn_rs[:, 1, m:m + 1])
                        r.then_inc(scaled, 1)

                    with act.Fori(0, LAYERS) as l:
                        act.wait_ge(scales_ready, l + 1)
                        norm_piece(0)
                        for t in range(NT + 1):
                            if t % PT == 0 and t // PT + 1 < NT // PT:
                                norm_piece(t // PT + 1)
                            if t < NT:
                                act.wait_ge(turned, l * NT + t + 1)
                                nc.scalar.activation(parts[:, t, :, 0, :], p_turn[t % 2][:], ACT.Copy, scale=dinv[:, t:t + 1]).then_inc(high_ready, 1)
                            if t > 0:
                                act.wait_ge(rest_ready, l * NT + t + 2)
                                nc.scalar.mul(parts[:, t - 1, :, 1, :], rest[(t - 1) % 2][:], LO).then_inc(low_ready, 1)
                        take_low(act, l, 0)
                        with act.Fori(0, NC // 2 - 1) as i:
                            for q in (1, 0):
                                c = i * 2 + (1 if q else 2)
                                take_low(act, l, c)
                                take_new(l, c - 1)
                        take_low(act, l, NC - 1)
                        take_new(l, NC - 2)
                        take_new(l, NC - 1)
                        act.wait_ge(var_ready, l + 1)
                        nc.scalar.activation(bn_rs[:, 0, :], bn_rs[:, 3, :], ACT.Sqrt).then_inc(root_ready, 1)
                    act.wait_ge(scales_ready, LAYERS + 1)
                    for m in range(2):
                        nc.scalar.activation(hT[:, m, :], hT[:, m, :], ACT.Identity, bias=bn_rs[:, 2, m:m + 1], scale=bn_rs[:, 1, m:m + 1])

                @block.vector
                def _(dve):
                    TT, TS, STT = nc.vector.tensor_tensor, nc.vector.tensor_scalar, nc.vector.scalar_tensor_tensor
                    dve.nop().then_inc(rest_ready, 2)
                    dve.nop().then_inc(w_used, 1)
                    dve.nop().then_inc(scales_ready, 1)
                    dve.nop().then_inc(agg_ready, 2)
                    o = Order(dve, bn_order)

                    o.begin(4)
                    with dve.Fori(0, LAYERS) as l:
                        o.enter(l)
                        for t in range(NT):
                            dve.wait_ge(high_ready, l * NT + t + 1)
                            if t >= 2:
                                dve.wait_ge(low_ready, l * NT + t - 1)
                            STT(rest[t % 2][:], p_turn[t % 2][:], dinv[:, t:t + 1], parts[:, t, :, 0, :], ALU.mult, ALU.subtract).then_inc(rest_ready, 1)
                        with dve.Fori(0, NC) as c:
                            sum_up(dve, l, c)
                        for c in range(NC):
                            for m in range(2):
                                if c % 2 == 0:
                                    dve.wait_ge(new_ready, l * (2 * NC) + c * 2 + 2 + 4) if m == 0 else None
                                n = min(W, N - c * W)
                                k = nc.vector.bn_stats(bn_raw[:, m, c, :], hT[:, m, c * W:c * W + n])
                        o.link(k)
                        dve.nop().then_inc(waits_passed, 1)
                        for m in range(2):
                            k = nc.vector.bn_aggr(bn_mv[:, m, :], bn_raw[:, m].rearrange("p c s -> p (c s)"))
                        o.link(k)
                        o.link(TS(bn_rs[:, 3, :], bn_mv[:, :, 1], EPS, None, ALU.add))
                        dve.nop().then_inc(var_ready, 1)
                        dve.wait_ge(root_ready, l + 1)
                        gain, offset = (bn_tab[:, bass.ds(l, 1), n, :].rearrange("p o m -> p (o m)") for n in (1, 2))
                        nc.vector.reciprocal(bn_rs[:, 1, :], bn_rs[:, 0, :]).then_inc(halfway2, 1)
                        dve.wait_ge(halfway2, l * 3 + 1)
                        TT(bn_rs[:, 1, :], bn_rs[:, 1, :], gain, ALU.mult).then_inc(halfway2, 1)
                        dve.wait_ge(halfway2, l * 3 + 2)
                        TT(bn_rs[:, 2, :], bn_mv[:, :, 0], bn_rs[:, 1, :], ALU.mult).then_inc(halfway2, 1)
                        dve.wait_ge(halfway2, l * 3 + 3)
                        o.link(TT(bn_rs[:, 2, :], offset, bn_rs[:, 2, :], ALU.subtract))
                        dve.nop().then_inc(scales_ready, 1)
                        dve.nop().then_inc(w_used, 1)

            with nc.Block() as block:
                @block.tensor
                def _(pe):
                    for t in range(NT):
                        if t >= 2:
                            pe.wait_ge(s_taken, 2 * NT + t - 1)
                        for m in range(2):
                            k = nc.tensor.transpose(p_turn[t % 2][:, m, :], hT[:, m, t * P:(t + 1) * P], ident[:])
                        k.then_inc(s_turned, 1)

                @block.vector
                def _(dve):
                    for t in range(NT):
                        dve.wait_ge(s_turned, 2 * NT + t + 1)
                        nc.vector.tensor_tensor(x_sb[:, t, :].rearrange("p (m d) -> p m d", m=2), x_sb[:, t, :].rearrange("p (m d) -> p m d", m=2),
                                                p_turn[t % 2][:], ALU.add).then_inc(s_taken, 1)
        end_stage()

        with ExitStack() as ctx:
            hx = sb("hx", [P, NT, D], F32, ctx)
            hxT = sb("hxT", [P, 2, NP], F32, ctx)
            hw_parts = sb("hw_parts", [P, NT, 2, D], F16, ctx)
            low_sb = [sb(f"g_low{q}", [P, D], F32, ctx) for q in range(2)]
            sum_sb = [sb(f"g_sum{q}", [P, D], F32, ctx) for q in range(2)]
            rest = [sb(f"g_rest{q}", [P, D], F32, ctx) for q in range(2)]
            rows = [sb(f"g_rows{q}", [P, NP], F16, ctx) for q in range(2)]
            rowsT = [sb(f"g_rowsT{q}", [P, NT, P], F16, ctx) for q in range(2)]
            gw = sb("gw", [P, 2, D], F32, ctx)
            g_brow = sb("g_brow", [P, D], F32, ctx)
            inv_deg = sb("inv_deg", [P, NT], F32, ctx)
            has_deg = sb("has_deg", [P, NT], F32, ctx)
            p_turn = [ps(f"g_p_turn{v}", [P, 2, P], F32, ctx) for v in range(2)]
            p_prod = [ps(f"g_p_prod{v}", [P, D], F32, ctx) for v in range(2)]
            p_block = [ps(f"g_p_block{v}", [P, 5, P], F16, ctx) for v in range(2)]
            p_conv = [ps(f"g_p_conv{v}", [P, 2, D], F32, ctx) for v in range(2)]
            norm_scales("n3", x_sb)
            applied = sem("g_applied")
            (g_in, g_order, turned, taken, products, hw_ready, high_ready, rest_ready, low_ready, blocks, blocks_out, conv_ready, low_out,
             x_added) = (sem("g_" + x) for x in (
                 "in", "order", "turned", "taken", "products", "hw_ready", "high_ready", "rest_ready", "low_ready", "blocks", "blocks_out",
                 "conv_ready", "low_out", "x_added"))
            rows_in = [sem(f"g_rows_in{q}") for q in range(2)]
            with nc.Block() as block:
                @block.sync
                def _(sp):
                    sp.dma_start(gw[:], a["L2_W"].rearrange("(k p) d -> p k d", k=2)).then_inc(g_in, 16)
                    sp.dma_start(g_brow[:], a["L2_b"].partition_broadcast(P)).then_inc(g_in, 16)

                @block.tensor
                def _(pe):
                    def turn(t):
                        if t >= 2:
                            pe.wait_ge(taken, t - 1)
                        pe.wait_ge(applied, t + 1)
                        for m in range(2):
                            k = nc.tensor.transpose(p_turn[t % 2][:, m, :], hx[:, t, m * P:(m + 1) * P], ident[:])
                        k.then_inc(turned, 1)

                    turn(0)
                    pe.wait_ge(g_in, 32)
                    for t in range(NT):
                        if t + 1 < NT:
                            turn(t + 1)
                        pe.wait_ge(taken, t + 1)
                        if t >= 2:
                            pe.wait_ge(hw_ready, t - 1)
                        for k in range(2):
                            r = nc.tensor.matmul(p_prod[t % 2][:], hxT[:, k, t * P:(t + 1) * P], gw[:, k, :], start=(k == 0), stop=(k == 1))
                        r.then_inc(products, 1)

                @block.scalar
                def _(act):
                    apply_tiles(x_sb, hx, applied)
                    for t in range(NT + 1):
                        if t < NT:
                            act.wait_ge(hw_ready, t + 1)
                            nc.scalar.copy(hw_parts[:, t, 0, :], hx[:, t, :]).then_inc(high_ready, 1)
                        if t > 0:
                            act.wait_ge(rest_ready, t)
                            nc.scalar.mul(hw_parts[:, t - 1, 1, :], rest[(t - 1) % 2][:], LO).then_inc(low_ready, 1)

                @block.vector
                def _(dve):
                    o = Order(dve, g_order)
                    o.did(nc.vector.tensor_scalar(has_deg[:], degsrc[:], 0.5, None, ALU.is_ge))
                    o.link(nc.vector.tensor_scalar(inv_deg[:], degsrc[:], 1.0, None, ALU.max))
                    o.link(nc.vector.reciprocal(inv_deg[:], inv_deg[:]))
                    nc.vector.tensor_tensor(inv_deg[:], inv_deg[:], has_deg[:], ALU.mult)

                    def take(t):
                        dve.wait_ge(turned, t + 1)
                        nc.vector.tensor_copy(hxT[:, :, t * P:(t + 1) * P], p_turn[t % 2][:]).then_inc(taken, 1)

                    def leave_rest(t):
                        dve.wait_ge(high_ready, t + 1)
                        if t >= 2:
                            dve.wait_ge(low_ready, t - 1)
                        nc.vector.tensor_tensor(rest[t % 2][:], hx[:, t, :], hw_parts[:, t, 0, :], ALU.subtract).then_inc(rest_ready, 1)

                    take(0)
                    dve.wait_ge(g_in, 32)
                    for t in range(NT):
                        if t + 1 < NT:
                            take(t + 1)
                        dve.wait_ge(products, t + 1)
                        nc.vector.tensor_tensor(hx[:, t, :], p_prod[t % 2][:], g_brow[:], ALU.add).then_inc(hw_ready, 1)
                        if t > 0:
                            leave_rest(t - 1)
                    leave_rest(NT - 1)

            with nc.Block() as block:
                def source_tiles(engine, work):
                    with engine.Fori(0, NT // 2) as i:
                        for q in range(2):
                            work(i * 2 + q, q, i)

                @block.sync
                def _(sp):
                    def load(t, q, i):
                        sp.wait_ge(blocks, t * 5 + 5)
                        sp.nop().then_inc(waits_passed, 1)
                        sp.dma_start(rows[q][:], by_src[bass.ds(t * P, P), :]).then_inc(rows_in[q], 16)

                    source_tiles(sp, load)
                    load(NT - 1, 0, 0)

                @block.tensor
                def _(pe):
                    pe.nop().then_inc(blocks, 10)

                    def turn(t, q, b):
                        pe.wait_ge(blocks_out, t * 5 + b + 1)
                        for k in range(5):
                            m = nc.tensor.transpose(p_block[(b + q) % 2][:, k, :], rows[q][:, (b * 5 + k) * P:(b * 5 + k + 1) * P], ident16[:])
                        m.then_inc(blocks, 1)

                    def convolve(q, b):
                        for k in range(b * 5, b * 5 + 5):
                            m = nc.tensor.matmul(p_conv[q][:].rearrange("p n d -> p (n d)"), rowsT[q][:, k, :],
                                                 hw_parts[:, k].rearrange("p n d -> p (n d)"), start=(k == 0), stop=(k == NT - 1))
                        return m

                    def work(t, q, i):
                        ahead = not (isinstance(t, int) and t == NT - 1)
                        if ahead:
                            pe.wait_ge(rows_in[1 - q], (i + q) * 16 + 16)
                        pe.wait_ge(blocks_out, t * 5 + 7)
                        pe.wait_ge(x_added, t + 1)
                        for b in range(5):
                            if ahead:
                                turn(t + 1, 1 - q, b)
                            m = convolve(q, b)
                        m.then_inc(conv_ready, 1)

                    pe.wait_ge(rows_in[0], 16)
                    for b in range(5):
                        turn(0, 0, b)
                    source_tiles(pe, work)
                    work(NT - 1, 0, 0)

                @block.scalar
                def _(act):
                    def low_sums(t, q, i):
                        act.wait_ge(conv_ready, t + 1)
                        act.wait_ge(x_added, t + 1)
                        nc.scalar.mul(low_sb[q][:], p_conv[q][:, 1, :], 1.0 / LO).then_inc(low_out, 1)

                    source_tiles(act, low_sums)
                    low_sums(NT - 1, 0, 0)

                @block.vector
                def _(dve):
                    dve.nop().then_inc(blocks_out, 2)
                    dve.nop().then_inc(x_added, 2)
                    o = Order(dve, g_order)
                    o.base = 3

                    def take(t, q):
                        for b in range(5):
                            dve.wait_ge(blocks, t * 5 + b + 11)
                            nc.vector.tensor_copy(rowsT[q][:, b * 5:b * 5 + 5, :], p_block[(b + q) % 2][:]).then_inc(blocks_out, 1)

                    def finish(t, q):
                        dve.wait_ge(low_out, t + 1)
                        o.link(nc.vector.tensor_tensor(sum_sb[q][:], p_conv[q][:, 0, :], low_sb[q][:], ALU.add))
                        own = x_sb[:, bass.ds(t, 1), :].rearrange("p o d -> p (o d)")
                        nc.vector.scalar_tensor_tensor(own, sum_sb[q][:], column(inv_deg, t), own, ALU.mult, ALU.add).then_inc(x_added, 1)

                    def work(t, q, i):
                        o.enter(t)
                        take(t + 1, 1 - q)
                        finish(t, q)

                    take(0, 0)
                    o.begin(1)
                    source_tiles(dve, work)
                    o.leave(NT - 1)
                    finish(NT - 1, 0)
        end_stage()

        with ExitStack() as ctx:
            h3 = sb("h3", [P, NT, D], F32, ctx)
            h3T = sb("h3T", [P, 2, NP], F32, ctx)
            m_in = sem("m_in")
            norm_scales("n4", x_sb)

            src_dram = dram("src_dram", [NP, D], F32)
            with ExitStack() as inner:
                dst_part = sb("dst_part", [P, NT, D], F32, inner)
                attr_w = sb("attr_w", [ED, D], F32, inner)
                with ExitStack() as inmost:
                    node_w = sb("node_w", [P, 4, D], F32, inmost)
                    m_brow = sb("m_brow", [P, D], F32, inmost)
                    src_part = sb("src_part", [P, NT, D], F32, inmost)
                    p_turn = [ps(f"m_p_turn{v}", [P, 2, P], F32, inmost) for v in range(2)]
                    p_parts = [[ps(f"m_p_parts{v}{n}", [P, D], F32, inmost) for n in range(2)] for v in range(2)]
                    applied, turned, taken, products, src_ready, dst_ready, src_out = (
                        sem("m_" + x) for x in ("applied", "turned", "taken", "products", "src_ready", "dst_ready", "src_out"))
                    with nc.Block() as block:
                        @block.sync
                        def _(sp):
                            sp.dma_start(node_w[:], a["m_W1T"][0:2 * D].rearrange("(k p) d -> p k d", p=P)).then_inc(m_in, 16)
                            sp.dma_start(attr_w[:], a["m_W1T"][2 * D:]).then_inc(m_in, 16)
                            sp.dma_start(m_brow[:], a["m_b1"].partition_broadcast(P)).then_inc(m_in, 16)
                            for part in range(5):
                                sp.wait_ge(src_ready, (part + 1) * 5)
                                sp.dma_start(src_dram.rearrange("(t p) d -> p t d", p=P)[:, part * 5:part * 5 + 5, :],
                                             src_part[:, part * 5:part * 5 + 5, :]).then_inc(src_out, 16)
                            sp.wait_ge(src_out, 80)

                        @block.tensor
                        def _(pe):
                            def turn(t):
                                if t >= 2:
                                    pe.wait_ge(taken, t - 1)
                                pe.wait_ge(applied, t + 1)
                                for m in range(2):
                                    k = nc.tensor.transpose(p_turn[t % 2][:, m, :], h3[:, t, m * P:(m + 1) * P], ident[:])
                                k.then_inc(turned, 1)

                            turn(0)
                            pe.wait_ge(m_in, 48)
                            for t in range(NT):
                                if t + 1 < NT:
                                    turn(t + 1)
                                pe.wait_ge(taken, t + 1)
                                if t >= 2:
                                    pe.wait_ge(src_ready, t - 1)
                                    pe.wait_ge(dst_ready, t - 1)
                                for n in range(2):
                                    for k in range(2):
                                        r = nc.tensor.matmul(p_parts[t % 2][n][:], h3T[:, k, t * P:(t + 1) * P], node_w[:, 2 * n + k, :],
                                                             start=(k == 0), stop=(k == 1))
                                r.then_inc(products, 1)

                        @block.scalar
                        def _(act):
                            apply_tiles(x_sb, h3, applied)
                            for t in range(NT):
                                act.wait_ge(products, t + 1)
                                nc.scalar.copy(dst_part[:, t, :], p_parts[t % 2][1][:]).then_inc(dst_ready, 1)

                        @block.vector
                        def _(dve):
                            def take(t):
                                dve.wait_ge(turned, t + 1)
                                nc.vector.tensor_copy(h3T[:, :, t * P:(t + 1) * P], p_turn[t % 2][:]).then_inc(taken, 1)

                            take(0)
                            dve.wait_ge(m_in, 48)
                            for t in range(NT):
                                if t + 1 < NT:
                                    take(t + 1)
                                dve.wait_ge(products, t + 1)
                                nc.vector.tensor_tensor(src_part[:, t, :], p_parts[t % 2][0][:], m_brow[:], ALU.add).then_inc(src_ready, 1)

                msg_step = sb("msg_step", [P, S], F32, inner)
                own_row = sb("own_row", [P, 1], F32, inner)
                idx = [sb(f"m_idx{q}", [P, 4], I32, inner) for q in range(2)]
                src_rows = [sb(f"src_rows{q}", [P, 4, D], F32, inner) for q in range(2)]
                msg = [sb(f"m_msg{q}", [P, 4, D], F32, inner) for q in range(2)]
                attrT = [sb(f"attrT{q}", [ED, 4, P], F32, inner) for q in range(2)]
                pair = [sb(f"pair{q}", [P, 4, 2, P], F32, inner) for q in range(2)]
                hotT = [sb(f"m_hotT{q}", [P, 4, P], F32, inner) for q in range(2)]
                same = [sb(f"m_same{q}", [P, 4, P], F32, inner) for q in range(2)]
                earlier = sb("m_earlier", [P, 4, P], F32, inner)
                prior = sb("m_prior", [P, 4], F32, inner)
                place_f = sb("m_place_f", [P, 4], F32, inner)
                place = [sb(f"m_place{q}", [P, 4], I32, inner) for q in range(2)]
                merged = [sb(f"merged{q}", [P, 4, D], F32, inner) for q in range(2)]
                valid = sb("m_valid", [P, S], F32, inner)
                p_pre = [ps(f"p_pre{q}", [P, 4, D], F32, inner) for q in range(2)]
                p_merged = [ps(f"p_merged{q}", [P, 4, D], F32, inner) for q in range(2)]
                (m_order, loop_order, idx_ready, hot_ready, place_ready, pair_used, pre_done, pre_added, msg_ready, merge_done, out_ready,
                 places_free) = (sem("e_" + x) for x in (
                     "order", "loop_order", "idx_ready", "hot_ready", "place_ready", "pair_used", "pre_done", "pre_added", "msg_ready", "merge_done",
                     "out_ready", "places_free"))
                rows_in = [sem(f"e_rows_in{q}") for q in range(2)]
                edges_in = [sem(f"e_edges_in{q}") for q in range(2)]
                landed = [sem(f"e_landed{n}") for n in range(RS)]
                with nc.Block() as block:
                    @block.vector
                    def _(dve):
                        o = Order(dve, m_order)
                        TS, STT = nc.vector.tensor_scalar, nc.vector.scalar_tensor_tensor
                        o.did(TS(own_row[:], pidx[:], float(NP), None, ALU.add))
                        o.did(TS(valid[:], dl_step[:], 0.0, None, ALU.is_ge))
                        o.link(nc.vector.tensor_copy(msg_step[:], src_step[:]))
                        o.link(STT(valid[:], dl_step[:], float(P), valid[:], ALU.is_lt, ALU.mult))
                        o.link(TS(msg_step[:], msg_step[:], own_row[:, 0:1], None, ALU.subtract))
                        o.link(nc.vector.tensor_tensor(msg_step[:], msg_step[:], valid[:], ALU.mult))
                        TS(msg_step[:], msg_step[:], own_row[:, 0:1], None, ALU.add)

                with nc.Block() as block:
                    def groups(engine, work):
                        def pair_of(i):
                            work(i * 2, 0, i)
                            work(i * 2 + 1, 1, i)
                        looped(engine, G4 // 2 - 1, pair_of)

                    @block.sync
                    def _(sp):
                        def load_pair(i):
                            first = read_registers(nc, step_table, i * 8 + S, 8, ET.SP, (CH - 1) * P)
                            for q in range(2):
                                g = i * 2 + q
                                sp.wait_ge(pre_done, g + 1)
                                sp.wait_ge(pair_used, g + 1)
                                sp.nop().then_inc(waits_passed, 1)
                                sp.dma_start(pair[q][:].rearrange("p u n e -> p (u n e)"),
                                             pair_dram[bass.ds(g * 4, 4)].rearrange("s n e -> (s n e)").partition_broadcast(P)).then_inc(edges_in[q], 16)
                                for u in range(4):
                                    sp.dma_start(attrT[q][:, u, :], a["attr64T"][:, bass.ds(first[q * 4 + u], P)]).then_inc(edges_in[q], 16)

                        looped(sp, G4 // 2, load_pair)

                    @block.gpsimd
                    def _(pool):
                        def gather(g, q):
                            pool.wait_ge(idx_ready, g + 1)
                            pool.nop().then_inc(waits_passed, 1)
                            for u in range(4):
                                nc.gpsimd.indirect_dma_start(
                                    src_rows[q][:, u, :], None, src_dram,
                                    bass.IndirectOffsetOnAxis(ap=idx[q][:, u:u + 1].bitcast(U32), axis=0)).then_inc(rows_in[q], 16)

                        def scatter(g, q):
                            pool.wait_ge(place_ready, g + 1)
                            pool.wait_ge(out_ready, g + 3)
                            pool.nop().then_inc(waits_passed, 1)
                            for u in range(4):
                                nc.gpsimd.indirect_dma_start(
                                    sums_dram[u], bass.IndirectOffsetOnAxis(ap=place[q][:, u:u + 1].bitcast(U32), axis=0),
                                    merged[q][:, u, :], None, compute_op=ALU.add).then_inc(landed[u], 16)

                        def work(g, q, i):
                            pool.wait_ge(pre_added, g + 3)
                            gather(g + 2, q)
                            for n in range(RS):
                                pool.wait_ge(landed[n], g * 16)
                            pool.nop().then_inc(places_free, 1)
                            scatter(g, q)

                        gather(0, 0)
                        gather(1, 1)
                        groups(pool, work)
                        for g, q in ((G4 - 2, 0), (G4 - 1, 1)):
                            for n in range(RS):
                                pool.wait_ge(landed[n], g * 16)
                            pool.nop().then_inc(places_free, 1)
                            scatter(g, q)
                        for n in range(RS):
                            pool.wait_ge(landed[n], G4 * 16)

                    @block.scalar
                    def _(act):
                        act.nop().then_inc(out_ready, 2)

                        def indices(g, q):
                            nc.scalar.copy(idx[q][:], src_step[:, bass.ds(g * 4, 4)]).then_inc(idx_ready, 1)

                        def finish(g, q, ahead):
                            act.wait_ge(pre_added, g + 3)
                            if ahead:
                                indices(g + 2, q)
                            nc.scalar.activation(msg[q][:], msg[q][:], ACT.Relu).then_inc(msg_ready, 1)
                            act.wait_ge(merge_done, g + 3)
                            act.wait_ge(places_free, g)
                            nc.scalar.copy(merged[q][:], p_merged[q][:]).then_inc(out_ready, 1)

                        indices(0, 0)
                        indices(1, 1)
                        groups(act, lambda g, q, i: finish(g, q, True))
                        finish(G4 - 2, 0, False)
                        finish(G4 - 1, 1, False)

                    @block.tensor
                    def _(pe):
                        pe.nop().then_inc(pre_done, 2)
                        pe.nop().then_inc(merge_done, 2)

                        def products(g, q, i, tiles):
                            pe.wait_ge(edges_in[q], i * 80 + 80)
                            pe.wait_ge(hot_ready, g + 1)
                            pe.wait_ge(pre_added, g + 1)
                            for u in range(4):
                                nc.tensor.matmul(p_pre[q][:, u, :], hotT[q][:, u, :],
                                                 dst_part[:, bass.ds(tiles[u], 1), :].rearrange("p o d -> p (o d)"), start=True, stop=False)
                                r = nc.tensor.matmul(p_pre[q][:, u, :], attrT[q][:, u, :], attr_w[:], start=False, stop=True)
                            r.then_inc(pre_done, 1)

                        def merge(g, q):
                            pe.wait_ge(msg_ready, g + 1)
                            pe.wait_ge(place_ready, g + 1)
                            pe.wait_ge(out_ready, g + 1)
                            for u in range(4):
                                r = nc.tensor.matmul(p_merged[q][:, u, :], same[q][:, u, :], msg[q][:, u, :], start=True, stop=True)
                            r.then_inc(merge_done, 1)

                        def pair_of(i):
                            tiles = read_registers(nc, step_table, i * 8 + 4, 8, ET.PE, NT - 1)
                            products(i * 2 + 1, 1, i, tiles[0:4])
                            merge(i * 2, 0)
                            products(i * 2 + 2, 0, i + 1, tiles[4:8])
                            merge(i * 2 + 1, 1)

                        products(0, 0, 0, read_registers(nc, step_table, 0, 4, ET.PE, NT - 1))
                        looped(pe, G4 // 2 - 1, pair_of)
                        products(G4 - 1, 1, G4 // 2 - 1, read_registers(nc, step_table, S - 4, 4, ET.PE, NT - 1))
                        merge(G4 - 2, 0)
                        merge(G4 - 1, 1)

                    @block.vector
                    def _(dve):
                        TT, TS = nc.vector.tensor_tensor, nc.vector.tensor_scalar
                        o = Order(dve, loop_order)
                        dve.nop().then_inc(pair_used, 2)
                        dve.nop().then_inc(pre_added, 2)
                        spread = [P, 4, P]

                        def choose(g, q, i):
                            dve.wait_ge(edges_in[q], i * 80 + 80)
                            dve.wait_ge(pre_done, g + 1)
                            TS(hotT[q][:], pair[q][:, :, 0, :], pidx[:, 0:1], None, ALU.is_equal).then_inc(hot_ready, 1)
                            here = msg_step[:, bass.ds(g * 4, 4)]
                            dve.wait_ge(merge_done, g + 1)
                            o.link(TT(same[q][:], pair[q][:, :, 1, :], here.unsqueeze(2).broadcast_to(spread), ALU.is_equal))
                            dve.nop().then_inc(pair_used, 1)
                            o.link(TT(earlier[:], same[q][:], lower[:].unsqueeze(1).broadcast_to(spread), ALU.mult))
                            o.link(nc.vector.tensor_reduce(prior[:], earlier[:], AX.X, ALU.add))
                            o.link(TS(prior[:], prior[:], 0.5, None, ALU.is_lt))
                            o.link(TT(place_f[:], here, own_row[:].broadcast_to([P, 4]), ALU.subtract))
                            o.link(TT(place_f[:], place_f[:], prior[:], ALU.mult))

                        def choose_place(g, q):
                            dve.wait_ge(places_free, g)
                            TT(place[q][:], place_f[:], own_row[:].broadcast_to([P, 4]), ALU.add).then_inc(place_ready, 1)

                        def sum_parts(g, q, i):
                            dve.wait_ge(rows_in[q], i * 64 + 64)
                            dve.wait_ge(pre_done, g + 3)
                            dve.wait_ge(merge_done, g + 1)
                            for v in range(2):
                                k = TT(msg[q][:, 2 * v:2 * v + 2, :], src_rows[q][:, 2 * v:2 * v + 2, :], p_pre[q][:, 2 * v:2 * v + 2, :], ALU.add)
                            k.then_inc(pre_added, 1)

                        def work(g, q, i):
                            o.enter(g)
                            choose(g + 1, 1 - q, i + q)
                            sum_parts(g, q, i)
                            choose_place(g + 1, 1 - q)

                        choose(0, 0, 0)
                        choose_place(0, 0)
                        o.begin(6)
                        groups(dve, work)
                        o.leave(G4 - 2)
                        choose(G4 - 1, 1, G4 // 2 - 1)
                        sum_parts(G4 - 2, 0, G4 // 2 - 1)
                        choose_place(G4 - 1, 1)
                        sum_parts(G4 - 1, 1, G4 // 2 - 1)
            w2 = sb("m_w2", [P, 2, D], F32, ctx)
            wi = sb("m_wi", [P, 2, 3 * D], F32, ctx)
            wh = sb("m_wh", [P, 2, 3 * D], F32, ctx)
            b2 = sb("m_b2row", [P, D], F32, ctx)
            bi = sb("m_bi", [P, 3 * D], F32, ctx)
            bh = sb("m_bh", [P, 3 * D], F32, ctx)
            parts_in = [sb(f"parts_in{q}", [P, RS, D], F32, ctx) for q in range(2)]
            agg = [sb(f"u_agg{q}", [P, D], F32, ctx) for q in range(2)]
            aggT = [sb(f"u_aggT{q}", [P, 2, P], F32, ctx) for q in range(2)]
            agg2 = [sb(f"u_agg2{q}", [P, D], F32, ctx) for q in range(2)]
            agg2T = [sb(f"u_agg2T{q}", [P, 2, P], F32, ctx) for q in range(2)]
            hslot = [sb(f"u_hslot{q}", [P, 2, P], F32, ctx) for q in range(2)]
            gates = [sb(f"gates{q}", [P, 2 * D], F32, ctx) for q in range(2)]
            cand = [sb(f"cand{q}", [P, 2 * D], F32, ctx) for q in range(2)]
            p_t = [ps(f"u_p_t{q}", [P, 2, P], F32, ctx) for q in range(2)]
            p_2 = [ps(f"u_p_2{q}", [P, D], F32, ctx) for q in range(2)]
            p_rz = [ps(f"u_p_rz{q}", [P, 2 * D], F32, ctx) for q in range(2)]
            p_n = [ps(f"u_p_n{q}", [P, 2 * D], F32, ctx) for q in range(2)]
            (u_in, u_order, bias_ready, agg_ready, turns, copies, second, agg2_ready, slot_ready, gates_ps, rz_ready, rz_done, tanh_in,
             tanh_done, rows_ready, parts_free) = (sem("u_" + x) for x in (
                 "in", "order", "bias_ready", "agg_ready", "turns", "copies", "second", "agg2_ready", "slot_ready", "gates_ps", "rz_ready",
                 "rz_done", "tanh_in", "tanh_done", "rows_ready", "parts_free"))
            u_parts = [sem(f"u_parts{q}") for q in range(2)]
            stored = sem("stored")

            def each_tile(engine, work):
                def tiles_of(i):
                    for q in range(2):
                        work(i * 2 + q, q, i)
                looped(engine, NT // 2 - 1, tiles_of)
                for t in range(NT - 3, NT):
                    work(t, t % 2, t // 2)

            with nc.Block() as block:
                @block.sync
                def _(sp):
                    sp.dma_start(w2[:], a["m_W2T"].rearrange("(k p) d -> p k d", k=2)).then_inc(u_in, 16)
                    sp.dma_start(wi[:], a["m_W_ihT"].rearrange("(k p) d -> p k d", k=2)).then_inc(u_in, 16)
                    sp.dma_start(wh[:], a["m_W_hhT"].rearrange("(k p) d -> p k d", k=2)).then_inc(u_in, 16)
                    for name, row in (("m_b2", b2), ("m_b_ih", bi), ("m_b_hh", bh)):
                        sp.dma_start(row[:], a[name].partition_broadcast(P)).then_inc(u_in, 16)

                    def load(t, q, i):
                        sp.wait_ge(parts_free, t)
                        sp.nop().then_inc(waits_passed, 1)
                        for n in range(RS):
                            sp.dma_start(parts_in[q][:, n, :], sums_dram[n][bass.ds(t * P, P), :]).then_inc(u_parts[q], 16)

                    each_tile(sp, load)

                @block.gpsimd
                def _(pool):
                    def store(t, q, i):
                        pool.wait_ge(rows_ready, t + 1)
                        pool.nop().then_inc(waits_passed, 1)
                        pool.dma_start(out[bass.ds(t * P, P), :], x_sb[:, bass.ds(t, 1), :].rearrange("p o d -> p (o d)")).then_inc(stored, 16)

                    with pool.Fori(0, NT - 1) as t:
                        store(t, 0, 0)
                    pool.wait_ge(rows_ready, NT)
                    pool.dma_start(out[(NT - 1) * P:N, :], x_sb[0:N - (NT - 1) * P, NT - 1, :]).then_inc(stored, 16)
                    pool.wait_ge(stored, 16 * NT)

                @block.tensor
                def _(pe):
                    pe.wait_ge(u_in, 96)

                    def turn(g, q, n, source):
                        for m in range(2):
                            r = nc.tensor.transpose(p_t[n][:, m, :], source[q][:, m * P:(m + 1) * P], ident[:])
                        r.then_inc(turns, 1)

                    def output_product(q):
                        for k in range(2):
                            r = nc.tensor.matmul(p_2[q][:], aggT[q][:, k, :], w2[:, k, :], start=(k == 0), stop=(k == 1))
                        r.then_inc(second, 1)

                    pe.wait_ge(agg_ready, 1)
                    turn(0, 0, 0, agg)
                    pe.wait_ge(copies, 1)
                    output_product(0)
                    pe.wait_ge(agg2_ready, 2)
                    turn(0, 0, 1, agg2)

                    def work(t, q, i):
                        ahead = not (isinstance(t, int) and t == NT - 1)
                        if ahead:
                            pe.wait_ge(agg_ready, t + 2)
                            pe.wait_ge(copies, t * 2 + 1)
                            turn(t + 1, 1 - q, 0, agg)
                        pe.wait_ge(slot_ready, t + 1)
                        pe.wait_ge(rz_ready, t)
                        pe.wait_ge(tanh_in, t)
                        for k in range(2):
                            nc.tensor.matmul(p_rz[q][:], hslot[q][:, k, :], wh[:, k, 0:2 * D], start=(k == 0), stop=False)
                        for k in range(2):
                            nc.tensor.matmul(p_n[q][:, D:], hslot[q][:, k, :], wh[:, k, 2 * D:], start=(k == 0), stop=(k == 1))
                        pe.wait_ge(copies, t * 2 + 2)
                        if ahead:
                            pe.wait_ge(copies, t * 2 + 3)
                            pe.wait_ge(agg2_ready, t + 1)
                            output_product(1 - q)
                        for k in range(2):
                            nc.tensor.matmul(p_rz[q][:], agg2T[q][:, k, :], wi[:, k, 0:2 * D], start=False, stop=(k == 1))
                        if ahead:
                            pe.wait_ge(agg2_ready, t + 3)
                            turn(t + 1, 1 - q, 1, agg2)
                        for k in range(2):
                            r = nc.tensor.matmul(p_n[q][:, 0:D], agg2T[q][:, k, :], wi[:, k, 2 * D:], start=(k == 0), stop=(k == 1))
                        r.then_inc(gates_ps, 1)

                    each_tile(pe, work)

                @block.scalar
                def _(act):
                    act.nop().then_inc(gates_ps, 1)

                    def take_first(t, q):
                        nc.scalar.copy(hslot[q][:], h3T[:, :, bass.ds(t * P, P)]).then_inc(slot_ready, 1)
                        act.wait_ge(turns, t * 2 + 1)
                        nc.scalar.copy(aggT[q][:], p_t[0][:]).then_inc(copies, 1)

                    def take_second(t, q):
                        act.wait_ge(turns, t * 2 + 2)
                        nc.scalar.copy(agg2T[q][:], p_t[1][:]).then_inc(copies, 1)

                    def work(t, q, i):
                        left = NT - t if isinstance(t, int) else NT
                        if left > 1:
                            take_second(t + 1, 1 - q)
                        act.wait_ge(rz_ready, t + 2)
                        nc.scalar.activation(gates[q][:], gates[q][:], ACT.Sigmoid).then_inc(rz_done, 1)
                        if left > 2:
                            take_first(t + 2, q)
                        act.wait_ge(tanh_in, t + 2)
                        nc.scalar.activation(cand[q][:, 0:D], cand[q][:, 0:D], ACT.Tanh).then_inc(tanh_done, 1)

                    take_first(0, 0)
                    take_second(0, 0)
                    take_first(1, 1)
                    each_tile(act, work)

                @block.vector
                def _(dve):
                    TT, STT = nc.vector.tensor_tensor, nc.vector.scalar_tensor_tensor
                    o = Order(dve, u_order)
                    for s in (parts_free, agg2_ready, rz_ready, tanh_in):
                        dve.nop().then_inc(s, 1)
                    dve.wait_ge(u_in, 96)
                    o.link(TT(bh[:, 0:2 * D], bh[:, 0:2 * D], bi[:, 0:2 * D], ALU.add))

                    def add_parts(t, q, i):
                        dve.wait_ge(u_parts[q], i * (16 * RS) + 16 * RS)
                        o.link(TT(parts_in[q][:, 0:2, :], parts_in[q][:, 0:2, :], parts_in[q][:, 2:4, :], ALU.add))
                        TT(agg[q][:], parts_in[q][:, 0, :], parts_in[q][:, 1, :], ALU.add).then_inc(agg_ready, 1)
                        dve.wait_ge(agg_ready, t + 1)
                        dve.nop().then_inc(parts_free, 1)

                    def add_bias(t, q):
                        dve.wait_ge(second, t + 1)
                        STT(agg2[q][:], b2[:], column(degsrc, t), p_2[q][:], ALU.mult, ALU.add).then_inc(agg2_ready, 1)

                    def work(t, q, i):
                        o.enter(t)
                        left = NT - t if isinstance(t, int) else NT
                        if left > 1:
                            add_bias(t + 1, 1 - q)
                        if left > 2:
                            add_parts(t + 2, q, i + 1)
                        dve.wait_ge(gates_ps, t + 2)
                        TT(gates[q][:], p_rz[q][:], bh[:, 0:2 * D], ALU.add).then_inc(rz_ready, 1)
                        TT(cand[q][:, 0:D], p_n[q][:, 0:D], bi[:, 2 * D:], ALU.add)
                        o.link(TT(cand[q][:, D:], p_n[q][:, D:], bh[:, 2 * D:], ALU.add))
                        dve.wait_ge(rz_done, t + 1)
                        o.link(TT(cand[q][:, D:], cand[q][:, D:], gates[q][:, 0:D], ALU.mult))
                        TT(cand[q][:, 0:D], cand[q][:, 0:D], cand[q][:, D:], ALU.add).then_inc(tanh_in, 1)
                        dve.wait_ge(tanh_done, t + 1)
                        own = x_sb[:, bass.ds(t, 1), :].rearrange("p o d -> p (o d)")
                        o.did(TT(own, own, cand[q][:, 0:D], ALU.add))
                        o.link(TT(cand[q][:, D:], h3[:, bass.ds(t, 1), :].rearrange("p o d -> p (o d)"), cand[q][:, 0:D], ALU.subtract))
                        o.link(TT(cand[q][:, D:], cand[q][:, D:], gates[q][:, D:], ALU.mult))
                        TT(own, own, cand[q][:, D:], ALU.add).then_inc(rows_ready, 1)
                        if left <= 2:
                            o.did(dve.nop())

                    add_parts(0, 0, 0)
                    add_parts(1, 1, 0)
                    add_bias(0, 0)
                    o.begin(6)
                    each_tile(dve, work)
                    o.leave(NT)


NAMES = {
    "gamma": "L0_gnn_gamma", "beta": "L0_gnn_beta", "W1": "L0_gnn_W1", "a_src1": "L0_gnn_a_src1", "a_dst1": "L0_gnn_a_dst1",
    "b1": "L0_gnn_b1", "W2": "L0_gnn_W2", "a_src2": "L0_gnn_a_src2", "a_dst2": "L0_gnn_a_dst2", "b2": "L0_gnn_b2",
    "Wu": "L0_gnn_Wu", "bu": "L0_gnn_bu",
    "mlp_w": "L1_gnn_mlp_w", "mlp_b": "L1_gnn_mlp_b", "ew1": "L1_gnn_ew1", "ew2": "L1_gnn_ew2", "bn_g": "L1_gnn_bn_g", "bn_b": "L1_gnn_bn_b",
    "L2_W": "L2_gnn_W", "L2_b": "L2_gnn_b",
    "m_b1": "L3_gnn_b1", "m_b2": "L3_gnn_b2", "m_b_ih": "L3_gnn_b_ih", "m_b_hh": "L3_gnn_b_hh",
}
TURNED = {"m_W1T": "L3_gnn_W1", "m_W2T": "L3_gnn_W2", "m_W_ihT": "L3_gnn_W_ih", "m_W_hhT": "L3_gnn_W_hh"}


def kernel(**inputs):
    import concourse.bacc as bacc
    from concourse.bass_utils import run_bass_kernel_spmd

    given = {name: np.asarray(value) for name, value in inputs.items()}

    def padded(array, rows, fill=0):
        whole = np.full((rows,) + array.shape[1:], fill, array.dtype)
        whole[:array.shape[0]] = array
        return whole

    arrays = {
        "x": padded(given["x"], NP),
        "src": padded(given["src"], EP),
        "dst": padded(given["dst"], EP, PADDST),
        "attr4": padded(given["edge_attr_4"], EP),
        "attr64T": np.ascontiguousarray(padded(given["edge_attr_64"], EP).T),
    }
    arrays.update({short: np.ascontiguousarray(given[name]) for short, name in NAMES.items()})
    arrays.update({short: np.ascontiguousarray(given[name].T) for short, name in TURNED.items()})

    nc = bacc.Bacc("TRN2", target_bir_lowering=False, num_devices=1)
    a = {name: nc.dram_tensor("in_" + name, array.shape, mybir.dt.from_np(array.dtype), kind="ExternalInput").ap()
         for name, array in arrays.items()}
    out = nc.dram_tensor("out", [N, D], F32, kind="ExternalOutput").ap()
    program(nc, a, out)
    result = run_bass_kernel_spmd(nc, [{"in_" + name: array for name, array in arrays.items()}], core_ids=[0])
    return result.results[0]["out"]
```
